# Optimizing a Trainium2 kernel written in Bass

```python
import numpy as np
import jax
import jax.numpy as jnp

def _softmax(x, axis=-1):
    return jax.nn.softmax(x, axis=axis)

def _gelu(x):
    return jax.nn.gelu(x, approximate=True)

def _silu(x):
    return jax.nn.silu(x)

def _sigmoid(x):
    return jax.nn.sigmoid(x)

def _layernorm(x, axis=-1, eps=1e-05):
    m = jnp.mean(x, axis=axis, keepdims=True)
    v = jnp.var(x, axis=axis, keepdims=True)
    return (x - m) / jnp.sqrt(v + eps)

def _scatter_add(tgt, idx, src, axis=0):
    return tgt.at[idx].add(src)

def _segment_sum(src, seg, n):
    return jax.ops.segment_sum(src, seg, n)
kernel_name = 'mk_flamingo_gated_d2_seqx_r8_be4e16'

def setup_inputs(seed: int=0):
    np.random.seed(seed)
    _w = jnp.asarray

    def _rec_inputs():
        import jax
        import jax.numpy as jnp
        _rk = jax.random.key(seed)
        x = -0.0002928 + 1 * jax.random.normal(jax.random.fold_in(_rk, 1), (4, 512, 128), jnp.float32)
        _lenS = 512 - jax.random.randint(jax.random.fold_in(_rk, 7), (4,), 0, max(1, 512 // 4) + 1, jnp.int32)
        _lenS2 = 77 - jax.random.randint(jax.random.fold_in(_rk, 8), (4,), 0, max(1, 77 // 4) + 1, jnp.int32)
        _ctx_1024P = jax.random.normal(jax.random.fold_in(_rk, 11), (4, 16, 128), jnp.float32)
        _ctx_1024c = jax.random.dirichlet(jax.random.fold_in(_rk, 511), 0.3 * jnp.ones((16,), jnp.float32), (4, 77))
        _ctx_1024t = jnp.einsum('bsk,bkd->bsd', _ctx_1024c, _ctx_1024P)
        _ctx_1024t = _ctx_1024t * jax.lax.rsqrt(jnp.mean(jnp.square(_ctx_1024t)) + 1e-12) * 0.953939
        ctx_1024 = -1.39393e-06 + 0.999914 * (_ctx_1024t + 0.3 * jax.random.normal(jax.random.fold_in(_rk, 611), (4, 77, 128), jnp.float32))
        _validS = jnp.arange(512)[None, :] < _lenS[:, None]
        _validS2 = jnp.arange(77)[None, :] < _lenS2[:, None]
        _causal = jnp.tril(jnp.ones((512, 512), dtype=bool))
        mask_SxS2_ik0 = jnp.where(jnp.broadcast_to(_validS2[0:1, :], (512, 77)), 0, 1).astype(jnp.int32)
        _g = jax.random.normal(jax.random.fold_in(_rk, 9001), (2, 2), jnp.float32)
        _g = jnp.sign(_g) * jnp.maximum(jnp.abs(_g), 1.0) + (_g == 0) * 1.0
        g_xattn = _g[0]
        g_ffn = _g[1]
        return (x, ctx_1024, mask_SxS2_ik0, g_xattn, g_ffn)
    x, ctx_1024, mask_SxS2_ik0, g_xattn, g_ffn = _rec_inputs()

    def _L0_xattn_setup():
        import jax, jax.numpy as jnp
        import numpy as np
        NUM_HEADS = 16

        def _rope_tables(seq_len, head_dim, dtype):
            inv_freq = 1.0 / 10000.0 ** (jnp.arange(0, head_dim, 2, dtype=jnp.float32) / head_dim)
            freqs = jnp.arange(seq_len, dtype=jnp.float32)[:, None] * inv_freq[None, :]
            emb = jnp.concatenate([freqs, freqs], axis=-1)
            return (jnp.cos(emb).astype(dtype), jnp.sin(emb).astype(dtype))

        def _rotate_half(t):
            d = t.shape[-1] // 2
            return jnp.concatenate([-t[..., d:], t[..., :d]], axis=-1)

        def _apply_rope(t):
            cos, sin = _rope_tables(t.shape[2], t.shape[3], t.dtype)
            return t * cos[None, None] + _rotate_half(t) * sin[None, None]

        def _forward(x, context, Wq, Wkv, Wo, bo):
            B, Nq, C = x.shape
            Nkv = context.shape[1]
            H = NUM_HEADS
            hd = C // H
            scale = hd ** (-0.5)
            q = (x @ Wq).reshape(B, Nq, H, hd).transpose(0, 2, 1, 3)
            kv = (context @ Wkv).reshape(B, Nkv, 2, H, hd).transpose(2, 0, 3, 1, 4)
            k, v = (kv[0], kv[1])
            q = _apply_rope(q)
            k = _apply_rope(k)
            attn = jnp.einsum('bhqd,bhkd->bhqk', q, k) * scale
            attn = jax.nn.softmax(attn, axis=-1)
            out = jnp.einsum('bhqk,bhkd->bhqd', attn, v)
            out = out.transpose(0, 2, 1, 3).reshape(B, Nq, C)
            return out @ Wo + bo
        key = jax.random.key(seed)
        ks = jax.random.split(key, 6)
        B, N, C = (2, 256, 128)
        s = C ** (-0.5)
        return {'x': jax.random.normal(ks[0], (B, N, C), dtype=jnp.float32), 'context': jax.random.normal(ks[1], (B, N, C), dtype=jnp.float32), 'Wq': jax.random.normal(ks[2], (C, C), dtype=jnp.float32) * s, 'Wkv': jax.random.normal(ks[3], (C, 2 * C), dtype=jnp.float32) * s, 'Wo': jax.random.normal(ks[4], (C, C), dtype=jnp.float32) * s, 'bo': jnp.zeros((C,), dtype=jnp.float32)}
    _L0_xattn_all = _L0_xattn_setup()
    _L0_xattn_in = {k: v for k, v in _L0_xattn_all.items() if k in ('Wq', 'Wkv', 'Wo', 'bo')}
    del _L0_xattn_all

    def _L0_ffn_setup():
        import jax, jax.numpy as jnp
        import numpy as np
        B, S, D, H, E = (4, 256, 128, 256, 8)
        key = jax.random.key(seed)
        ks = jax.random.split(key, 8)
        scale = 0.02
        return {'x': jax.random.normal(ks[0], (B, S, D), dtype=jnp.float32), 'Wr': jax.random.normal(ks[1], (D, E), dtype=jnp.float32) * scale, 'br': jnp.zeros((E,), dtype=jnp.float32), 'W1': jax.random.normal(ks[2], (E, D, H), dtype=jnp.float32) * scale, 'b1': jnp.zeros((E, H), dtype=jnp.float32), 'W2': jax.random.normal(ks[3], (E, H, D), dtype=jnp.float32) * scale, 'b2': jnp.zeros((E, D), dtype=jnp.float32)}
    _L0_ffn_all = _L0_ffn_setup()
    _L0_ffn_in = {k: v for k, v in _L0_ffn_all.items() if k in ('Wr', 'br', 'W1', 'b1', 'W2', 'b2')}
    del _L0_ffn_all

    def _L1_xattn_setup():
        import jax, jax.numpy as jnp
        import numpy as np
        B, S, D, H = (2, 256, 128, 16)
        HD = D // H
        DENSITY = 0.1
        key = jax.random.key(seed)
        ks = jax.random.split(key, 12)
        scale = 0.02
        inp = {'query': jax.random.normal(ks[0], (B, S, D), jnp.float32), 'key': jax.random.normal(ks[1], (B, S, D), jnp.float32), 'value': jax.random.normal(ks[2], (B, S, D), jnp.float32)}
        m = jax.random.uniform(ks[3], (S, S)) < DENSITY
        m = m.at[jnp.arange(S), jnp.arange(S)].set(True)
        inp['mask'] = m.astype(jnp.int32)
        inp['Wq'] = jax.random.normal(ks[4], (D, D), jnp.float32) * scale
        inp['bq'] = jax.random.normal(ks[5], (D,), jnp.float32) * scale
        inp['Wk'] = jax.random.normal(ks[6], (D, D), jnp.float32) * scale
        inp['bk'] = jax.random.normal(ks[7], (D,), jnp.float32) * scale
        inp['Wv'] = jax.random.normal(ks[8], (D, D), jnp.float32) * scale
        inp['bv'] = jax.random.normal(ks[9], (D,), jnp.float32) * scale
        inp['Wo'] = jax.random.normal(ks[10], (D, D), jnp.float32) * scale
        inp['bo'] = jax.random.normal(ks[11], (D,), jnp.float32) * scale
        return inp
    _L1_xattn_all = _L1_xattn_setup()
    _L1_xattn_in = {k: v for k, v in _L1_xattn_all.items() if k in ('Wq', 'bq', 'Wk', 'bk', 'Wv', 'bv', 'Wo', 'bo')}
    del _L1_xattn_all

    def _L1_ffn_setup():
        import jax, jax.numpy as jnp
        import numpy as np
        B, T, C = (4, 256, 128)
        H = 2 * C
        E = 8
        TOP_K = 2
        key = jax.random.key(seed)
        ks = jax.random.split(key, 5)
        s_in = 1.0 / np.sqrt(C)
        s_h = 1.0 / np.sqrt(H)
        return {'x': jax.random.normal(ks[0], (B, T, C), dtype=jnp.float32), 'w_gate': jax.random.normal(ks[1], (E, C), dtype=jnp.float32) * s_in, 'w_gate_proj': jax.random.normal(ks[2], (E, H, C), dtype=jnp.float32) * s_in, 'w_up_proj': jax.random.normal(ks[3], (E, H, C), dtype=jnp.float32) * s_in, 'w_down_proj': jax.random.normal(ks[4], (E, C, H), dtype=jnp.float32) * s_h}
    _L1_ffn_all = _L1_ffn_setup()
    _L1_ffn_in = {k: v for k, v in _L1_ffn_all.items() if k in ('w_gate', 'w_gate_proj', 'w_up_proj', 'w_down_proj')}
    del _L1_ffn_all
    return {'x': x, 'ctx_1024': ctx_1024, 'mask_SxS2_ik0': mask_SxS2_ik0, 'g_xattn': g_xattn, 'g_ffn': g_ffn, 'L0_xattn_Wq': _L0_xattn_in['Wq'], 'L0_xattn_Wkv': _L0_xattn_in['Wkv'], 'L0_xattn_Wo': _L0_xattn_in['Wo'], 'L0_xattn_bo': _L0_xattn_in['bo'], 'L0_ffn_Wr': _L0_ffn_in['Wr'], 'L0_ffn_br': _L0_ffn_in['br'], 'L0_ffn_W1': _L0_ffn_in['W1'], 'L0_ffn_b1': _L0_ffn_in['b1'], 'L0_ffn_W2': _L0_ffn_in['W2'], 'L0_ffn_b2': _L0_ffn_in['b2'], 'L1_xattn_Wq': _L1_xattn_in['Wq'], 'L1_xattn_bq': _L1_xattn_in['bq'], 'L1_xattn_Wk': _L1_xattn_in['Wk'], 'L1_xattn_bk': _L1_xattn_in['bk'], 'L1_xattn_Wv': _L1_xattn_in['Wv'], 'L1_xattn_bv': _L1_xattn_in['bv'], 'L1_xattn_Wo': _L1_xattn_in['Wo'], 'L1_xattn_bo': _L1_xattn_in['bo'], 'L1_ffn_w_gate': _L1_ffn_in['w_gate'], 'L1_ffn_w_gate_proj': _L1_ffn_in['w_gate_proj'], 'L1_ffn_w_up_proj': _L1_ffn_in['w_up_proj'], 'L1_ffn_w_down_proj': _L1_ffn_in['w_down_proj']}

def reference(x, ctx_1024, mask_SxS2_ik0, g_xattn, g_ffn, L0_xattn_Wq, L0_xattn_Wkv, L0_xattn_Wo, L0_xattn_bo, L0_ffn_Wr, L0_ffn_br, L0_ffn_W1, L0_ffn_b1, L0_ffn_W2, L0_ffn_b2, L1_xattn_Wq, L1_xattn_bq, L1_xattn_Wk, L1_xattn_bk, L1_xattn_Wv, L1_xattn_bv, L1_xattn_Wo, L1_xattn_bo, L1_ffn_w_gate, L1_ffn_w_gate_proj, L1_ffn_w_up_proj, L1_ffn_w_down_proj):
    import jax
    import jax.numpy as jnp

    def _L0_xattn_ref(x, context, Wq, Wkv, Wo, bo):
        import jax, jax.numpy as jnp
        import numpy as np
        NUM_HEADS = 16

        def _rope_tables(seq_len, head_dim, dtype):
            inv_freq = 1.0 / 10000.0 ** (jnp.arange(0, head_dim, 2, dtype=jnp.float32) / head_dim)
            freqs = jnp.arange(seq_len, dtype=jnp.float32)[:, None] * inv_freq[None, :]
            emb = jnp.concatenate([freqs, freqs], axis=-1)
            return (jnp.cos(emb).astype(dtype), jnp.sin(emb).astype(dtype))

        def _rotate_half(t):
            d = t.shape[-1] // 2
            return jnp.concatenate([-t[..., d:], t[..., :d]], axis=-1)

        def _apply_rope(t):
            cos, sin = _rope_tables(t.shape[2], t.shape[3], t.dtype)
            return t * cos[None, None] + _rotate_half(t) * sin[None, None]

        def _forward(x, context, Wq, Wkv, Wo, bo):
            B, Nq, C = x.shape
            Nkv = context.shape[1]
            H = NUM_HEADS
            hd = C // H
            scale = hd ** (-0.5)
            q = (x @ Wq).reshape(B, Nq, H, hd).transpose(0, 2, 1, 3)
            kv = (context @ Wkv).reshape(B, Nkv, 2, H, hd).transpose(2, 0, 3, 1, 4)
            k, v = (kv[0], kv[1])
            q = _apply_rope(q)
            k = _apply_rope(k)
            attn = jnp.einsum('bhqd,bhkd->bhqk', q, k) * scale
            attn = jax.nn.softmax(attn, axis=-1)
            out = jnp.einsum('bhqk,bhkd->bhqd', attn, v)
            out = out.transpose(0, 2, 1, 3).reshape(B, Nq, C)
            return out @ Wo + bo
        return _forward(x, context, Wq, Wkv, Wo, bo)

    def _L0_ffn_ref(x, Wr, br, W1, b1, W2, b2):
        import jax, jax.numpy as jnp
        import numpy as np
        B, S, D, H, E = (4, 256, 128, 256, 8)
        d = x.shape[-1]
        tokens = x.reshape(-1, d)
        logits = tokens @ Wr + br
        probs = jax.nn.softmax(logits, axis=-1)
        expert = jnp.argmax(probs, axis=-1)
        max_prob = jnp.take_along_axis(probs, expert[:, None], axis=-1)
        h = jax.nn.relu(jnp.einsum('td,edh->teh', tokens, W1) + b1[None])
        y = jnp.einsum('teh,ehd->ted', h, W2) + b2[None]
        out = jnp.take_along_axis(y, expert[:, None, None], axis=1)[:, 0, :]
        return (out * max_prob).reshape(x.shape)

    def _L1_xattn_ref(query, key, value, mask, Wq, bq, Wk, bk, Wv, bv, Wo, bo):
        import jax, jax.numpy as jnp
        import numpy as np
        B, S, D, H = (2, 256, 128, 16)
        HD = D // H
        DENSITY = 0.1
        b = query.shape[0]
        q = (query @ Wq + bq).reshape(b, -1, H, HD).transpose(0, 2, 1, 3)
        k = (key @ Wk + bk).reshape(b, -1, H, HD).transpose(0, 2, 1, 3)
        v = (value @ Wv + bv).reshape(b, -1, H, HD).transpose(0, 2, 1, 3)
        keep = mask.astype(bool)
        scores = jnp.einsum('bhsd,bhtd->bhst', q, k) / jnp.sqrt(jnp.asarray(HD, q.dtype))
        neg = jnp.finfo(scores.dtype).min
        scores = jnp.where(keep[None, None], scores, neg)
        w = jax.nn.softmax(scores, axis=-1)
        w = jnp.where(keep[None, None], w, jnp.asarray(0, w.dtype))
        out = jnp.einsum('bhst,bhtd->bhsd', w, v)
        out = out.transpose(0, 2, 1, 3).reshape(b, -1, D)
        return out @ Wo + bo

    def _L1_ffn_ref(x, w_gate, w_gate_proj, w_up_proj, w_down_proj):
        import jax, jax.numpy as jnp
        import numpy as np
        B, T, C = (4, 256, 128)
        H = 2 * C
        E = 8
        TOP_K = 2
        gate_logits = jnp.einsum('btc,ec->bte', x, w_gate)
        topk_vals, topk_idx = jax.lax.top_k(gate_logits, TOP_K)
        probs = jax.nn.softmax(topk_vals, axis=-1)
        out = jnp.zeros_like(x)
        for e in range(E):
            w_e = jnp.sum(probs * (topk_idx == e).astype(x.dtype), axis=-1)
            g = jax.nn.silu(jnp.einsum('btc,hc->bth', x, w_gate_proj[e]))
            u = jnp.einsum('btc,hc->bth', x, w_up_proj[e])
            y = jnp.einsum('bth,ch->btc', g * u, w_down_proj[e])
            out = out + y * w_e[..., None]
        return out
    x = x + jnp.tanh(g_xattn[0]) * _L0_xattn_ref(_layernorm(x, axis=-1), ctx_1024, L0_xattn_Wq, L0_xattn_Wkv, L0_xattn_Wo, L0_xattn_bo)
    x = x + jnp.tanh(g_ffn[0]) * _L0_ffn_ref(_layernorm(x, axis=-1), L0_ffn_Wr, L0_ffn_br, L0_ffn_W1, L0_ffn_b1, L0_ffn_W2, L0_ffn_b2)
    x = x + jnp.tanh(g_xattn[1]) * _L1_xattn_ref(_layernorm(x, axis=-1), ctx_1024, ctx_1024, mask_SxS2_ik0, L1_xattn_Wq, L1_xattn_bq, L1_xattn_Wk, L1_xattn_bk, L1_xattn_Wv, L1_xattn_bv, L1_xattn_Wo, L1_xattn_bo)
    x = x + jnp.tanh(g_ffn[1]) * _L1_ffn_ref(_layernorm(x, axis=-1), L1_ffn_w_gate, L1_ffn_w_gate_proj, L1_ffn_w_up_proj, L1_ffn_w_down_proj)
    return x

_drawn_inputs = setup_inputs


def setup_inputs(seed=0):
    import zlib

    import numpy as np

    out = dict(_drawn_inputs(seed))
    spreads = {'g_ffn': (-1.0, 0.6),
     'L0_xattn_bo': (0.0, 0.1),
     'L0_ffn_br': (0.0, 0.277),
     'L0_ffn_b1': (0.0, 0.609),
     'L0_ffn_b2': (0.0, 0.277)}
    factors = {'L0_ffn_W1': 4.386,
     'L0_ffn_W2': 2.995,
     'L1_xattn_Wq': 8.0,
     'L1_xattn_bq': 35.097,
     'L1_xattn_Wk': 8.0,
     'L1_xattn_bk': 64.0,
     'L1_xattn_bv': 3.724}
    for name, (base, spread) in spreads.items():
        noise = np.random.default_rng([zlib.crc32(name.encode()), seed]).standard_normal(out[name].shape)
        drawn = base * np.exp(spread * noise) if base else spread * noise
        out[name] = jnp.asarray(drawn.astype(out[name].dtype))
    for name, factor in factors.items():
        out[name] = (out[name] * factor).astype(out[name].dtype)
    return out
```

```python
from contextlib import ExitStack

import concourse.bass as bass
from concourse import mybir

F32 = mybir.dt.float32
F32R = mybir.dt.float32r
BF16 = mybir.dt.bfloat16
I32 = mybir.dt.int32
ALU = mybir.AluOpType
ACT = mybir.ActivationFunctionType
AX = mybir.AxisListType

P = 128
D = 128
LAYERS = 2
NB, SEQ, KEYS = 4, 512, 77
TPB = SEQ // P
NT = NB * TPB
TOKENS = NB * SEQ
HEADS, HD = 16, 8
GROUPS, HPG = 4, 4
GK = HPG * KEYS
KT = 3
KROWS = 103
KSIZE = [min(KROWS, GK - KROWS * j) for j in range(KT)]
NS = KT * GROUPS
SCALE = float(HD) ** -0.5
EPS = 1e-5
E, HID = 8, 256
HC = HID // P
MASKED = -1e30
CLAMP = 1e25
SLOTS = 4
CHOICES = [1, 2]
FT = [-(-((TOKENS * c + E * (P - 1)) // P) // SLOTS) * SLOTS for c in CHOICES]
DUMMY = E * NT
PAY = D + 2
FW = [2 * HID + D + HC, 3 * HID]
NOROW = 1 << 20

C_ID, C_COS, C_SIN = 0, P, P + SEQ
C_HM = C_SIN + SEQ
C_HMV = C_HM + HPG
C_U = C_HMV + KT * 32
C_DESC = C_U + P
C_EB = C_DESC + E
C_K128 = C_EB + E
C_LT = C_K128 + NT
C_J = C_LT + E * E
C_END = C_J + max(FT)
W_Q, W_QR, W_K, W_KR, W_V, W_O, W_BV, W_BO = [D * i for i in range(8)]
W_R = 8 * D
W_BR = W_R + E
W_BQ = W_BR + E
W_BK = W_BQ + 1
W_END = W_BK + 1
AUG_KEY = 32


def bcast(ap, axis, n):
    ap = ap.unsqueeze(axis)
    shape = list(ap.shape)
    shape[axis] = n
    return ap.broadcast_to(shape)


def two_layers(nc, x_in, ctx_in, mask_in, gates_in, w0_in, w1_in, f0_in, f1_in, const_in, aug_in, ids_in, pad_in, out):
    w_in, f_in = [w0_in, w1_in], [f0_in, f1_in]
    with ExitStack() as ctx:
        def sb(name, shape, dt=F32):
            return ctx.enter_context(nc.sbuf_tensor(name, shape, dt))

        def pb(name):
            return ctx.enter_context(nc.psum_tensor(name, [P, 512], F32))

        def sem(name):
            return ctx.enter_context(nc.semaphore(name))

        routed = [nc.dram_tensor(f"routed{l}", (DUMMY * P + P, PAY), F32, kind="Internal").ap() for l in range(LAYERS)]
        expert_out = [nc.dram_tensor(f"expert_out{l}", (CHOICES[l] * TOKENS, D), F32, kind="Internal").ap() for l in range(LAYERS)]

        x = sb("x", [P, NT, D])
        cst = sb("cst", [P, C_END])
        ident = cst[:, C_ID:C_ID + P]
        cos, sin = cst[:, C_COS:C_COS + SEQ], cst[:, C_SIN:C_SIN + SEQ]
        hm = cst[:, C_HM:C_HM + HPG]
        hmv = cst[:, C_HMV:C_HMV + KT * 32].rearrange("p (j c) -> p j c", j=KT)
        desc, ebase = cst[:, C_DESC:C_DESC + E], cst[:, C_EB:C_EB + E]
        probs = [sb(f"probs{i}", [P, NS, SEQ]) for i in range(2)]
        spare = [probs[i][:, :, :].rearrange("p s c -> p (s c)") for i in range(2)]
        augf = spare[1][:, 0:GROUPS * GK]
        aug = sb("aug", [P, GROUPS, GK], F32R)
        ids = sb("ids", [P, 2, NT], I32)
        pad = sb("pad", [P, PAY])
        cx = sb("cx", [P, NB, KEYS])
        cx4 = sb("cx4", [P, NB, HPG, KEYS])
        maski = sb("maski", [P, TPB, KEYS], I32)
        gates = sb("gates", [P, 4])
        tg = sb("tg", [P, 4])
        w = [sb(f"w{l}", [P, W_END]) for l in range(LAYERS)]
        prefix16 = sb("prefix16", [P, P], BF16)
        ones16 = sb("ones16", [P, P], BF16)
        half = sb("half", [P, TPB])
        kr1 = sb("kr1", [P, NB * KEYS])
        kr2 = sb("kr2", [P, NB * KEYS])
        khl = [sb(f"khl{i}", [P, NB * KEYS], F32R) for i in range(2)]
        kblk = [spare[1][:, (1 + i) * GROUPS * GK:(2 + i) * GROUPS * GK].bitcast(F32R)
                .rearrange("p (b h k) -> p b h k", b=NB, h=HPG) for i in range(2)]
        ks = sb("ks", [P, GROUPS, NB, GK], F32R)
        vb = sb("vb", [P, KT, NB, D])
        tgbo = [sb(f"tgbo{l}", [P, D]) for l in range(LAYERS)]
        st = sb("st", [P, TPB, 6])
        mv = sb("mv", [P, TPB, 2])
        ve = sb("ve", [P, TPB])
        rstd = sb("rstd", [P, TPB])
        nrm = sb("nrm", [P, TPB, D])
        nT = sb("nT", [P, SEQ])
        qr1 = sb("qr1", [P, SEQ])
        qr2 = sb("qr2", [P, SEQ])
        qhl = [sb(f"qhl{i}", [P, SEQ], F32R) for i in range(2)]
        qs = [sb(f"qs{i}", [P, GROUPS, SEQ], F32R) for i in range(3)]
        negm = sb("negm", [P, TPB, HEADS])
        negmh = sb("negmh", [P, TPB, HEADS], F32R)
        augt = [sb(f"augt{l}", [P, TPB, P]) for l in range(LAYERS)]
        augT = [sb(f"augT{i}", [P, SEQ], F32R) for i in range(2)]
        maskT = sb("maskT", [P, SEQ], F32R)
        nums = sb("nums", [P, SEQ])
        dens = sb("dens", [P, SEQ])
        rd = sb("rd", [P, TPB, HEADS])
        rdx = dens
        att = sb("att", [P, SEQ])
        vtmp = att
        st2 = sb("st2", [P, TPB, 6])
        mv2 = sb("mv2", [P, TPB, 2])
        ve2 = sb("ve2", [P, TPB])
        rstd2 = sb("rstd2", [P, TPB])
        pay = [sb(f"pay{c}", [P, NT, PAY]) for c in range(2)]
        nT2 = sb("nT2", [P, SEQ])
        lg = sb("lg", [P, TPB, E])
        lg2 = sb("lg2", [P, TPB, E])
        wt = sb("wt", [P, TPB, E])
        wm = sb("wm", [P, TPB])
        mx = [sb(f"mx{i}", [P, TPB]) for i in range(2)]
        oh = [sb(f"oh{i}", [P, TPB, E], BF16) for i in range(2)]
        ohs = sb("ohs", [P, TPB, E], BF16)
        run = [sb(f"run{l}", [P, NT + 1, E], BF16) for l in range(LAYERS)]
        shifted = sb("shifted", [P, TPB, E])
        expd = sb("expd", [P, TPB, E])
        se = sb("se", [P, TPB])
        re = sb("re", [P, TPB])
        rk = sb("rk", [P, TPB, E])
        slotf = sb("slotf", [P, TPB])
        slot = [sb(f"slot{c}", [P, NT], I32) for c in range(2)]
        gt = sb("gt", [P, E, NT])
        tiles = sb("tiles", [P, E])
        cumx = sb("cumx", [P, E, E])
        cum = sb("cum", [P, E])
        le = sb("le", [P, max(FT), E])
        let = sb("let", [P, max(FT), E])
        ej = sb("ej", [P, max(FT)])
        kj = sb("kj", [P, max(FT)])
        bj = sb("bj", [P, max(FT)])
        meta = [sb(f"meta{l}", [1, 2, FT[l]], I32) for l in range(LAYERS)]
        xt = [sb(f"xt{i}", [P, PAY]) for i in range(SLOTS)]
        fw = [spare[0][:, i * max(FW):(i + 1) * max(FW)] for i in range(SLOTS)]
        xT = [sb(f"xT{i}", [P, P]) for i in range(SLOTS)]
        hid = [(nums, dens)[i // 2][:, (i % 2) * HID:(i % 2 + 1) * HID].rearrange("p (c t) -> p c t", c=HC) for i in range(SLOTS)]
        tanhs = [qr1[:, i * HID:(i + 1) * HID] for i in range(2)]
        silu = [qr2[:, i * HID:(i + 1) * HID] for i in range(2)]
        rows_at = [sb(f"rows_at{i}", [P, 1], I32) for i in range(SLOTS)]
        yb = [qr1[:, i * D:(i + 1) * D] for i in range(SLOTS)]
        yo = [sb(f"yo{i}", [P, D]) for i in range(SLOTS)]
        yin = [[sb(f"yin{b}", [P, SEQ])[:, :] for b in range(NB)], [probs[1][:, b, :] for b in range(NB)]]

        ps_s = [pb(f"ps_s{i}") for i in range(3)]
        ps_a = [pb(f"ps_a{i}") for i in range(2)]
        ps_t = pb("ps_t")
        ps_n = pb("ps_n")
        ps_d = pb("ps_d")

        ld_x = [sem(f"ld_x{b}") for b in range(NB)]
        ld_m = sem("ld_m")
        ld_c, ld_k, ld_aug = sem("ld_c"), sem("ld_k"), sem("ld_aug")
        ld_w = [sem(f"ld_w{l}") for l in range(LAYERS)]
        padded = [sem(f"padded{l}") for l in range(LAYERS)]
        s_cx4, s_aug, s_tanh, s_const, s_masked = sem("s_cx4"), sem("s_aug"), sem("s_tanh"), sem("s_const"), sem("s_masked")
        s_tgbo = sem("s_tgbo")
        ring_full, ring_used = sem("ring_full"), sem("ring_used")
        s_khl, s_kblk, kspread = sem("s_khl"), sem("s_kblk"), sem("kspread")
        s_vb = sem("s_vb")
        var1, rstd1_ok, nrm_ok, nrmT_ok, nT_ok = sem("var1"), sem("rstd1_ok"), sem("nrm_ok"), sem("nrmT_ok"), sem("nT_ok")
        rot_ok, q_ok, qh_ok, ql_ok, qspread = sem("rot_ok"), sem("q_ok"), sem("qh_ok"), sem("ql_ok"), sem("qspread")
        augt_ok, augt_tr, augT_ok = sem("augt_ok"), sem("augt_tr"), sem("augT_ok")
        mask_tr, maskT_ok = sem("mask_tr"), sem("maskT_ok")
        sc_full, exp_ok, pv_ok, nd_ok = sem("sc_full"), sem("exp_ok"), sem("pv_ok"), sem("nd_ok")
        rdx_ok = sem("rdx_ok")
        den_tr, rd_ok, rd_tr, att_ok = sem("den_tr"), sem("rd_ok"), sem("rd_tr"), sem("att_ok")
        xb_ok = sem("xb_ok")
        var2, rstd2_ok, nrm2_ok, pay_tr, nT2_ok = sem("var2"), sem("rstd2_ok"), sem("nrm2_ok"), sem("pay_tr"), sem("nT2_ok")
        pay2_ok = sem("pay2_ok")
        sh_ok, ex_ok, ohs_ok, slot_ok, scattered = sem("sh_ok"), sem("ex_ok"), sem("ohs_ok"), sem("slot_ok"), sem("scattered")
        meta_ok = sem("meta_ok")
        s_dve, s_act, s_pool = sem("s_dve"), sem("s_act"), sem("s_pool")
        def per_layer(name):
            return [sem(f"{name}{l}") for l in range(LAYERS)]
        f_ld = [[sem(f"f_ld{l}_{i}") for i in range(SLOTS)] for l in range(LAYERS)]
        f_xtr, f_xT, f_up, f_hid, f_dn = map(per_layer, ("f_xtr", "f_xT", "f_up", "f_hid", "f_dn"))
        f_th, f_y, f_silu, f_turn = map(per_layer, ("f_th", "f_y", "f_silu", "f_turn"))
        f_put = [[sem(f"f_put{l}_{i}") for i in range(SLOTS)] for l in range(LAYERS)]
        y_ld = [[sem(f"y_ld{l}_{b}") for b in range(NB)] for l in range(LAYERS)]
        x_ok, o_put = sem("x_ok"), sem("o_put")

        block = ctx.enter_context(nc.Block())

        def score_tile(s):
            return s // GROUPS, s % GROUPS

        class Count:
            def __init__(self, n=0):
                self.n = n

            def next(self):
                self.n += 1
                return self.n - 1

        def rounds(eng, l, body):
            body(0, True)
            with eng.Fori(1, FT[l] // SLOTS) as r:
                body(r, False)

        @block.sync
        def _(sp):
            sp.dma_start(x[:, 0:TPB, :], x_in[:, 0:TPB, :]).then_inc(ld_x[0], 16)
            sp.dma_start(cst[:, :], const_in).then_inc(ld_c, 16)
            sp.dma_start(cx[:, :, :], ctx_in).then_inc(ld_k, 16)
            sp.dma_start(w[0][:, :], w_in[0]).then_inc(ld_w[0], 16)
            sp.dma_start(gates[:, :], gates_in).then_inc(ld_c, 16)
            sp.dma_start(ids[:, :, :], ids_in).then_inc(ld_c, 16)
            sp.dma_start(maski[:, :, :], mask_in).then_inc(ld_m, 16)
            for b in range(1, NB):
                sp.dma_start(x[:, b * TPB:(b + 1) * TPB, :], x_in[:, b * TPB:(b + 1) * TPB, :]).then_inc(ld_x[b], 16)

            def spread_k(l):
                sp.wait_ge(s_kblk, l + 1)
                for blk in range(4):
                    for g in range(GROUPS):
                        sp.dma_start(ks[32 * blk:32 * blk + 32, g, :, :].rearrange("p b k -> p (b k)").bitcast(F32),
                                     kblk[blk // 2][32 * g:32 * g + 32, :, :, :].rearrange("p b h k -> p (b h k)").bitcast(F32)).then_inc(kspread, 16)

            def spread_q(n):
                sp.wait_ge(qh_ok, n + 1)
                sp.wait_ge(ql_ok, n + 1)
                if n >= 3:
                    sp.wait_ge(sc_full, NS * (n - 2))
                for blk in range(4):
                    for g in range(GROUPS):
                        sp.dma_start(qs[n % 3][32 * blk:32 * blk + 32, g, :].bitcast(F32), qhl[blk % 2][32 * g:32 * g + 32, :].bitcast(F32)).then_inc(qspread, 16)

            def load_tiles(l):
                sp.wait_ge(meta_ok, l + 1)

                def body(r, first):
                    for i in range(SLOTS):
                        j = r * SLOTS + i
                        at_w = sp.value_load(meta[l][0:1, 0, bass.ds(j, 1)], min_val=0, max_val=(E - 1) * P * FW[l])
                        at_x = sp.value_load(meta[l][0:1, 1, bass.ds(j, 1)], min_val=0, max_val=DUMMY * P * PAY)
                        if not first:
                            sp.wait_ge(f_y[l], (r - 1) * SLOTS + i + 1)
                            sp.sem_inc(f_turn[l], 1)
                        sp.dma_start(fw[i][:, 0:FW[l]], f_in[l].rearrange("e p f -> (e p f)")[bass.ds(at_w, P * FW[l])].rearrange("(p f) -> p f", p=P)).then_inc(f_ld[l][i], 16)
                        if first and i == 0:
                            sp.wait_ge(scattered, 16 * sum(CHOICES[:l + 1]) * NT)
                        sp.dma_start(xt[i][:, :], routed[l].rearrange("k c -> (k c)")[bass.ds(at_x, P * PAY)].rearrange("(p c) -> p c", p=P)).then_inc(f_ld[l][i], 16)

                rounds(sp, l, body)

            def load_results(l):
                for i in range(SLOTS):
                    sp.wait_ge(f_put[l][i], 16 * FT[l] // SLOTS)
                for b in range(NB):
                    for c in range(CHOICES[l]):
                        src = expert_out[l][c * TOKENS + b * SEQ:c * TOKENS + (b + 1) * SEQ, :].rearrange("(t p) d -> p t d", p=P)
                        if l and not c:
                            sp.wait_ge(x_ok, b + 1)
                        sp.dma_start(yin[c][b].rearrange("p (t c) -> p t c", c=D), src).then_inc(y_ld[l][b], 16)

            for l in range(LAYERS):
                if l == 0:
                    spread_k(0)
                    sp.dma_start(w[1][:, :], w_in[1]).then_inc(ld_w[1], 16)
                spread_q(NB * l)
                spread_q(NB * l + 1)
                spread_q(NB * l + 2)
                spread_q(NB * l + 3)
                load_tiles(l)
                if l == 0:
                    spread_k(1)
                load_results(l)
            for b in range(NB):
                sp.wait_ge(x_ok, NB + b + 1)
                sp.dma_start(out[:, b * TPB:(b + 1) * TPB, :], x[:, b * TPB:(b + 1) * TPB, :]).then_inc(o_put, 16)
            sp.wait_ge(o_put, 16 * NB)

        @block.gpsimd
        def _(pool):
            chain = Count()

            def link(ins):
                ins.then_inc(s_pool, 1)
                pool.wait_ge(s_pool, chain.next() + 1)

            nc.gpsimd.memset(half[:, :], -0.5)
            nc.gpsimd.memset(ones16[:, :], 1.0)
            for l in range(LAYERS):
                nc.gpsimd.memset(augt[l][:, :, :], 0.0)
                nc.gpsimd.memset(run[l][:, 0, :], 0.0)
            nc.gpsimd.memset(xt[0][:, :], 0.0).then_inc(s_const, 1)
            pool.wait_ge(ld_k, 16)
            for h in range(HPG):
                last = nc.gpsimd.tensor_copy(cx4[:, :, h, :], cx[:, :, :])
            last.then_inc(s_cx4, 1)

            def power(var, ve_, rstd_, done, n):
                pool.wait_ge(var, n + 1)
                link(nc.gpsimd.tensor_scalar(ve_[:, :], (mv if var is var1 else mv2)[:, :, 1], EPS, None, ALU.add))
                nc.gpsimd.tensor_tensor(rstd_[:, :], ve_[:, :], half[:, :], ALU.pow).then_inc(done, 1)

            def add_q(n):
                pool.wait_ge(rot_ok, n + 1)
                if n:
                    pool.wait_ge(ql_ok, n)
                nc.gpsimd.tensor_tensor(qr1[:, :], qr1[:, :], qr2[:, :], ALU.add).then_inc(q_ok, 1)

            def add_bias(n):
                l, b = divmod(n, NB)
                pool.wait_ge(s_tgbo, l + 1)
                pool.wait_ge(nrm_ok, n + 1)
                xb = x[:, b * TPB:(b + 1) * TPB, :]
                nc.gpsimd.tensor_tensor(xb, xb, bcast(tgbo[l][:, :], 1, TPB), ALU.add).then_inc(xb_ok, 1)

            def scatter(n):
                l, b = divmod(n, NB)
                pool.wait_ge(slot_ok, n + 1)
                if b == 0:
                    pool.wait_ge(padded[l], 16)
                for i in range(TPB):
                    for c in range(CHOICES[l]):
                        t = b * TPB + i
                        pool.indirect_dma_start(
                            out=routed[l], out_offset=bass.IndirectOffsetOnAxis(ap=slot[c][:, t:t + 1], axis=0),
                            in_=pay[c][:, t, :], in_offset=None).then_inc(scattered, 16)

            def second_copy(n):
                b = n % NB
                pool.wait_ge(nrm2_ok, n + 1)
                nc.gpsimd.tensor_copy(pay[1][:, b * TPB:(b + 1) * TPB, 0:D], pay[0][:, b * TPB:(b + 1) * TPB, 0:D]).then_inc(pay2_ok, 1)

            def put_tiles(l):
                last_row = pool.alloc_register(f"last_row{l}")
                pool.reg_mov(last_row, CHOICES[l] * TOKENS - 1)

                def body(r, first):
                    for i in range(SLOTS):
                        pool.wait_ge(f_y[l], r * SLOTS + i + 1)
                        pool.sem_inc(f_turn[l], 1)
                        pool.indirect_dma_start(
                            out=expert_out[l], out_offset=bass.IndirectOffsetOnAxis(ap=rows_at[i][:, :], axis=0),
                            in_=yo[i][:, :], in_offset=None, bounds_check=last_row, oob_is_err=False).then_inc(f_put[l][i], 16)

                rounds(pool, l, body)

            for l in range(LAYERS):
                n0 = NB * l
                for n in (n0, n0 + 1):
                    power(var1, ve, rstd, rstd1_ok, n)
                    if l == 0:
                        add_q(n)
                    add_bias(n)
                for b in range(NB + 1):
                    n = n0 + b
                    if b < NB - 2:
                        power(var1, ve, rstd, rstd1_ok, n + 2)
                    if b >= 1:
                        power(var2, ve2, rstd2, rstd2_ok, n - 1)
                    if b < NB - 2 and l == 0:
                        add_q(n + 2)
                    if b < NB - 2:
                        add_bias(n + 2)
                    if b >= 1:
                        if l:
                            second_copy(n - 1)
                        scatter(n - 1)
                put_tiles(l)

        @block.scalar
        def _(act):
            act.dma_start(pad[:, :], pad_in).then_inc(ld_c, 16)
            act.dma_start(augf, aug_in).then_inc(ld_aug, 16)
            act.wait_ge(ld_c, 64)
            nc.scalar.activation(tg[:, :], gates[:, :], ACT.Tanh).then_inc(s_tanh, 1)
            for l in range(LAYERS):
                act.dma_start(routed[l].rearrange("(k p) c -> p k c", p=P), bcast(pad[:, :], 1, DUMMY + 1)).then_inc(padded[l], 16)
            act.wait_ge(ld_aug, 16)
            nc.scalar.activation(aug[:, :, :].rearrange("p g k -> p (g k)"), augf, ACT.Copy).then_inc(s_aug, 1)

            def copy_nT(n):
                act.wait_ge(nrmT_ok, n + 1)
                nc.scalar.activation(nT[:, :], ps_t[:, :], ACT.Copy).then_inc(nT_ok, 1)

            def high_q(n):
                act.wait_ge(q_ok, n + 1)
                if n:
                    act.wait_ge(qspread, 256 * n)
                nc.scalar.activation(qhl[0][:, :], qr1[:, :], ACT.Copy).then_inc(qh_ok, 1)

            def copy_augT(n):
                act.wait_ge(augt_tr, n + 1)
                if n >= 2:
                    act.wait_ge(sc_full, NS * (n - 1))
                nc.scalar.activation(augT[n % 2][:, :], ps_t[:, :], ACT.Copy).then_inc(augT_ok, 1)

            def exps(n, s):
                j, g = score_tile(s)
                act.wait_ge(sc_full, NS * n + s + 1)
                if n >= 2 and s == 0:
                    act.wait_ge(pv_ok, KT * (n - 1))
                nc.scalar.activation(probs[n % 2][0:KSIZE[j], s, :], ps_s[(NS * n + s) % 3][0:KSIZE[j], :], ACT.Exp, scale=SCALE).then_inc(exp_ok, 1)

            def copy_nd(n):
                act.wait_ge(pv_ok, KT * (n + 1))
                if n:
                    act.wait_ge(att_ok, n)
                nc.scalar.activation(dens[:, :], ps_d[:, :], ACT.Copy).then_inc(nd_ok, 1)
                nc.scalar.activation(nums[:, :], ps_n[:, :], ACT.Copy).then_inc(nd_ok, 1)

            def widen_rd(n):
                act.wait_ge(rd_ok, n + 1)
                if n:
                    act.wait_ge(rd_tr, n)
                nc.scalar.activation(rdx[:, :].rearrange("p (q d) -> p q d", d=HD),
                                     bcast(rd[:, :, :].rearrange("p t h -> p (t h)"), 2, HD), ACT.Copy).then_inc(rdx_ok, 1)

            def copy_nT2(n):
                act.wait_ge(pay_tr, n + 1)
                nc.scalar.activation(nT2[:, :], ps_t[:, :], ACT.Copy).then_inc(nT2_ok, 1)

            def route_exp(n):
                act.wait_ge(sh_ok, n + 1)
                if n < NB:
                    nc.scalar.activation(expd[:, :, :], shifted[:, :, :], ACT.Exp).then_inc(ex_ok, 1)
                else:
                    nc.scalar.activation(se[:, :], shifted[:, :, 0], ACT.Exp).then_inc(ex_ok, 1)

            def tiles_relu(l):
                def body(r, first):
                    for i in range(SLOTS):
                        j = r * SLOTS + i
                        act.wait_ge(f_up[l], j + 1)
                        if not first:
                            act.wait_ge(f_dn[l], j + 1 - SLOTS)
                        for c in range(HC):
                            last = nc.scalar.activation(hid[i][:, c, :], ps_s[i % 2][:, c * P:(c + 1) * P], ACT.Relu,
                                                        bias=fw[i][:, FW[0] - HC + c:FW[0] - HC + c + 1])
                        last.then_inc(f_hid[l], 1)

                rounds(act, l, body)

            def tiles_tanh(l):
                def body(r, first):
                    for i in range(SLOTS):
                        j = r * SLOTS + i
                        act.wait_ge(f_xtr[l], j + 1)
                        if not first:
                            act.wait_ge(f_up[l], j + 1 - SLOTS)
                        nc.scalar.activation(xT[i][:, :], ps_a[i % 2][:, 0:P], ACT.Copy).then_inc(f_xT[l], 1)
                        act.wait_ge(f_up[l], j + 1)
                        if not first:
                            act.wait_ge(f_hid[l], j - 1)
                        elif i >= 2:
                            act.wait_ge(f_hid[l], i - 1)
                        nc.scalar.activation(tanhs[i % 2], ps_s[i % 2][:, 0:HID], ACT.Tanh, scale=0.5).then_inc(f_th[l], 1)

                rounds(act, l, body)

            for l in range(LAYERS):
                n0 = NB * l
                for n in (n0, n0 + 1):
                    copy_nT(n)
                    high_q(n)
                    if l and n == n0:
                        act.wait_ge(mask_tr, 1)
                        nc.scalar.activation(maskT[:, :], ps_t[:, :], ACT.Copy).then_inc(maskT_ok, 1)
                copy_augT(n0)
                for b in range(NB + 1):
                    n = n0 + b
                    for s in range(NS):
                        if b < NB:
                            exps(n, s)
                        if s == 1 and b:
                            copy_nd(n - 1)
                        if s == 3 and b:
                            widen_rd(n - 1)
                        if s == 4 and b < NB - 2:
                            copy_nT(n + 2)
                        if s == 6 and b < NB - 2:
                            high_q(n + 2)
                        if s == 8 and b:
                            copy_nT2(n - 1)
                        if s == 10 and b:
                            route_exp(n - 1)
                        if s == 11 and b < NB - 1:
                            copy_augT(n + 1)
                (tiles_tanh if l else tiles_relu)(l)

        @block.tensor
        def _(pe):
            unit = Count()
            reader = []

            def ring():
                u = unit.next()
                if u >= 2:
                    pe.wait_ge(ring_used, u - 1)
                return ps_a[u % 2]

            def keys_values(l):
                pe.wait_ge(ld_w[l], 16)
                pe.wait_ge(ld_k, 16)
                for c in ((W_K,) if l else (W_K, W_KR)):
                    nc.tensor.matmul(ring()[:, 0:NB * KEYS], w[l][:, c:c + D], cx[:, :, :].rearrange("p b k -> p (b k)"),
                                     start=True, stop=True).then_inc(ring_full, 1)
                pe.wait_ge(s_cx4, 1)
                for j in range(KT):
                    bank = ring()
                    for b in range(NB):
                        src = cx4[:, b, :, :].rearrange("p h k -> p (h k)")[:, KROWS * j:KROWS * j + KSIZE[j]]
                        last = nc.tensor.matmul(bank[0:KSIZE[j], b * D:(b + 1) * D], src, w[l][:, W_V:W_V + D], start=True, stop=True)
                    last.then_inc(ring_full, 1)

            def transposes(src, done, read, value):
                if reader:
                    pe.wait_ge(*reader[-1])
                reader.append((read, value))
                for i in range(TPB):
                    last = nc.tensor.transpose(ps_t[:, i * P:(i + 1) * P], src(i), ident)
                last.then_inc(done, 1)

            def project(n):
                pe.wait_ge(nT_ok, n + 1)
                for c in ((W_Q, W_QR) if n < NB else (W_Q,)):
                    nc.tensor.matmul(ring()[:, :], w[n // NB][:, c:c + D], nT[:, :], start=True, stop=True).then_inc(ring_full, 1)

            def front(n):
                pe.wait_ge(nrm_ok, n + 1)
                transposes(lambda i: nrm[:, i, :], nrmT_ok, nT_ok, n + 1)

            def scores_for_max(n, u):
                l, b = divmod(n, NB)
                i, g = divmod(u, GROUPS)
                if u == 0:
                    pe.wait_ge(qspread, 256 * (n + 1))
                    if b == 0:
                        pe.wait_ge(kspread, 256 * (l + 1))
                bank = ring()
                if l:
                    if n == NB and u == 0:
                        pe.wait_ge(maskT_ok, 1)
                    nc.tensor.matmul(bank[:, 0:GK], maskT[:, i * P:(i + 1) * P], aug[:, g, :], start=True, stop=False)
                nc.tensor.matmul(bank[:, 0:GK], qs[n % 3][:, g, i * P:(i + 1) * P], ks[:, g, b, :], start=not l, stop=True).then_inc(ring_full, 1)

            def augmenting(n):
                pe.wait_ge(augt_ok, n + 1)
                transposes(lambda i: augt[n // NB][:, i, :], augt_tr, augT_ok, n + 1)

            def scores(n, s):
                l, b = divmod(n, NB)
                j, g = score_tile(s)
                k = NS * n + s
                if s == 0:
                    pe.wait_ge(augT_ok, n + 1)
                    if n == 0:
                        pe.wait_ge(s_aug, 1)
                if k >= 3:
                    pe.wait_ge(exp_ok, k - 2)
                bank = ps_s[k % 3][0:KSIZE[j], :]
                lo, hi = KROWS * j, KROWS * j + KSIZE[j]
                nc.tensor.matmul(bank, ks[:, g, b, lo:hi], qs[n % 3][:, g, :], start=True, stop=False)
                nc.tensor.matmul(bank, aug[:, g, lo:hi], augT[n % 2][:, :], start=False, stop=True).then_inc(sc_full, 1)

            def weigh(n, j):
                l, b = divmod(n, NB)
                pe.wait_ge(exp_ok, NS * n + GROUPS * (j + 1))
                if j == 0:
                    if b == 0:
                        pe.wait_ge(s_vb, KT * (l + 1))
                    if n:
                        pe.wait_ge(nd_ok, 2 * n)
                kk = KSIZE[j]
                for bank, lhs in ((ps_n, lambda g: vb[0:kk, j, b, 32 * g:32 * g + 32]), (ps_d, lambda g: hmv[0:kk, j, :])):
                    for g in range(GROUPS):
                        last = nc.tensor.matmul(bank[32 * g:32 * g + 32, :], lhs(g), probs[n % 2][0:kk, j * GROUPS + g, :],
                                                start=j == 0, stop=j == KT - 1)
                last.then_inc(pv_ok, 1)

            def den_to_tokens(n):
                pe.wait_ge(nd_ok, 2 * n + 1)
                transposes(lambda i: dens[:, i * P:(i + 1) * P], den_tr, rd_ok, n + 1)

            def rden_to_dims(n):
                pe.wait_ge(rdx_ok, n + 1)
                transposes(lambda i: rdx[:, i * P:(i + 1) * P], rd_tr, att_ok, n + 1)

            def output(n):
                pe.wait_ge(att_ok, n + 1)
                bank = ring()
                for i in range(TPB):
                    last = nc.tensor.matmul(bank[:, i * D:(i + 1) * D], att[:, i * P:(i + 1) * P], w[n // NB][:, W_O:W_O + D], start=True, stop=True)
                last.then_inc(ring_full, 1)

            def routed_T(n):
                pe.wait_ge(nrm2_ok, n + 1)
                transposes(lambda i: pay[0][:, (n % NB) * TPB + i, 0:D], pay_tr, nT2_ok, n + 1)

            def router(n):
                pe.wait_ge(nT2_ok, n + 1)
                bank = ring()
                for i in range(TPB):
                    last = nc.tensor.matmul(bank[:, i * E:(i + 1) * E], nT2[:, i * P:(i + 1) * P], w[n // NB][:, W_R:W_R + E], start=True, stop=True)
                last.then_inc(ring_full, 1)

            def ranks(n):
                l, b = divmod(n, NB)
                pe.wait_ge(ohs_ok, n + 1)
                if n == 0:
                    pe.wait_ge(s_const, 1)
                bank = ring()
                nc.tensor.matmul(bank[:, 0:TPB * E], prefix16[:, :], ohs[:, :, :].rearrange("p t e -> p (t e)"), start=True, stop=False)
                nc.tensor.matmul(bank[:, 0:TPB * E], ones16[:, :], run[l][:, b * TPB:(b + 1) * TPB, :].rearrange("p t e -> p (t e)"),
                                 start=False, stop=True).then_inc(ring_full, 1)

            def totals(l):
                nc.tensor.matmul(ring()[:, 0:E], ones16[:, :], run[l][:, NT, :], start=True, stop=True).then_inc(ring_full, 1)

            def tiles_pe(l):
                up = 2 * HC if l else HC
                dn0 = up * P

                def turn(i, j):
                    pe.wait_ge(f_ld[l][i], j["ld"])
                    if j["xT"] is not None:
                        pe.wait_ge(f_xT[l], j["xT"])
                    nc.tensor.transpose(ps_a[i % 2][:, 0:P], xt[i][:, 0:D], ident).then_inc(f_xtr[l], 1)

                def down(i, hid_count, y_count):
                    pe.wait_ge(f_hid[l], hid_count)
                    if y_count is not None:
                        pe.wait_ge(f_y[l], y_count)
                    bank = (ps_n, ps_d)[i % 2]
                    for c in range(HC):
                        last = nc.tensor.matmul(bank[:, 0:D], hid[i][:, c, :], fw[i][:, dn0 + c * D:dn0 + (c + 1) * D], start=c == 0, stop=c == HC - 1)
                    last.then_inc(f_dn[l], 1)

                def body(r, first):
                    for i in range(SLOTS):
                        j = r * SLOTS + i
                        turn(i, {"ld": 32 * (r + 1), "xT": (None if first and i < 2 else j - 1)})
                        if not (first and i == 0):
                            down((i - 1) % SLOTS, j, None if first and i < 3 else j - 2)
                        pe.wait_ge(f_xT[l], j + 1)
                        if not (first and i < 2):
                            pe.wait_ge(f_hid[l], j - 1)
                        for c in range(up):
                            last = nc.tensor.matmul(ps_s[i % 2][:, c * P:(c + 1) * P], fw[i][:, c * P:(c + 1) * P], xT[i][:, :], start=True, stop=True)
                        last.then_inc(f_up[l], 1)

                rounds(pe, l, body)
                down(SLOTS - 1, FT[l], FT[l] - 2)

            pe.wait_ge(ld_c, 64)
            for l in range(LAYERS):
                n0 = NB * l
                keys_values(l)
                for n in (n0, n0 + 1):
                    front(n)
                    project(n)
                    if n == n0:
                        if l:
                            pe.wait_ge(s_masked, 1)
                            transposes(lambda i: augt[1][:, i, :], mask_tr, maskT_ok, 1)
                        for u in range(TPB * GROUPS):
                            scores_for_max(n, u)
                augmenting(n0)
                for b in range(NB + 1):
                    n = n0 + b
                    for s in range(NS):
                        if b < NB:
                            scores(n, s)
                        if b and s == 0:
                            weigh(n - 1, KT - 1)
                        if b and s == 2:
                            den_to_tokens(n - 1)
                        if b and s == 3:
                            rden_to_dims(n - 1)
                        if b < NB - 2 and s == 4:
                            front(n + 2)
                        if b and s == 5:
                            output(n - 1)
                        if b < NB and s == 5:
                            weigh(n, 0)
                        if b < NB - 2 and s == 6:
                            project(n + 2)
                        if b and s == 7:
                            routed_T(n - 1)
                        if b and s == 8:
                            router(n - 1)
                        if b < NB and s == 9:
                            weigh(n, 1)
                        if b and s == 10:
                            ranks(n - 1)
                        if b < NB - 1 and s >= 1:
                            for u in MAX_UNITS[s]:
                                scores_for_max(n + 1, u)
                    if b < NB - 1:
                        augmenting(n + 1)
                totals(l)
                tiles_pe(l)

        @block.vector
        def _(dve):
            unit, chain = Count(), Count()

            def link(ins):
                ins.then_inc(s_dve, 1)
                dve.wait_ge(s_dve, chain.next() + 1)

            def ring():
                u = unit.next()
                dve.wait_ge(ring_full, u + 1)
                return ps_a[u % 2]

            def keys_values(l):
                wl = w[l]
                shape = "p (b k) -> p b k"
                a = ring()[:, 0:NB * KEYS]
                if l == 0:
                    nc.vector.tensor_tensor(kr1[:, :].rearrange(shape, b=NB), a.rearrange(shape, b=NB), bcast(cos[:, 0:KEYS], 1, NB),
                                            ALU.mult).then_inc(ring_used, 1)
                    a = ring()[:, 0:NB * KEYS]
                    nc.vector.tensor_tensor(kr2[:, :].rearrange(shape, b=NB), a.rearrange(shape, b=NB), bcast(sin[:, 0:KEYS], 1, NB),
                                            ALU.mult).then_inc(ring_used, 1)
                    dve.wait_ge(ring_used, unit.n)
                    link(nc.vector.tensor_tensor(kr1[:, :], kr1[:, :], kr2[:, :], ALU.add))
                else:
                    nc.vector.tensor_scalar(kr1[:, :], a, wl[:, W_BK:W_BK + 1], None, ALU.add).then_inc(ring_used, 1)
                    dve.wait_ge(ring_used, unit.n)
                link(nc.vector.tensor_copy(khl[0][:, :], kr1[:, :]))
                link(nc.vector.tensor_tensor(khl[1][:, :], kr1[:, :], khl[0][:, :].bitcast(F32), ALU.subtract))
                if l:
                    dve.wait_ge(kspread, 256)
                for i in range(2):
                    for b in range(NB):
                        last = nc.vector.tensor_tensor(kblk[i][:, b, :, :], bcast(khl[i][:, b * KEYS:(b + 1) * KEYS].bitcast(F32), 1, HPG),
                                                       bcast(hm, 2, KEYS), ALU.mult)
                last.then_inc(s_kblk, 1)
                for j in range(KT):
                    kk = KSIZE[j]
                    a = ring()
                    dst = vb[0:kk, j, :, :].rearrange("p b (g c) -> p (b g) c", g=GROUPS)
                    mask = bcast(hmv[0:kk, j, :], 1, NB * GROUPS)
                    nc.vector.tensor_tensor(vtmp[0:kk, :].rearrange("p (b c) -> p b c", b=NB), a[0:kk, :].rearrange("p (b c) -> p b c", b=NB),
                                            bcast(wl[0:kk, W_BV:W_BV + D], 1, NB), ALU.add).then_inc(ring_used, 1)
                    dve.wait_ge(ring_used, unit.n)
                    nc.vector.tensor_tensor(dst, vtmp[0:kk, :].rearrange("p (q c) -> p q c", c=32), mask, ALU.mult).then_inc(s_vb, 1)
                    dve.wait_ge(s_vb, KT * l + j + 1)
                nc.vector.tensor_scalar(tgbo[l][:, :], wl[:, W_BO:W_BO + D], tg[:, 2 * l:2 * l + 1], None, ALU.mult).then_inc(s_tgbo, 1)

            def statistics(src, st_, mv_, done):
                for i in range(TPB):
                    last = nc.vector.bn_stats(st_[:, i, :], src[:, i, :])
                link(last)
                for i in range(TPB):
                    last = nc.vector.bn_aggr(mv_[:, i, :], st_[:, i, :])
                last.then_inc(done, 1)

            def normalise(src, dst, mv_, rstd_, done):
                for i in range(TPB):
                    last = nc.vector.tensor_scalar(dst(i), src[:, i, :], mv_[:, i, 0:1], rstd_[:, i:i + 1], ALU.subtract, ALU.mult)
                last.then_inc(done, 1)

            def xs(n):
                b = n % NB
                return x[:, b * TPB:(b + 1) * TPB, :]

            def front_stats(n):
                if n < NB:
                    dve.wait_ge(ld_x[n], 16)
                if n:
                    dve.wait_ge(rstd1_ok, n)
                statistics(xs(n), st, mv, var1)

            def front_normalise(n):
                dve.wait_ge(rstd1_ok, n + 1)
                dve.wait_ge(var1, n + 1)
                if n:
                    dve.wait_ge(nrmT_ok, n)
                normalise(xs(n), lambda i: nrm[:, i, :], mv, rstd, nrm_ok)

            def rotate(n):
                wl = w[n // NB]
                if n:
                    dve.wait_ge(ql_ok, n)
                a = ring()
                if n < NB:
                    nc.vector.tensor_tensor(qr1[:, :], a[:, :], cos, ALU.mult).then_inc(ring_used, 1)
                    a = ring()
                    nc.vector.tensor_tensor(qr2[:, :], a[:, :], sin, ALU.mult).then_inc(ring_used, 1)
                    dve.wait_ge(ring_used, unit.n)
                    dve.sem_inc(rot_ok, 1)
                else:
                    nc.vector.tensor_scalar(qr1[:, :], a[:, :], wl[:, W_BQ:W_BQ + 1], None, ALU.add).then_inc(ring_used, 1)
                    dve.wait_ge(ring_used, unit.n)
                    dve.sem_inc(q_ok, 1)

            def low_q(n):
                dve.wait_ge(qh_ok, n + 1)
                dve.wait_ge(q_ok, n + 1)
                if n:
                    dve.wait_ge(qspread, 256 * n)
                nc.vector.tensor_tensor(qhl[1][:, :], qr1[:, :], qhl[0][:, :].bitcast(F32), ALU.subtract).then_inc(ql_ok, 1)

            def maxima(n, u):
                i, g = divmod(u, GROUPS)
                a = ring()
                nc.vector.tensor_reduce(negm[:, i, g * HPG:(g + 1) * HPG], a[:, 0:GK].rearrange("p (h k) -> p h k", h=HPG),
                                        AX.X, ALU.max, negate=True).then_inc(ring_used, 1)

            def split_max(n):
                l = n // NB
                at = augt[l]
                dve.wait_ge(ring_used, unit.n)
                if n == 0:
                    dve.wait_ge(s_const, 1)
                if n % NB:
                    dve.wait_ge(augt_tr, n)
                if l:
                    link(nc.vector.tensor_scalar(negm[:, :, :], negm[:, :, :], CLAMP, None, ALU.min))
                link(nc.vector.tensor_copy(negmh[:, :, :], negm[:, :, :]))
                nc.vector.tensor_copy(at[:, :, 0:HEADS], negmh[:, :, :].bitcast(F32))
                nc.vector.tensor_tensor(at[:, :, HEADS:2 * HEADS], negm[:, :, :], negmh[:, :, :].bitcast(F32), ALU.subtract).then_inc(augt_ok, 1)

            def recip_den(n):
                dve.wait_ge(den_tr, n + 1)
                if n:
                    dve.wait_ge(rdx_ok, n)
                link(nc.vector.tensor_scalar(rd[:, :, :], ps_t[:, :].rearrange("p (t h d) -> p t h d", t=TPB, d=HD)[:, :, :, 0], 1e-30, None, ALU.max))
                nc.vector.reciprocal(rd[:, :, :], rd[:, :, :]).then_inc(rd_ok, 1)

            def weigh_out(n):
                dve.wait_ge(rd_tr, n + 1)
                dve.wait_ge(nd_ok, 2 * n + 2)
                nc.vector.tensor_tensor(att[:, :], ps_t[:, :], nums[:, :], ALU.mult).then_inc(att_ok, 1)

            def residual(n):
                l = n // NB
                a = ring()
                dve.wait_ge(xb_ok, n + 1)
                nc.vector.scalar_tensor_tensor(xs(n).rearrange("p t c -> p (t c)"), a[:, :], tg[:, 2 * l:2 * l + 1],
                                               xs(n).rearrange("p t c -> p (t c)"), ALU.mult, ALU.add).then_inc(ring_used, 1)
                dve.wait_ge(ring_used, unit.n)
                statistics(xs(n), st2, mv2, var2)

            def normalise2(n):
                dve.wait_ge(rstd2_ok, n + 1)
                dve.wait_ge(var2, n + 1)
                b = n % NB
                normalise(xs(n), lambda i: pay[0][:, b * TPB + i, 0:D], mv2, rstd2, nrm2_ok)

            def best(src, m, one_hot):
                link(nc.vector.tensor_reduce(m[:, :], src[:, :, :], AX.X, ALU.max))
                link(nc.vector.tensor_tensor(wt[:, :, :], src[:, :, :], bcast(m[:, :], 2, E), ALU.is_equal))
                link(nc.vector.tensor_tensor(wt[:, :, :], wt[:, :, :], bcast(desc, 1, TPB), ALU.mult))
                link(nc.vector.tensor_reduce(wm[:, :], wt[:, :, :], AX.X, ALU.max))
                link(nc.vector.tensor_tensor(one_hot[:, :, :], wt[:, :, :], bcast(wm[:, :], 2, E), ALU.is_equal))

            def choose(n):
                l, b = divmod(n, NB)
                a = ring()
                link(nc.vector.tensor_tensor(lg[:, :, :], a[:, 0:TPB * E].rearrange("p (t e) -> p t e", t=TPB),
                                             bcast(w[l][:, W_BR:W_BR + E], 1, TPB), ALU.add))
                dve.sem_inc(ring_used, 1)
                best(lg, mx[0], oh[0])
                if l == 0:
                    nc.vector.tensor_tensor(shifted[:, :, :], lg[:, :, :], bcast(mx[0][:, :], 2, E), ALU.subtract).then_inc(sh_ok, 1)
                    nc.vector.tensor_copy(ohs[:, :, :], oh[0][:, :, :])
                    src = oh[0]
                else:
                    link(nc.vector.scalar_tensor_tensor(lg2[:, :, :], oh[0][:, :, :], MASKED, lg[:, :, :], ALU.mult, ALU.add))
                    best(lg2, mx[1], oh[1])
                    nc.vector.tensor_tensor(shifted[:, :, 0], mx[1][:, :], mx[0][:, :], ALU.subtract).then_inc(sh_ok, 1)
                    link(nc.vector.tensor_tensor(ohs[:, :, :], oh[0][:, :, :], oh[1][:, :, :], ALU.add))
                    src = ohs
                for i in range(TPB):
                    t = b * TPB + i
                    link(nc.vector.tensor_tensor(run[l][:, t + 1, :], run[l][:, t, :], src[:, i, :], ALU.add))
                dve.sem_inc(ohs_ok, 1)

            def gate(n):
                l, b = divmod(n, NB)
                t0 = b * TPB
                dve.wait_ge(ex_ok, n + 1)
                scale = tg[:, 2 * l + 1:2 * l + 2]
                gcol = [pay[c][:, t0:t0 + TPB, D + 1] for c in range(2)]
                if l == 0:
                    link(nc.vector.tensor_reduce(se[:, :], expd[:, :, :], AX.X, ALU.add))
                    link(nc.vector.reciprocal(re[:, :], se[:, :]))
                    nc.vector.tensor_scalar(gcol[0], re[:, :], scale, None, ALU.mult)
                else:
                    link(nc.vector.tensor_scalar(re[:, :], se[:, :], 1.0, None, ALU.add))
                    link(nc.vector.reciprocal(wm[:, :], re[:, :]))
                    link(nc.vector.tensor_scalar(gcol[0], wm[:, :], scale, 0.5, ALU.mult, ALU.mult))
                    nc.vector.tensor_tensor(gcol[1], gcol[0], se[:, :], ALU.mult)
                for c in range(CHOICES[l]):
                    nc.vector.tensor_copy(pay[c][:, t0:t0 + TPB, D].bitcast(I32), ids[:, c, t0:t0 + TPB])

            def slots(n):
                l, b = divmod(n, NB)
                a = ring()
                link(nc.vector.tensor_tensor(rk[:, :, :], a[:, 0:TPB * E].rearrange("p (t e) -> p t e", t=TPB), bcast(ebase, 1, TPB), ALU.add))
                dve.sem_inc(ring_used, 1)
                if l:
                    dve.wait_ge(pay2_ok, n - NB + 1)
                for c in range(CHOICES[l]):
                    link(nc.vector.tensor_tensor(wt[:, :, :], rk[:, :, :], oh[c][:, :, :], ALU.mult))
                    link(nc.vector.tensor_reduce(slotf[:, :], wt[:, :, :], AX.X, ALU.add))
                    last = nc.vector.tensor_copy(slot[c][:, b * TPB:(b + 1) * TPB], slotf[:, :])
                    if c < CHOICES[l] - 1:
                        link(last)
                last.then_inc(slot_ok, 1)

            def plan(l):
                nt = FT[l]
                a = ring()
                link(nc.vector.tensor_tensor(gt[:, :, :], bcast(a[:, 0:E], 2, NT), bcast(cst[:, C_K128:C_K128 + NT], 1, E), ALU.is_gt))
                dve.sem_inc(ring_used, 1)
                link(nc.vector.tensor_reduce(tiles[:, :], gt[:, :, :], AX.X, ALU.add))
                link(nc.vector.tensor_tensor(cumx[:, :, :], bcast(tiles[:, :], 1, E), cst[:, C_LT:C_LT + E * E].rearrange("p (e f) -> p e f", e=E), ALU.mult))
                link(nc.vector.tensor_reduce(cum[:, :], cumx[:, :, :], AX.X, ALU.add))
                jj = cst[:, C_J:C_J + nt]
                link(nc.vector.tensor_tensor(le[:, 0:nt, :], bcast(cum[:, :], 1, nt), bcast(jj, 2, E), ALU.is_le))
                nc.vector.tensor_tensor(let[:, 0:nt, :], le[:, 0:nt, :], bcast(tiles[:, :], 1, nt), ALU.mult)
                link(nc.vector.tensor_reduce(ej[:, 0:nt], le[:, 0:nt, :], AX.X, ALU.add))
                link(nc.vector.tensor_reduce(kj[:, 0:nt], let[:, 0:nt, :], AX.X, ALU.add))
                link(nc.vector.tensor_tensor(kj[:, 0:nt], jj, kj[:, 0:nt], ALU.subtract))
                link(nc.vector.scalar_tensor_tensor(bj[:, 0:nt], ej[:, 0:nt], float(NT), kj[:, 0:nt], ALU.mult, ALU.add))
                nc.vector.tensor_scalar(meta[l][0:1, 0, :], ej[0:1, 0:nt], float(E - 1), float(P * FW[l]), ALU.min, ALU.mult)
                nc.vector.tensor_scalar(meta[l][0:1, 1, :], bj[0:1, 0:nt], float(DUMMY), float(P * PAY), ALU.min, ALU.mult).then_inc(meta_ok, 1)

            def tiles_dve(l):
                def finish(i, count, put):
                    dve.wait_ge(f_dn[l], count)
                    if put is not None:
                        dve.wait_ge(f_put[l][i], put)
                    bank = (ps_n, ps_d)[i % 2]
                    if l == 0:
                        link_f = nc.vector.tensor_tensor(yb[i], bank[:, 0:D], fw[i][:, 2 * HID:2 * HID + D], ALU.add)
                        link_f.then_inc(f_th[l], 1)
                        dve.wait_ge(f_th[l], count)
                        src = yb[i]
                    else:
                        src = bank[:, 0:D]
                    nc.vector.tensor_copy(rows_at[i][:, :], xt[i][:, D:D + 1].bitcast(I32))
                    nc.vector.tensor_scalar(yo[i][:, :], src, xt[i][:, D + 1:D + 2], None, ALU.mult).then_inc(f_y[l], 1)

                def body(r, first):
                    for i in range(SLOTS):
                        j = r * SLOTS + i
                        if l == 0:
                            dve.wait_ge(f_xtr[l], j + 1)
                            if not first:
                                dve.wait_ge(f_up[l], j + 1 - SLOTS)
                            nc.vector.tensor_copy(xT[i][:, :], ps_a[i % 2][:, 0:P]).then_inc(f_xT[l], 1)
                        else:
                            dve.wait_ge(f_th[l], j + 1)
                            nc.vector.scalar_tensor_tensor(silu[i % 2], tanhs[i % 2], 1.0, ps_s[i % 2][:, 0:HID], ALU.add, ALU.mult).then_inc(f_silu[l], 1)
                            dve.wait_ge(f_silu[l], j + 1)
                            if not first:
                                dve.wait_ge(f_dn[l], j + 1 - SLOTS)
                            nc.vector.tensor_tensor(hid[i][:, :, :].rearrange("p c t -> p (c t)"), silu[i % 2], ps_s[i % 2][:, HID:2 * HID], ALU.mult).then_inc(f_hid[l], 1)
                        if not (first and i == 0):
                            k = (i - 1) % SLOTS
                            finish(k, j, None if first or not i else 16 * r)
                    if not first:
                        dve.wait_ge(f_put[l][SLOTS - 1], 16 * r)

                rounds(dve, l, body)
                finish(SLOTS - 1, FT[l], None)

            def add_results(l, b):
                dve.wait_ge(y_ld[l][b], 16 * CHOICES[l])
                dst = xs(b).rearrange("p t c -> p (t c)")
                for c in range(CHOICES[l]):
                    last = nc.vector.tensor_tensor(dst, dst, yin[c][b], ALU.add)
                    if c < CHOICES[l] - 1:
                        link(last)
                last.then_inc(x_ok, 1)

            dve.wait_ge(ld_c, 64)
            nc.vector.tensor_copy(prefix16[:, :], cst[:, C_U:C_U + P])
            dve.wait_ge(ld_m, 16)
            dve.wait_ge(s_const, 1)
            nc.vector.tensor_scalar(augt[1][:, :, AUG_KEY:AUG_KEY + KEYS], maski[:, :, :], 0.0, MASKED, ALU.is_equal, ALU.mult).then_inc(s_masked, 1)
            dve.wait_ge(s_tanh, 1)
            dve.wait_ge(ld_w[0], 16)
            front_stats(0)
            for l in range(LAYERS):
                n0 = NB * l
                if l:
                    dve.wait_ge(ld_w[1], 16)
                keys_values(l)
                if l:
                    add_results(0, 0)
                    dve.wait_ge(x_ok, 1)
                    front_stats(n0)
                front_normalise(n0)
                rotate(n0)
                low_q(n0)
                if l:
                    add_results(0, 1)
                    dve.wait_ge(x_ok, 2)
                front_stats(n0 + 1)
                front_normalise(n0 + 1)
                for u in range(TPB * GROUPS):
                    maxima(n0, u)
                split_max(n0)
                rotate(n0 + 1)
                low_q(n0 + 1)
                for b in range(NB + 1):
                    n = n0 + b
                    for s in range(NS):
                        if b and s == 2:
                            recip_den(n - 1)
                        if b and s == 3:
                            weigh_out(n - 1)
                        if b < NB - 2 and s == 3:
                            if l:
                                add_results(0, b + 2)
                                dve.wait_ge(x_ok, b + 3)
                            front_stats(n + 2)
                        if b < NB - 2 and s == 4:
                            front_normalise(n + 2)
                        if b and s == 5:
                            residual(n - 1)
                        if b < NB - 2 and s == 6:
                            rotate(n + 2)
                        if b and s == 6:
                            normalise2(n - 1)
                        if b < NB - 2 and s == 7:
                            low_q(n + 2)
                        if b and s == 8:
                            choose(n - 1)
                        if b and s == 10:
                            gate(n - 1)
                            slots(n - 1)
                        if b < NB - 1 and s >= 1:
                            for u in MAX_UNITS[s]:
                                maxima(n + 1, u)
                    if b < NB - 1:
                        split_max(n + 1)
                plan(l)
                tiles_dve(l)
            for b in range(NB):
                add_results(1, b)


MAX_UNITS = [[]] + [[2 * i, 2 * i + 1] for i in range(5)] + [[10 + i] for i in range(6)]


def _constants():
    import numpy as np

    c = np.zeros((P, C_END), np.float32)
    c[:, C_ID:C_ID + P] = np.eye(P)
    inv = (1.0 / np.float32(10000.0) ** (np.arange(0, HD, 2, dtype=np.float32) / np.float32(HD))).astype(np.float32)
    ang = (np.arange(SEQ, dtype=np.float32)[:, None] * inv[None, :]).astype(np.float32)
    for p in range(P):
        d = p % HD
        c[p, C_COS:C_COS + SEQ] = np.cos(ang[:, d % (HD // 2)])
        c[p, C_SIN:C_SIN + SEQ] = np.sin(ang[:, d % (HD // 2)]) * (-1 if d < HD // 2 else 1)
        c[p, C_HM + (p // HD) % HPG] = 1
    aug = np.zeros((P, GROUPS, GK), np.float32)
    for j in range(KT):
        for r in range(KSIZE[j]):
            h = (KROWS * j + r) // KEYS
            c[r, C_HMV + 32 * j + HD * h:C_HMV + 32 * j + HD * (h + 1)] = 1
    for g in range(GROUPS):
        for f in range(GK):
            h, k = divmod(f, KEYS)
            aug[g * HPG + h, g, f] = aug[HEADS + g * HPG + h, g, f] = 1
            aug[AUG_KEY + k, g, f] = 1
    c[:, C_U:C_U + P] = np.triu(np.ones((P, P)), 1)
    c[:, C_DESC:C_DESC + E] = E - np.arange(E)
    c[:, C_EB:C_EB + E] = TOKENS * np.arange(E)
    c[:, C_K128:C_K128 + NT] = P * np.arange(NT)
    c[:, C_LT:C_LT + E * E] = np.tril(np.ones((E, E))).reshape(-1)
    c[:, C_J:C_END] = np.arange(max(FT))
    token = np.arange(P)[:, None] + P * np.arange(NT)[None, :]
    ids = np.stack([token, token + TOKENS], 1).astype(np.int32)
    pad = np.zeros((P, PAY), np.float32)
    pad[:, D] = np.full(P, NOROW, np.int32).view(np.float32)
    return c, aug.reshape(P, -1), ids, pad


def kernel(**a):
    import numpy as np
    import concourse.bacc as bacc
    from concourse.bass_utils import run_bass_kernel_spmd

    a = {k: np.asarray(v) for k, v in a.items()}
    half_turned = np.arange(D).reshape(HEADS, 2, HD // 2)[:, ::-1].reshape(-1)
    rows = lambda v: np.broadcast_to(v[None, :], (P, v.shape[0]))
    col = lambda v: v[:, None]
    zero = np.zeros(D, np.float32)

    def attention(wq, wk, wv, wo, bq, bk, bv, bo, wr, br):
        return np.ascontiguousarray(np.concatenate(
            [wq, wq[:, half_turned], wk, wk[:, half_turned], wv, wo, rows(bv), rows(bo), wr, rows(br),
             col(bq), col(bk)], 1))

    wkv = a["L0_xattn_Wkv"]
    w0 = attention(a["L0_xattn_Wq"], wkv[:, :D], wkv[:, D:], a["L0_xattn_Wo"], zero, zero, zero, a["L0_xattn_bo"],
                   a["L0_ffn_Wr"], a["L0_ffn_br"])
    w1 = attention(a["L1_xattn_Wq"], a["L1_xattn_Wk"], a["L1_xattn_Wv"], a["L1_xattn_Wo"], a["L1_xattn_bq"], a["L1_xattn_bk"],
                   a["L1_xattn_bv"], a["L1_xattn_bo"], a["L1_ffn_w_gate"].T, np.zeros(E, np.float32))
    by_chunk = lambda m: m.reshape(E, HC, P, D).transpose(0, 2, 1, 3).reshape(E, P, HC * D)
    f0 = np.ascontiguousarray(np.concatenate(
        [a["L0_ffn_W1"], by_chunk(a["L0_ffn_W2"]), np.broadcast_to(a["L0_ffn_b2"][:, None, :], (E, P, D)),
         a["L0_ffn_b1"].reshape(E, HC, P).transpose(0, 2, 1)], 2))
    f1 = np.ascontiguousarray(np.concatenate(
        [a["L1_ffn_w_gate_proj"].transpose(0, 2, 1), a["L1_ffn_w_up_proj"].transpose(0, 2, 1),
         by_chunk(a["L1_ffn_w_down_proj"].transpose(0, 2, 1))], 2))
    const, aug, ids, pad = _constants()
    arrays = {
        "x_in": np.ascontiguousarray(a["x"].reshape(NT, P, D).transpose(1, 0, 2)),
        "ctx_in": np.ascontiguousarray(a["ctx_1024"].transpose(2, 0, 1)),
        "mask_in": np.ascontiguousarray(a["mask_SxS2_ik0"].reshape(TPB, P, KEYS).transpose(1, 0, 2)),
        "gates_in": np.ascontiguousarray(rows(np.concatenate([a["g_xattn"][:1], a["g_ffn"][:1], a["g_xattn"][1:], a["g_ffn"][1:]]))),
        "w0_in": w0, "w1_in": w1, "f0_in": f0, "f1_in": f1,
        "const_in": const, "aug_in": aug, "ids_in": ids, "pad_in": pad,
    }
    nc = bacc.Bacc("TRN2", target_bir_lowering=False, num_devices=1)
    aps = {k: nc.dram_tensor(k, v.shape, mybir.dt.from_np(v.dtype), kind="ExternalInput").ap() for k, v in arrays.items()}
    out = nc.dram_tensor("out", (P, NT, D), F32, kind="ExternalOutput").ap()
    two_layers(nc, **aps, out=out)
    r = run_bass_kernel_spmd(nc, [arrays], core_ids=[0])
    got = r.results[0]["out"]
    return np.ascontiguousarray(got.transpose(1, 0, 2).reshape(NB, SEQ, D))
```

```python
from contextlib import ExitStack

import concourse.bass as bass
from concourse import mybir

F32 = mybir.dt.float32
F32R = mybir.dt.float32r
BF16 = mybir.dt.bfloat16
I32 = mybir.dt.int32
ALU = mybir.AluOpType
ACT = mybir.ActivationFunctionType
AX = mybir.AxisListType

P = 128
D = 128
LAYERS = 2
NB, SEQ, KEYS = 4, 512, 77
TPB = SEQ // P
NT = NB * TPB
TOKENS = NB * SEQ
HEADS, HD = 16, 8
GROUPS, HPG = 4, 4
GK = HPG * KEYS
KT = 3
KROWS = 103
KSIZE = [min(KROWS, GK - KROWS * j) for j in range(KT)]
NS = KT * GROUPS
SCALE = float(HD) ** -0.5
EPS = 1e-5
E, HID = 8, 256
HC = HID // P
MASKED = -1e30
CLAMP = 1e25
SLOTS = 8
SHORT = 4
LAG_UP, LAG_DOWN, LAG_OUT = 1, 3, 4
CHOICES = [1, 2]
FT = [-(-((TOKENS * c + E * (P - 1)) // P) // SLOTS) * SLOTS for c in CHOICES]
REGION = TOKENS + P
BLOCKS = REGION // P
DUMMY = E * BLOCKS
PAY = D + 2
FW = [2 * HID + D + HC, 3 * HID]
NOROW = 1 << 20

C_ID, C_COS, C_SIN = 0, P, P + SEQ
C_HM = C_SIN + SEQ
C_HMV = C_HM + HPG
C_U = C_HMV + KT * 32
C_DESC = C_U + P
C_EB = C_DESC + E
C_K128 = C_EB + E
C_LT = C_K128 + NT
C_J = C_LT + E * E
C_END = C_J + max(FT)
W_Q, W_QR, W_K, W_KR, W_V, W_O, W_BV, W_BO = [D * i for i in range(8)]
W_R = 8 * D
W_BR = W_R + E
W_BQ = W_BR + E
W_BK = W_BQ + 1
W_END = W_BK + 1
AUG_KEY = 32

AT = {
    "results": -28, "stats": -27, "normalise": -25, "bias": -24, "turn": -22, "project": -20, "high": -19, "low": -18,
    "split": -4, "augment": -3,
    "weigh0": 5, "weigh1": 9, "weigh2": 13, "sums": 13, "den": 15, "widen": 16, "rden": 17,
    "output": 18, "stats2": 19, "normalise2": 22, "turn2": 23, "router": 24, "route_exp": 25, "ranks": 26,
    "scatter0": 27, "scatter1": 28, "scatter2": 32, "scatter3": 34,
}
MAX_FIRST, MAX_STEPS = -11, 8
FRONT = {"results", "stats", "normalise", "bias", "turn", "project", "high", "low"}
SECOND_FRONT = 4
STEPS = range(AT["results"], NS * (NB - 1) + AT["scatter3"] + 1)
LAST = NS * (NB - 1)
KEYS_AT = [-26, LAST + 14]
VALUES_AT = [[-15, -14, -13], [LAST + 16, LAST + 20, LAST + 21]]
BLOCKS_AT = [-17, LAST + 27]
MASK_AT = -5


def due(stage, k):
    return [b for b in range(NB) if (SECOND_FRONT if b == 1 and stage in FRONT else NS * b) + AT[stage] == k]


def max_units(k):
    per = TPB * GROUPS // MAX_STEPS
    return [(b, (k - NS * b - MAX_FIRST) * per + u) for b in range(NB) for u in range(per)
            if 0 <= k - NS * b - MAX_FIRST < MAX_STEPS]


def bcast(ap, axis, n):
    ap = ap.unsqueeze(axis)
    shape = list(ap.shape)
    shape[axis] = n
    return ap.broadcast_to(shape)


def two_layers(nc, x_in, ctx_in, mask_in, gates_in, w0_in, w1_in, f0_in, f1_in, const_in, aug_in, ids_in, pad_in, out):
    w_in, f_in = [w0_in, w1_in], [f0_in, f1_in]
    with ExitStack() as ctx:
        def sb(name, shape, dt=F32):
            return ctx.enter_context(nc.sbuf_tensor(name, shape, dt))

        def pb(name):
            return ctx.enter_context(nc.psum_tensor(name, [P, 512], F32))

        def sem(name):
            return ctx.enter_context(nc.semaphore(name))

        routed = [nc.dram_tensor(f"routed{l}", (DUMMY * P + P, PAY), F32, kind="Internal").ap() for l in range(LAYERS)]
        q_rows = nc.dram_tensor("q_rows", (LAYERS * NB, GROUPS, 2, 32, SEQ), F32, kind="Internal").ap()
        k_rows = nc.dram_tensor("k_rows", (LAYERS, GROUPS, 4, 32, NB * KEYS), F32, kind="Internal").ap()
        expert_out = [nc.dram_tensor(f"expert_out{l}", (CHOICES[l] * TOKENS, D), F32, kind="Internal").ap() for l in range(LAYERS)]

        x = sb("x", [P, NT, D])
        cst = sb("cst", [P, C_END])
        ident = cst[:, C_ID:C_ID + P]
        cos, sin = cst[:, C_COS:C_COS + SEQ], cst[:, C_SIN:C_SIN + SEQ]
        hm = cst[:, C_HM:C_HM + HPG]
        hmv = cst[:, C_HMV:C_HMV + KT * 32].rearrange("p (j c) -> p j c", j=KT)
        desc, ebase = cst[:, C_DESC:C_DESC + E], cst[:, C_EB:C_EB + E]
        probs = [sb(f"probs{i}", [P, NS, SEQ]) for i in range(2)]
        spare = [probs[i][:, :, :].rearrange("p s c -> p (s c)") for i in range(2)]
        augf = spare[1][:, 0:GROUPS * GK]
        aug = sb("aug", [P, GROUPS, GK], F32R)
        ids = sb("ids", [P, 2, NT], I32)
        pad = sb("pad", [P, PAY])
        cx4 = sb("cx4", [P, NB, HPG, KEYS])
        maski = sb("maski", [P, TPB, KEYS], I32)
        gates = sb("gates", [P, 4])
        tg = sb("tg", [P, 4])
        w = [sb(f"w{l}", [P, W_END]) for l in range(LAYERS)]
        prefix16 = sb("prefix16", [P, P], BF16)
        ones16 = sb("ones16", [P, P], BF16)
        half = sb("half", [P, TPB])
        kr1 = sb("kr1", [P, NB * KEYS])
        kr2 = sb("kr2", [P, NB * KEYS])
        khl = [sb(f"khl{i}", [P, NB * KEYS], F32R) for i in range(2)]
        ksp = spare[1][:, GROUPS * GK:2 * GROUPS * GK]
        ks = sb("ks", [P, GROUPS, NB, GK], F32R)
        ks_by_head = ks[:, :, :, :].rearrange("p g b c -> p (g b) c")
        vb = sb("vb", [P, KT, NB, D])
        tgbo = [sb(f"tgbo{l}", [P, D]) for l in range(LAYERS)]
        st = sb("st", [P, TPB, 6])
        mv = sb("mv", [P, TPB, 2])
        ve = sb("ve", [P, TPB])
        rstd = sb("rstd", [P, TPB])
        nrm = sb("nrm", [P, TPB, D])
        nT = sb("nT", [P, SEQ])
        qr1 = sb("qr1", [P, SEQ])
        qr2 = sb("qr2", [P, SEQ])
        qhl = [sb(f"qhl{i}", [P, SEQ], F32R) for i in range(2)]
        qs = [sb(f"qs{i}", [P, GROUPS, SEQ], F32R) for i in range(3)]
        negm = sb("negm", [P, TPB, HEADS])
        negmh = sb("negmh", [P, TPB, HEADS], F32R)
        augt = [sb(f"augt{l}", [P, TPB, P]) for l in range(LAYERS)]
        augT = [sb(f"augT{i}", [P, SEQ], F32R) for i in range(2)]
        maskT = sb("maskT", [P, SEQ], F32R)
        nums = sb("nums", [P, SEQ])
        dens = sb("dens", [P, SEQ])
        rd = sb("rd", [P, TPB, HEADS])
        rdx = dens
        att = sb("att", [P, SEQ])
        st2 = sb("st2", [P, TPB, 6])
        mv2 = sb("mv2", [P, TPB, 2])
        ve2 = sb("ve2", [P, TPB])
        rstd2 = sb("rstd2", [P, TPB])
        pay = [sb(f"pay{c}", [P, NT, PAY]) for c in range(2)]
        nT2 = sb("nT2", [P, SEQ])
        lg = sb("lg", [P, TPB, E])
        lg2 = sb("lg2", [P, TPB, E])
        wt = sb("wt", [P, TPB, E])
        wm = sb("wm", [P, TPB])
        mx = [sb(f"mx{i}", [P, TPB]) for i in range(2)]
        oh = [sb(f"oh{i}", [P, TPB, E], BF16) for i in range(2)]
        ohs = sb("ohs", [P, TPB, E], BF16)
        run = [sb(f"run{l}", [P, NT + 1, E], BF16) for l in range(LAYERS)]
        shifted = sb("shifted", [P, TPB, E])
        expd = sb("expd", [P, TPB, E])
        se = sb("se", [P, TPB])
        re = sb("re", [P, TPB])
        rk = sb("rk", [P, TPB, E])
        slotf = sb("slotf", [P, TPB])
        slot = [sb(f"slot{c}", [P, NT], I32) for c in range(2)]
        gt = sb("gt", [P, E, NT])
        tiles = sb("tiles", [P, E])
        cumx = sb("cumx", [P, E, E])
        cum = sb("cum", [P, E])
        le = sb("le", [P, max(FT), E])
        let = sb("let", [P, max(FT), E])
        ej = sb("ej", [P, max(FT)])
        kj = sb("kj", [P, max(FT)])
        bj = sb("bj", [P, max(FT)])
        meta = [sb(f"meta{l}", [1, 2, FT[l]], I32) for l in range(LAYERS)]
        pad_row = sb("pad_row", [1, E])
        pad_at = [sb(f"pad_at{l}", [1, E], I32) for l in range(LAYERS)]
        xt = [sb(f"xt{i}", [P, PAY])[:, :] for i in range(SHORT)] + [spare[1][:, (8 + i) * SEQ:(8 + i) * SEQ + PAY] for i in range(SLOTS - SHORT)]
        fw = [spare[0][:, i * max(FW):(i + 1) * max(FW)] for i in range(SLOTS)]
        xT = [sb(f"xT{i}", [P, P]) for i in range(SHORT)]
        hid = [(nums, dens)[i // 2][:, (i % 2) * HID:(i % 2 + 1) * HID].rearrange("p (c t) -> p c t", c=HC) for i in range(SHORT)]
        tanhs = [qr1[:, i * HID:(i + 1) * HID] for i in range(2)]
        silu = [qr2[:, i * HID:(i + 1) * HID] for i in range(2)]
        rows_at = [sb(f"rows_at{i}", [P, 1], I32) for i in range(SHORT)]
        yb = [qr1[:, i * D:(i + 1) * D] for i in range(SHORT)]
        yo = [sb(f"yo{i}", [P, D]) for i in range(SHORT)]
        yin = [[sb(f"yin{b}", [P, SEQ])[:, :] for b in range(NB)], [probs[1][:, b, :] for b in range(NB)]]

        ps_s = [pb(f"ps_s{i}") for i in range(3)]
        ps_a = [pb(f"ps_a{i}") for i in range(2)]
        ps_t = pb("ps_t")
        ps_n = pb("ps_n")
        ps_d = pb("ps_d")

        up_bank = [*ps_s, ps_t]
        down_bank = [ps_n, ps_d]
        vtmp = yin[0]

        ld_x = [sem(f"ld_x{b}") for b in range(NB)]
        ld_m = sem("ld_m")
        ld_c, ld_k, ld_aug = sem("ld_c"), sem("ld_k"), sem("ld_aug")
        ld_w = [sem(f"ld_w{l}") for l in range(LAYERS)]
        padded = [sem(f"padded{l}") for l in range(LAYERS)]
        s_aug, s_tanh, s_const, s_masked = sem("s_aug"), sem("s_tanh"), sem("s_const"), sem("s_masked")
        s_tgbo = sem("s_tgbo")
        ring_full, ring_used = sem("ring_full"), sem("ring_used")
        k_split, k_put, kspread, ks_ok, q_put = sem("k_split"), sem("k_put"), sem("kspread"), sem("ks_ok"), sem("q_put")
        pad_ok = sem("pad_ok")
        s_vb = sem("s_vb")
        var1, rstd1_ok, nrm_ok, nrmT_ok, nT_ok = sem("var1"), sem("rstd1_ok"), sem("nrm_ok"), sem("nrmT_ok"), sem("nT_ok")
        rot_ok, q_ok, qh_ok, ql_ok, qspread = sem("rot_ok"), sem("q_ok"), sem("qh_ok"), sem("ql_ok"), [sem(f"qspread{i}") for i in range(3)]
        augt_ok, augt_tr, augT_ok = sem("augt_ok"), sem("augt_tr"), sem("augT_ok")
        mask_tr, maskT_ok = sem("mask_tr"), sem("maskT_ok")
        sc_full, exp_ok, pv_ok, nd_ok = sem("sc_full"), sem("exp_ok"), sem("pv_ok"), sem("nd_ok")
        rdx_ok = sem("rdx_ok")
        den_tr, rd_ok, rd_tr, att_ok = sem("den_tr"), sem("rd_ok"), sem("rd_tr"), sem("att_ok")
        xb_ok = sem("xb_ok")
        var2, rstd2_ok, nrm2_ok, pay_tr, nT2_ok = sem("var2"), sem("rstd2_ok"), sem("nrm2_ok"), sem("pay_tr"), sem("nT2_ok")
        pay2_ok = sem("pay2_ok")
        sh_ok, ex_ok, ohs_ok, slot_ok, scattered = sem("sh_ok"), sem("ex_ok"), sem("ohs_ok"), sem("slot_ok"), sem("scattered")
        meta_ok = sem("meta_ok")
        s_dve, s_act, s_pool = sem("s_dve"), sem("s_act"), sem("s_pool")
        def per_layer(name):
            return [sem(f"{name}{l}") for l in range(LAYERS)]
        f_ld = [[sem(f"f_ld{l}_{i}") for i in range(SLOTS)] for l in range(LAYERS)]
        f_xtr, f_xT, f_up, f_hid, f_dn = map(per_layer, ("f_xtr", "f_xT", "f_up", "f_hid", "f_dn"))
        f_th, f_y, f_silu, f_turn = map(per_layer, ("f_th", "f_y", "f_silu", "f_turn"))
        f_put = [[sem(f"f_put{l}_{i}") for i in range(SHORT)] for l in range(LAYERS)]
        y_ld = [[sem(f"y_ld{l}_{b}") for b in range(NB)] for l in range(LAYERS)]
        x_ok, o_put = sem("x_ok"), sem("o_put")

        block = ctx.enter_context(nc.Block())

        def score_tile(s):
            return s // GROUPS, s % GROUPS

        class Count:
            def __init__(self, n=0):
                self.n = n

            def next(self):
                self.n += 1
                return self.n - 1

        def rounds(eng, l, body):
            body(0, True)
            with eng.Fori(1, FT[l] // SLOTS) as r:
                body(r, False)

        @block.sync
        def _(sp):
            sp.dma_start(x[:, 0:TPB, :], x_in[:, 0:TPB, :]).then_inc(ld_x[0], 16)
            sp.dma_start(w[0][:, :], w_in[0]).then_inc(ld_w[0], 16)
            sp.dma_start(cst[:, :], const_in).then_inc(ld_c, 16)
            sp.dma_start(gates[:, :], gates_in).then_inc(ld_c, 16)
            sp.dma_start(ids[:, :, :], ids_in).then_inc(ld_c, 16)
            sp.dma_start(maski[:, :, :], mask_in).then_inc(ld_m, 16)
            for b in range(1, NB):
                sp.dma_start(x[:, b * TPB:(b + 1) * TPB, :], x_in[:, b * TPB:(b + 1) * TPB, :]).then_inc(ld_x[b], 16)

            def spread_k(l):
                sp.wait_ge(k_split, l + 1)
                for c in range(4):
                    sp.dma_start(k_rows[l, :, c, :, :], khl[c // 2][:, :].bitcast(F32)).then_inc(k_put, 16)
                sp.wait_ge(k_put, 64 * (l + 1))
                if l:
                    sp.wait_ge(pv_ok, KT * NB * l)
                sp.dma_start(ksp.rearrange("p (g k) -> p g k", g=GROUPS), k_rows[l].rearrange("g c r k -> (c r) g k")).then_inc(kspread, 16)

            def spread_q(n):
                sp.wait_ge(qh_ok, n + 1)
                sp.dma_start(q_rows[n, :, 0, :, :], qhl[0][:, :].bitcast(F32)).then_inc(q_put, 16)
                sp.wait_ge(ql_ok, n + 1)
                sp.dma_start(q_rows[n, :, 1, :, :], qhl[1][:, :].bitcast(F32)).then_inc(q_put, 16)
                sp.wait_ge(q_put, 32 * (n + 1))
                if n >= 3:
                    sp.wait_ge(sc_full, NS * (n - 2))
                for c in range(2):
                    sp.dma_start(qs[n % 3][64 * c:64 * c + 64, :, :].bitcast(F32), q_rows[n].rearrange("g c r k -> (c r) g k")).then_inc(qspread[n % 3], 16)

            def load_tiles(l):
                sp.wait_ge(meta_ok, l + 1)

                def body(r, first):
                    for i in range(SLOTS):
                        j = r * SLOTS + i
                        at_w = sp.value_load(meta[l][0:1, 0, bass.ds(j, 1)], min_val=0, max_val=(E - 1) * P * FW[l])
                        at_x = sp.value_load(meta[l][0:1, 1, bass.ds(j, 1)], min_val=0, max_val=DUMMY * P * PAY)
                        if not first:
                            sp.wait_ge(f_y[l], (r - 1) * SLOTS + i + 1)
                            sp.sem_inc(f_turn[l], 1)
                        sp.dma_start(fw[i][:, 0:FW[l]], f_in[l].rearrange("e p f -> (e p f)")[bass.ds(at_w, P * FW[l])].rearrange("(p f) -> p f", p=P)).then_inc(f_ld[l][i], 16)
                        if first and i == 0:
                            sp.wait_ge(scattered, 16 * sum(CHOICES[:l + 1]) * NT)
                            sp.wait_ge(padded[l], 16 * (E + 1))
                        sp.dma_start(xt[i], routed[l].rearrange("k c -> (k c)")[bass.ds(at_x, P * PAY)].rearrange("(p c) -> p c", p=P)).then_inc(f_ld[l][i], 16)

                rounds(sp, l, body)

            def load_results(l):
                for i in range(SHORT):
                    sp.wait_ge(f_put[l][i], 16 * (FT[l] // SHORT))
                for b in range(NB):
                    for c in range(CHOICES[l]):
                        src = expert_out[l][c * TOKENS + b * SEQ:c * TOKENS + (b + 1) * SEQ, :].rearrange("(t p) d -> p t d", p=P)
                        if l and not c:
                            sp.wait_ge(x_ok, b + 1)
                        sp.dma_start(yin[c][b].rearrange("p (t c) -> p t c", c=D), src).then_inc(y_ld[l][b], 16)

            for l in range(LAYERS):
                if l == 0:
                    spread_k(0)
                    sp.dma_start(w[1][:, :], w_in[1]).then_inc(ld_w[1], 16)
                spread_q(NB * l)
                spread_q(NB * l + 1)
                spread_q(NB * l + 2)
                spread_q(NB * l + 3)
                if l == 0:
                    spread_k(1)
                load_tiles(l)
                load_results(l)
            for b in range(NB):
                sp.wait_ge(x_ok, NB + b + 1)
                sp.dma_start(out[:, b * TPB:(b + 1) * TPB, :], x[:, b * TPB:(b + 1) * TPB, :]).then_inc(o_put, 16)
            sp.wait_ge(o_put, 16 * NB)

        @block.gpsimd
        def _(pool):
            chain = Count()

            def link(ins):
                ins.then_inc(s_pool, 1)
                pool.wait_ge(s_pool, chain.next() + 1)

            nc.gpsimd.memset(half[:, :], -0.5)
            nc.gpsimd.memset(ones16[:, :], 1.0)
            for l in range(LAYERS):
                nc.gpsimd.memset(augt[l][:, :, :], 0.0)
                nc.gpsimd.memset(run[l][:, 0, :], 0.0)
            nc.gpsimd.memset(rows_at[0][:, :], 0).then_inc(s_const, 1)

            def power(var, ve_, rstd_, done, n):
                pool.wait_ge(var, n + 1)
                link(nc.gpsimd.tensor_scalar(ve_[:, :], (mv if var is var1 else mv2)[:, :, 1], EPS, None, ALU.add))
                nc.gpsimd.tensor_tensor(rstd_[:, :], ve_[:, :], half[:, :], ALU.pow).then_inc(done, 1)

            def add_q(n):
                pool.wait_ge(rot_ok, n + 1)
                if n:
                    pool.wait_ge(ql_ok, n)
                nc.gpsimd.tensor_tensor(qr1[:, :], qr1[:, :], qr2[:, :], ALU.add).then_inc(q_ok, 1)

            def add_bias(n):
                l, b = divmod(n, NB)
                pool.wait_ge(s_tgbo, l + 1)
                pool.wait_ge(nrm_ok, n + 1)
                xb = x[:, b * TPB:(b + 1) * TPB, :]
                nc.gpsimd.tensor_tensor(xb, xb, bcast(tgbo[l][:, :], 1, TPB), ALU.add).then_inc(xb_ok, 1)

            def scatter(n, i):
                l, b = divmod(n, NB)
                if i == 0:
                    pool.wait_ge(slot_ok, n + 1)
                for c in range(CHOICES[l]):
                    t = b * TPB + i
                    pool.indirect_dma_start(
                        out=routed[l], out_offset=bass.IndirectOffsetOnAxis(ap=slot[c][:, t:t + 1], axis=0),
                        in_=pay[c][:, t, :], in_offset=None).then_inc(scattered, 16)

            def second_copy(n):
                b = n % NB
                pool.wait_ge(nrm2_ok, n + 1)
                nc.gpsimd.tensor_copy(pay[1][:, b * TPB:(b + 1) * TPB, 0:D], pay[0][:, b * TPB:(b + 1) * TPB, 0:D]).then_inc(pay2_ok, 1)

            def put_tiles(l):
                last_row = pool.alloc_register(f"last_row{l}")
                pool.reg_mov(last_row, CHOICES[l] * TOKENS - 1)

                def body(r, first):
                    for i in range(SLOTS):
                        pool.wait_ge(f_y[l], r * SLOTS + i + 1)
                        pool.sem_inc(f_turn[l], 1)
                        pool.indirect_dma_start(
                            out=expert_out[l], out_offset=bass.IndirectOffsetOnAxis(ap=rows_at[i % SHORT][:, :], axis=0),
                            in_=yo[i % SHORT][:, :], in_offset=None, bounds_check=last_row, oob_is_err=False).then_inc(f_put[l][i % SHORT], 16)

                rounds(pool, l, body)

            for l in range(LAYERS):
                n0 = NB * l
                for k in STEPS:
                    for b in due("stats", k):
                        power(var1, ve, rstd, rstd1_ok, n0 + b)
                    for b in due("bias", k):
                        add_bias(n0 + b)
                    for b in due("project", k):
                        if l == 0:
                            add_q(n0 + b)
                    for b in due("stats2", k):
                        power(var2, ve2, rstd2, rstd2_ok, n0 + b)
                    for b in due("normalise2", k):
                        if l:
                            second_copy(n0 + b)
                    for i in range(TPB):
                        for b in due(f"scatter{i}", k):
                            scatter(n0 + b, i)
                put_tiles(l)

        @block.scalar
        def _(act):
            act.dma_start(cx4[:, :, :, :], ctx_in).then_inc(ld_k, 16)
            act.dma_start(pad[:, :], pad_in).then_inc(ld_c, 16)
            act.dma_start(augf, aug_in).then_inc(ld_aug, 16)
            act.wait_ge(ld_c, 64)
            nc.scalar.activation(tg[:, :], gates[:, :], ACT.Tanh).then_inc(s_tanh, 1)
            for l in range(LAYERS):
                act.dma_start(routed[l][DUMMY * P:(DUMMY + 1) * P, :], pad[:, :]).then_inc(padded[l], 16)
            act.wait_ge(ld_aug, 16)
            nc.scalar.activation(aug[:, :, :].rearrange("p g k -> p (g k)"), augf, ACT.Copy).then_inc(s_aug, 1)

            def copy_nT(n):
                act.wait_ge(nrmT_ok, n + 1)
                nc.scalar.activation(nT[:, :], ps_t[:, :], ACT.Copy).then_inc(nT_ok, 1)

            def high_q(n):
                act.wait_ge(q_ok, n + 1)
                if n:
                    act.wait_ge(q_put, 32 * n)
                nc.scalar.activation(qhl[0][:, :], qr1[:, :], ACT.Copy).then_inc(qh_ok, 1)

            def copy_augT(n):
                act.wait_ge(augt_tr, n + 1)
                if n >= 2:
                    act.wait_ge(sc_full, NS * (n - 1))
                nc.scalar.activation(augT[n % 2][:, :], ps_t[:, :], ACT.Copy).then_inc(augT_ok, 1)

            def exps(n, s):
                j, g = score_tile(s)
                act.wait_ge(sc_full, NS * n + s + 1)
                if n >= 2 and s == 0:
                    act.wait_ge(pv_ok, KT * (n - 1))
                nc.scalar.activation(probs[n % 2][0:KSIZE[j], s, :], ps_s[(NS * n + s) % 3][0:KSIZE[j], :], ACT.Exp, scale=SCALE).then_inc(exp_ok, 1)

            def copy_nd(n):
                act.wait_ge(pv_ok, KT * (n + 1))
                if n:
                    act.wait_ge(att_ok, n)
                nc.scalar.activation(dens[:, :], ps_d[:, :], ACT.Copy).then_inc(nd_ok, 1)
                nc.scalar.activation(nums[:, :], ps_n[:, :], ACT.Copy).then_inc(nd_ok, 1)

            def widen_rd(n):
                act.wait_ge(rd_ok, n + 1)
                if n:
                    act.wait_ge(rd_tr, n)
                nc.scalar.activation(rdx[:, :].rearrange("p (q d) -> p q d", d=HD),
                                     bcast(rd[:, :, :].rearrange("p t h -> p (t h)"), 2, HD), ACT.Copy).then_inc(rdx_ok, 1)

            def copy_nT2(n):
                act.wait_ge(pay_tr, n + 1)
                nc.scalar.activation(nT2[:, :], ps_t[:, :], ACT.Copy).then_inc(nT2_ok, 1)

            def route_exp(n):
                act.wait_ge(sh_ok, n + 1)
                if n < NB:
                    nc.scalar.activation(expd[:, :, :], shifted[:, :, :], ACT.Exp).then_inc(ex_ok, 1)
                else:
                    nc.scalar.activation(se[:, :], shifted[:, :, 0], ACT.Exp).then_inc(ex_ok, 1)

            def mask_keys(l):
                act.wait_ge(kspread, 16 * (l + 1))
                if l:
                    act.wait_ge(sc_full, NS * NB * l)
                for h in range(HPG // 2):
                    last = nc.scalar.activation(ks_by_head[:, :, h * KEYS:(h + 1) * KEYS], ksp.rearrange("p (q k) -> p q k", k=KEYS),
                                                ACT.Copy, scale=hm[:, h:h + 1])
                last.then_inc(ks_ok, 1)

            def pad_rows(l):
                act.wait_ge(pad_ok, l + 1)
                for e in range(E):
                    at = act.value_load(pad_at[l][0:1, e:e + 1], min_val=0, max_val=(DUMMY - 1) * P * PAY)
                    act.dma_start(routed[l].rearrange("k c -> (k c)")[bass.ds(at, P * PAY)].rearrange("(p c) -> p c", p=P), pad[:, :]).then_inc(padded[l], 16)

            def relu(l, i, count, first):
                act.wait_ge(f_up[l], count)
                if not first:
                    act.wait_ge(f_dn[l], count - SHORT)
                for c in range(HC):
                    last = nc.scalar.activation(hid[i % SHORT][:, c, :], up_bank[i % SHORT][:, c * P:(c + 1) * P], ACT.Relu,
                                                bias=fw[i][:, FW[0] - HC + c:FW[0] - HC + c + 1])
                last.then_inc(f_hid[l], 1)

            def tanh(l, i, count, first):
                act.wait_ge(f_up[l], count)
                if not first:
                    act.wait_ge(f_silu[l], count - 2)
                nc.scalar.activation(tanhs[i % 2], up_bank[i % SHORT][:, 0:HID], ACT.Tanh, scale=0.5).then_inc(f_th[l], 1)

            def tiles_act(l):
                def body(r, first):
                    for i in range(SLOTS):
                        j = r * SLOTS + i
                        if l:
                            act.wait_ge(f_xtr[l], j + 1)
                            if not (first and i < SHORT):
                                act.wait_ge(f_up[l], j + 1 - SHORT)
                            nc.scalar.activation(xT[i % SHORT][:, :], ps_a[i % 2][:, 0:P], ACT.Copy).then_inc(f_xT[l], 1)
                        if not (first and i < LAG_UP):
                            if l:
                                tanh(l, (i - LAG_UP) % SLOTS, j, first and i < LAG_UP + 2)
                            else:
                                relu(l, (i - LAG_UP) % SLOTS, j, first and i < LAG_UP + SHORT)

                rounds(act, l, body)
                (tanh if l else relu)(l, SLOTS - 1, FT[l], False)

            for l in range(LAYERS):
                n0 = NB * l
                for k in STEPS:
                    if 0 <= k < NB * NS:
                        exps(n0 + k // NS, k % NS)
                    if l == 0 and k == MASK_AT:
                        act.wait_ge(mask_tr, 1)
                        nc.scalar.activation(maskT[:, :], ps_t[:, :], ACT.Copy).then_inc(maskT_ok, 1)
                    for b in due("turn", k):
                        copy_nT(n0 + b)
                    for b in due("high", k):
                        high_q(n0 + b)
                    for b in due("augment", k):
                        copy_augT(n0 + b)
                    for b in due("sums", k):
                        copy_nd(n0 + b)
                    for b in due("widen", k):
                        widen_rd(n0 + b)
                    for b in due("turn2", k):
                        copy_nT2(n0 + b)
                    for b in due("route_exp", k):
                        route_exp(n0 + b)
                    for kl in range(LAYERS):
                        if l == 0 and k == BLOCKS_AT[kl]:
                            mask_keys(kl)
                pad_rows(l)
                tiles_act(l)

        @block.tensor
        def _(pe):
            unit = Count()
            reader = []

            def ring():
                u = unit.next()
                if u >= 2:
                    pe.wait_ge(ring_used, u - 1)
                return ps_a[u % 2]

            def keys(l):
                pe.wait_ge(ld_w[l], 16)
                pe.wait_ge(ld_k, 16)
                for c in ((W_K,) if l else (W_K, W_KR)):
                    nc.tensor.matmul(ring()[:, 0:NB * KEYS], w[l][:, c:c + D], cx4[:, :, 0, :], start=True, stop=True).then_inc(ring_full, 1)

            def values(l, j):
                bank = ring()
                for b in range(NB):
                    src = cx4[:, b, :, :].rearrange("p h k -> p (h k)")[:, KROWS * j:KROWS * j + KSIZE[j]]
                    last = nc.tensor.matmul(bank[0:KSIZE[j], b * D:(b + 1) * D], src, w[l][:, W_V:W_V + D], start=True, stop=True)
                last.then_inc(ring_full, 1)

            def transposes(src, done, read, value):
                if reader:
                    pe.wait_ge(*reader[-1])
                reader.append((read, value))
                for i in range(TPB):
                    last = nc.tensor.transpose(ps_t[:, i * P:(i + 1) * P], src(i), ident)
                last.then_inc(done, 1)

            def project(n):
                pe.wait_ge(nT_ok, n + 1)
                for c in ((W_Q, W_QR) if n < NB else (W_Q,)):
                    nc.tensor.matmul(ring()[:, :], w[n // NB][:, c:c + D], nT[:, :], start=True, stop=True).then_inc(ring_full, 1)

            def front(n):
                pe.wait_ge(nrm_ok, n + 1)
                transposes(lambda i: nrm[:, i, :], nrmT_ok, nT_ok, n + 1)

            def scores_for_max(n, u):
                l, b = divmod(n, NB)
                i, g = divmod(u, GROUPS)
                if u == 0:
                    pe.wait_ge(qspread[n % 3], 32 * (n // 3 + 1))
                    if b == 0:
                        pe.wait_ge(ks_ok, 2 * (l + 1))
                bank = ring()
                if l:
                    if n == NB and u == 0:
                        pe.wait_ge(maskT_ok, 1)
                    nc.tensor.matmul(bank[:, 0:GK], maskT[:, i * P:(i + 1) * P], aug[:, g, :], start=True, stop=False)
                nc.tensor.matmul(bank[:, 0:GK], qs[n % 3][:, g, i * P:(i + 1) * P], ks[:, g, b, :], start=not l, stop=True).then_inc(ring_full, 1)

            def augmenting(n):
                pe.wait_ge(augt_ok, n + 1)
                transposes(lambda i: augt[n // NB][:, i, :], augt_tr, augT_ok, n + 1)

            def scores(n, s):
                l, b = divmod(n, NB)
                j, g = score_tile(s)
                k = NS * n + s
                if s == 0:
                    pe.wait_ge(augT_ok, n + 1)
                    if n == 0:
                        pe.wait_ge(s_aug, 1)
                if k >= 3:
                    pe.wait_ge(exp_ok, k - 2)
                bank = ps_s[k % 3][0:KSIZE[j], :]
                lo, hi = KROWS * j, KROWS * j + KSIZE[j]
                nc.tensor.matmul(bank, ks[:, g, b, lo:hi], qs[n % 3][:, g, :], start=True, stop=False)
                nc.tensor.matmul(bank, aug[:, g, lo:hi], augT[n % 2][:, :], start=False, stop=True).then_inc(sc_full, 1)

            def weigh(n, j):
                l, b = divmod(n, NB)
                pe.wait_ge(exp_ok, NS * n + GROUPS * (j + 1))
                if j == 0:
                    if b == 0:
                        pe.wait_ge(s_vb, KT * (l + 1))
                    if n:
                        pe.wait_ge(nd_ok, 2 * n)
                kk = KSIZE[j]
                for bank, lhs in ((ps_n, lambda g: vb[0:kk, j, b, 32 * g:32 * g + 32]), (ps_d, lambda g: hmv[0:kk, j, :])):
                    for g in range(GROUPS):
                        last = nc.tensor.matmul(bank[32 * g:32 * g + 32, :], lhs(g), probs[n % 2][0:kk, j * GROUPS + g, :],
                                                start=j == 0, stop=j == KT - 1)
                last.then_inc(pv_ok, 1)

            def den_to_tokens(n):
                pe.wait_ge(nd_ok, 2 * n + 1)
                transposes(lambda i: dens[:, i * P:(i + 1) * P], den_tr, rd_ok, n + 1)

            def rden_to_dims(n):
                pe.wait_ge(rdx_ok, n + 1)
                transposes(lambda i: rdx[:, i * P:(i + 1) * P], rd_tr, att_ok, n + 1)

            def output(n):
                pe.wait_ge(att_ok, n + 1)
                bank = ring()
                for i in range(TPB):
                    last = nc.tensor.matmul(bank[:, i * D:(i + 1) * D], att[:, i * P:(i + 1) * P], w[n // NB][:, W_O:W_O + D], start=True, stop=True)
                last.then_inc(ring_full, 1)

            def routed_T(n):
                pe.wait_ge(nrm2_ok, n + 1)
                transposes(lambda i: pay[0][:, (n % NB) * TPB + i, 0:D], pay_tr, nT2_ok, n + 1)

            def router(n):
                pe.wait_ge(nT2_ok, n + 1)
                bank = ring()
                for i in range(TPB):
                    last = nc.tensor.matmul(bank[:, i * E:(i + 1) * E], nT2[:, i * P:(i + 1) * P], w[n // NB][:, W_R:W_R + E], start=True, stop=True)
                last.then_inc(ring_full, 1)

            def ranks(n):
                l, b = divmod(n, NB)
                pe.wait_ge(ohs_ok, n + 1)
                if n == 0:
                    pe.wait_ge(s_const, 1)
                bank = ring()
                nc.tensor.matmul(bank[:, 0:TPB * E], prefix16[:, :], ohs[:, :, :].rearrange("p t e -> p (t e)"), start=True, stop=False)
                nc.tensor.matmul(bank[:, 0:TPB * E], ones16[:, :], run[l][:, b * TPB:(b + 1) * TPB, :].rearrange("p t e -> p (t e)"),
                                 start=False, stop=True).then_inc(ring_full, 1)

            def totals(l):
                nc.tensor.matmul(ring()[:, 0:E], ones16[:, :], run[l][:, NT, :], start=True, stop=True).then_inc(ring_full, 1)

            def tiles_pe(l):
                chunks = 2 * HC if l else HC
                dn0 = chunks * P

                def up(i, count):
                    pe.wait_ge(f_xT[l], count)
                    for c in range(chunks):
                        last = nc.tensor.matmul(up_bank[i % SHORT][:, c * P:(c + 1) * P], fw[i][:, c * P:(c + 1) * P], xT[i % SHORT][:, :], start=True, stop=True)
                    last.then_inc(f_up[l], 1)

                def down(i, count, first):
                    pe.wait_ge(f_hid[l], count)
                    if not first:
                        pe.wait_ge(f_y[l], count - 2)
                    for c in range(HC):
                        last = nc.tensor.matmul(down_bank[i % 2][:, 0:D], hid[i % SHORT][:, c, :], fw[i][:, dn0 + c * D:dn0 + (c + 1) * D], start=c == 0, stop=c == HC - 1)
                    last.then_inc(f_dn[l], 1)

                def body(r, first):
                    for i in range(SLOTS):
                        j = r * SLOTS + i
                        pe.wait_ge(f_ld[l][i], 32 * (r + 1))
                        if not (first and i < 2):
                            pe.wait_ge(f_xT[l], j - 1)
                        nc.tensor.transpose(ps_a[i % 2][:, 0:P], xt[i][:, 0:D], ident).then_inc(f_xtr[l], 1)
                        if not (first and i < LAG_UP):
                            up((i - LAG_UP) % SLOTS, j + 1 - LAG_UP)
                        if not (first and i < LAG_DOWN):
                            down((i - LAG_DOWN) % SLOTS, j + 1 - LAG_DOWN, first and i < LAG_DOWN + 2)

                rounds(pe, l, body)
                up(SLOTS - 1, FT[l])
                for i in range(SLOTS - LAG_DOWN, SLOTS):
                    down(i, FT[l] - SLOTS + i + 1, False)

            pe.wait_ge(ld_c, 64)
            for l in range(LAYERS):
                n0 = NB * l
                for k in STEPS:
                    if 0 <= k < NB * NS:
                        scores(n0 + k // NS, k % NS)
                    for b in due("router", k):
                        router(n0 + b)
                    for b in due("ranks", k):
                        ranks(n0 + b)
                    for b in due("project", k):
                        project(n0 + b)
                    for b in due("output", k):
                        output(n0 + b)
                    for b, u in max_units(k):
                        scores_for_max(n0 + b, u)
                    for kl in range(LAYERS):
                        if l == 0 and k == KEYS_AT[kl]:
                            keys(kl)
                        for j in range(KT):
                            if l == 0 and k == VALUES_AT[kl][j]:
                                values(kl, j)
                    if l == 0 and k == MASK_AT:
                        pe.wait_ge(s_masked, 1)
                        transposes(lambda i: augt[1][:, i, :], mask_tr, maskT_ok, 1)
                    for b in due("turn", k):
                        front(n0 + b)
                    for b in due("augment", k):
                        augmenting(n0 + b)
                    for b in due("den", k):
                        den_to_tokens(n0 + b)
                    for b in due("rden", k):
                        rden_to_dims(n0 + b)
                    for b in due("turn2", k):
                        routed_T(n0 + b)
                    for j in range(KT):
                        for b in due(f"weigh{j}", k):
                            weigh(n0 + b, j)
                totals(l)
                tiles_pe(l)

        @block.vector
        def _(dve):
            unit, chain = Count(), Count()

            def link(ins):
                ins.then_inc(s_dve, 1)
                dve.wait_ge(s_dve, chain.next() + 1)

            def ring():
                u = unit.next()
                dve.wait_ge(ring_full, u + 1)
                return ps_a[u % 2]

            def keys(l):
                wl = w[l]
                shape = "p (b k) -> p b k"
                a = ring()[:, 0:NB * KEYS]
                if l == 0:
                    nc.vector.tensor_tensor(kr1[:, :].rearrange(shape, b=NB), a.rearrange(shape, b=NB), bcast(cos[:, 0:KEYS], 1, NB),
                                            ALU.mult).then_inc(ring_used, 1)
                    a = ring()[:, 0:NB * KEYS]
                    nc.vector.tensor_tensor(kr2[:, :].rearrange(shape, b=NB), a.rearrange(shape, b=NB), bcast(sin[:, 0:KEYS], 1, NB),
                                            ALU.mult).then_inc(ring_used, 1)
                    dve.wait_ge(ring_used, unit.n)
                    link(nc.vector.tensor_tensor(kr1[:, :], kr1[:, :], kr2[:, :], ALU.add))
                else:
                    nc.vector.tensor_scalar(kr1[:, :], a, wl[:, W_BK:W_BK + 1], None, ALU.add).then_inc(ring_used, 1)
                    dve.wait_ge(ring_used, unit.n)
                if l:
                    dve.wait_ge(k_put, 64 * l)
                link(nc.vector.tensor_copy(khl[0][:, :], kr1[:, :]))
                link(nc.vector.tensor_tensor(khl[1][:, :], kr1[:, :], khl[0][:, :].bitcast(F32), ALU.subtract))
                dve.sem_inc(k_split, 1)
                nc.vector.tensor_scalar(tgbo[l][:, :], wl[:, W_BO:W_BO + D], tg[:, 2 * l:2 * l + 1], None, ALU.mult).then_inc(s_tgbo, 1)

            def values(l, j):
                kk = KSIZE[j]
                a = ring()
                if l:
                    dve.wait_ge(pv_ok, KT * NB * l)
                dst = vb[0:kk, j, :, :].rearrange("p b (g c) -> p (b g) c", g=GROUPS)
                link(nc.vector.tensor_tensor(vtmp[j][0:kk, :].rearrange("p (b c) -> p b c", b=NB), a[0:kk, :].rearrange("p (b c) -> p b c", b=NB),
                                             bcast(w[l][0:kk, W_BV:W_BV + D], 1, NB), ALU.add))
                dve.sem_inc(ring_used, 1)
                nc.vector.tensor_tensor(dst, vtmp[j][0:kk, :].rearrange("p (q c) -> p q c", c=32), bcast(hmv[0:kk, j, :], 1, NB * GROUPS), ALU.mult).then_inc(s_vb, 1)

            def mask_keys(l):
                dve.wait_ge(kspread, 16 * (l + 1))
                if l:
                    dve.wait_ge(sc_full, NS * NB * l)
                for h in range(HPG // 2, HPG):
                    last = nc.vector.tensor_scalar(ks_by_head[:, :, h * KEYS:(h + 1) * KEYS], ksp.rearrange("p (q k) -> p q k", k=KEYS),
                                                   hm[:, h:h + 1], None, ALU.mult)
                last.then_inc(ks_ok, 1)

            def statistics(src, st_, mv_, done):
                for i in range(TPB):
                    last = nc.vector.bn_stats(st_[:, i, :], src[:, i, :])
                link(last)
                for i in range(TPB):
                    last = nc.vector.bn_aggr(mv_[:, i, :], st_[:, i, :])
                last.then_inc(done, 1)

            def normalise(src, dst, mv_, rstd_, done):
                for i in range(TPB):
                    last = nc.vector.tensor_scalar(dst(i), src[:, i, :], mv_[:, i, 0:1], rstd_[:, i:i + 1], ALU.subtract, ALU.mult)
                last.then_inc(done, 1)

            def xs(n):
                b = n % NB
                return x[:, b * TPB:(b + 1) * TPB, :]

            def front_stats(n):
                if n < NB:
                    dve.wait_ge(ld_x[n], 16)
                if n:
                    dve.wait_ge(rstd1_ok, n)
                statistics(xs(n), st, mv, var1)

            def front_normalise(n):
                dve.wait_ge(rstd1_ok, n + 1)
                dve.wait_ge(var1, n + 1)
                if n:
                    dve.wait_ge(nrmT_ok, n)
                normalise(xs(n), lambda i: nrm[:, i, :], mv, rstd, nrm_ok)

            def rotate(n):
                wl = w[n // NB]
                if n:
                    dve.wait_ge(ql_ok, n)
                a = ring()
                if n < NB:
                    nc.vector.tensor_tensor(qr1[:, :], a[:, :], cos, ALU.mult).then_inc(ring_used, 1)
                    a = ring()
                    nc.vector.tensor_tensor(qr2[:, :], a[:, :], sin, ALU.mult).then_inc(ring_used, 1)
                    dve.wait_ge(ring_used, unit.n)
                    dve.sem_inc(rot_ok, 1)
                else:
                    nc.vector.tensor_scalar(qr1[:, :], a[:, :], wl[:, W_BQ:W_BQ + 1], None, ALU.add).then_inc(ring_used, 1)
                    dve.wait_ge(ring_used, unit.n)
                    dve.sem_inc(q_ok, 1)

            def low_q(n):
                dve.wait_ge(qh_ok, n + 1)
                dve.wait_ge(q_ok, n + 1)
                if n:
                    dve.wait_ge(q_put, 32 * n)
                nc.vector.tensor_tensor(qhl[1][:, :], qr1[:, :], qhl[0][:, :].bitcast(F32), ALU.subtract).then_inc(ql_ok, 1)

            def maxima(n, u):
                i, g = divmod(u, GROUPS)
                a = ring()
                nc.vector.tensor_reduce(negm[:, i, g * HPG:(g + 1) * HPG], a[:, 0:GK].rearrange("p (h k) -> p h k", h=HPG),
                                        AX.X, ALU.max, negate=True).then_inc(ring_used, 1)

            def split_max(n):
                l = n // NB
                at = augt[l]
                dve.wait_ge(ring_used, unit.n)
                if n == 0:
                    dve.wait_ge(s_const, 1)
                if n % NB:
                    dve.wait_ge(augt_tr, n)
                if l:
                    link(nc.vector.tensor_scalar(negm[:, :, :], negm[:, :, :], CLAMP, None, ALU.min))
                link(nc.vector.tensor_copy(negmh[:, :, :], negm[:, :, :]))
                nc.vector.tensor_copy(at[:, :, 0:HEADS], negmh[:, :, :].bitcast(F32))
                nc.vector.tensor_tensor(at[:, :, HEADS:2 * HEADS], negm[:, :, :], negmh[:, :, :].bitcast(F32), ALU.subtract).then_inc(augt_ok, 1)

            def recip_den(n):
                dve.wait_ge(den_tr, n + 1)
                if n:
                    dve.wait_ge(rdx_ok, n)
                link(nc.vector.tensor_scalar(rd[:, :, :], ps_t[:, :].rearrange("p (t h d) -> p t h d", t=TPB, d=HD)[:, :, :, 0], 1e-30, None, ALU.max))
                nc.vector.reciprocal(rd[:, :, :], rd[:, :, :]).then_inc(rd_ok, 1)

            def weigh_out(n):
                dve.wait_ge(rd_tr, n + 1)
                dve.wait_ge(nd_ok, 2 * n + 2)
                nc.vector.tensor_tensor(att[:, :], ps_t[:, :], nums[:, :], ALU.mult).then_inc(att_ok, 1)

            def residual(n):
                l = n // NB
                a = ring()
                dve.wait_ge(xb_ok, n + 1)
                nc.vector.scalar_tensor_tensor(xs(n).rearrange("p t c -> p (t c)"), a[:, :], tg[:, 2 * l:2 * l + 1],
                                               xs(n).rearrange("p t c -> p (t c)"), ALU.mult, ALU.add).then_inc(ring_used, 1)
                dve.wait_ge(ring_used, unit.n)

            def normalise2(n):
                dve.wait_ge(rstd2_ok, n + 1)
                dve.wait_ge(var2, n + 1)
                b = n % NB
                normalise(xs(n), lambda i: pay[0][:, b * TPB + i, 0:D], mv2, rstd2, nrm2_ok)

            def best(src, m, one_hot):
                link(nc.vector.tensor_reduce(m[:, :], src[:, :, :], AX.X, ALU.max))
                link(nc.vector.tensor_tensor(wt[:, :, :], src[:, :, :], bcast(m[:, :], 2, E), ALU.is_equal))
                link(nc.vector.tensor_tensor(wt[:, :, :], wt[:, :, :], bcast(desc, 1, TPB), ALU.mult))
                link(nc.vector.tensor_reduce(wm[:, :], wt[:, :, :], AX.X, ALU.max))
                link(nc.vector.tensor_tensor(one_hot[:, :, :], wt[:, :, :], bcast(wm[:, :], 2, E), ALU.is_equal))

            def choose(n):
                l, b = divmod(n, NB)
                a = ring()
                link(nc.vector.tensor_tensor(lg[:, :, :], a[:, 0:TPB * E].rearrange("p (t e) -> p t e", t=TPB),
                                             bcast(w[l][:, W_BR:W_BR + E], 1, TPB), ALU.add))
                dve.sem_inc(ring_used, 1)
                best(lg, mx[0], oh[0])
                if l == 0:
                    nc.vector.tensor_tensor(shifted[:, :, :], lg[:, :, :], bcast(mx[0][:, :], 2, E), ALU.subtract).then_inc(sh_ok, 1)
                    nc.vector.tensor_copy(ohs[:, :, :], oh[0][:, :, :])
                    src = oh[0]
                else:
                    link(nc.vector.scalar_tensor_tensor(lg2[:, :, :], oh[0][:, :, :], MASKED, lg[:, :, :], ALU.mult, ALU.add))
                    best(lg2, mx[1], oh[1])
                    nc.vector.tensor_tensor(shifted[:, :, 0], mx[1][:, :], mx[0][:, :], ALU.subtract).then_inc(sh_ok, 1)
                    link(nc.vector.tensor_tensor(ohs[:, :, :], oh[0][:, :, :], oh[1][:, :, :], ALU.add))
                    src = ohs
                for i in range(TPB):
                    t = b * TPB + i
                    link(nc.vector.tensor_tensor(run[l][:, t + 1, :], run[l][:, t, :], src[:, i, :], ALU.add))
                dve.sem_inc(ohs_ok, 1)

            def gate(n):
                l, b = divmod(n, NB)
                t0 = b * TPB
                dve.wait_ge(ex_ok, n + 1)
                scale = tg[:, 2 * l + 1:2 * l + 2]
                gcol = [pay[c][:, t0:t0 + TPB, D + 1] for c in range(2)]
                if l == 0:
                    link(nc.vector.tensor_reduce(se[:, :], expd[:, :, :], AX.X, ALU.add))
                    link(nc.vector.reciprocal(re[:, :], se[:, :]))
                    nc.vector.tensor_scalar(gcol[0], re[:, :], scale, None, ALU.mult)
                else:
                    link(nc.vector.tensor_scalar(re[:, :], se[:, :], 1.0, None, ALU.add))
                    link(nc.vector.reciprocal(wm[:, :], re[:, :]))
                    link(nc.vector.tensor_scalar(gcol[0], wm[:, :], scale, 0.5, ALU.mult, ALU.mult))
                    nc.vector.tensor_tensor(gcol[1], gcol[0], se[:, :], ALU.mult)
                for c in range(CHOICES[l]):
                    nc.vector.tensor_copy(pay[c][:, t0:t0 + TPB, D].bitcast(I32), ids[:, c, t0:t0 + TPB])

            def slots(n):
                l, b = divmod(n, NB)
                a = ring()
                link(nc.vector.tensor_tensor(rk[:, :, :], a[:, 0:TPB * E].rearrange("p (t e) -> p t e", t=TPB), bcast(ebase, 1, TPB), ALU.add))
                dve.sem_inc(ring_used, 1)
                if l:
                    dve.wait_ge(pay2_ok, n - NB + 1)
                for c in range(CHOICES[l]):
                    link(nc.vector.tensor_tensor(wt[:, :, :], rk[:, :, :], oh[c][:, :, :], ALU.mult))
                    link(nc.vector.tensor_reduce(slotf[:, :], wt[:, :, :], AX.X, ALU.add))
                    last = nc.vector.tensor_copy(slot[c][:, b * TPB:(b + 1) * TPB], slotf[:, :])
                    if c < CHOICES[l] - 1:
                        link(last)
                last.then_inc(slot_ok, 1)

            def plan(l):
                nt = FT[l]
                a = ring()
                link(nc.vector.tensor_tensor(pad_row[:, :], a[0:1, 0:E], ebase[0:1, :], ALU.add))
                nc.vector.tensor_scalar(pad_at[l][:, :], pad_row[:, :], float(PAY), None, ALU.mult).then_inc(pad_ok, 1)
                link(nc.vector.tensor_tensor(gt[:, :, :], bcast(a[:, 0:E], 2, NT), bcast(cst[:, C_K128:C_K128 + NT], 1, E), ALU.is_gt))
                dve.sem_inc(ring_used, 1)
                link(nc.vector.tensor_reduce(tiles[:, :], gt[:, :, :], AX.X, ALU.add))
                link(nc.vector.tensor_tensor(cumx[:, :, :], bcast(tiles[:, :], 1, E), cst[:, C_LT:C_LT + E * E].rearrange("p (e f) -> p e f", e=E), ALU.mult))
                link(nc.vector.tensor_reduce(cum[:, :], cumx[:, :, :], AX.X, ALU.add))
                jj = cst[:, C_J:C_J + nt]
                link(nc.vector.tensor_tensor(le[:, 0:nt, :], bcast(cum[:, :], 1, nt), bcast(jj, 2, E), ALU.is_le))
                nc.vector.tensor_tensor(let[:, 0:nt, :], le[:, 0:nt, :], bcast(tiles[:, :], 1, nt), ALU.mult)
                link(nc.vector.tensor_reduce(ej[:, 0:nt], le[:, 0:nt, :], AX.X, ALU.add))
                link(nc.vector.tensor_reduce(kj[:, 0:nt], let[:, 0:nt, :], AX.X, ALU.add))
                link(nc.vector.tensor_tensor(kj[:, 0:nt], jj, kj[:, 0:nt], ALU.subtract))
                link(nc.vector.scalar_tensor_tensor(bj[:, 0:nt], ej[:, 0:nt], float(BLOCKS), kj[:, 0:nt], ALU.mult, ALU.add))
                nc.vector.tensor_scalar(meta[l][0:1, 0, :], ej[0:1, 0:nt], float(E - 1), float(P * FW[l]), ALU.min, ALU.mult)
                nc.vector.tensor_scalar(meta[l][0:1, 1, :], bj[0:1, 0:nt], float(DUMMY), float(P * PAY), ALU.min, ALU.mult).then_inc(meta_ok, 1)

            def tiles_dve(l):
                def hidden(i, count, first):
                    dve.wait_ge(f_th[l], count)
                    bank = up_bank[i % SHORT]
                    nc.vector.scalar_tensor_tensor(silu[i % 2], tanhs[i % 2], 1.0, bank[:, 0:HID], ALU.add, ALU.mult).then_inc(f_silu[l], 1)
                    dve.wait_ge(f_silu[l], count)
                    if not first:
                        dve.wait_ge(f_dn[l], count - SHORT)
                    nc.vector.tensor_tensor(hid[i % SHORT].rearrange("p c t -> p (c t)"), silu[i % 2], bank[:, HID:2 * HID], ALU.mult).then_inc(f_hid[l], 1)

                def finish(i, count, put):
                    dve.wait_ge(f_dn[l], count)
                    if put is not None:
                        dve.wait_ge(f_put[l][i % SHORT], put)
                    src = down_bank[i % 2][:, 0:D]
                    nc.vector.tensor_copy(rows_at[i % SHORT][:, :], xt[i][:, D:D + 1].bitcast(I32))
                    if l == 0:
                        nc.vector.tensor_tensor(yb[i % SHORT], src, fw[i][:, 2 * HID:2 * HID + D], ALU.add).then_inc(f_th[l], 1)
                        dve.wait_ge(f_th[l], count)
                        src = yb[i % SHORT]
                    nc.vector.tensor_scalar(yo[i % SHORT][:, :], src, xt[i][:, D + 1:D + 2], None, ALU.mult).then_inc(f_y[l], 1)

                per = SLOTS // SHORT

                def body(r, first):
                    for i in range(SLOTS):
                        j = r * SLOTS + i
                        if l == 0:
                            dve.wait_ge(f_xtr[l], j + 1)
                            if not (first and i < SHORT):
                                dve.wait_ge(f_up[l], j + 1 - SHORT)
                            nc.vector.tensor_copy(xT[i % SHORT][:, :], ps_a[i % 2][:, 0:P]).then_inc(f_xT[l], 1)
                        elif not (first and i < LAG_UP):
                            hidden((i - LAG_UP) % SLOTS, j, first and i < LAG_UP + SHORT)
                        if not (first and i < LAG_OUT):
                            finish((i - LAG_OUT) % SLOTS, j + 1 - LAG_OUT, None if first else 16 * (r * per + i // SHORT - 1))

                rounds(dve, l, body)
                if l:
                    hidden(SLOTS - 1, FT[l], False)
                for i in range(SLOTS - LAG_OUT, SLOTS):
                    finish(i, FT[l] - SLOTS + i + 1, 16 * (FT[l] // SHORT - 1))

            def add_results(l, b):
                dve.wait_ge(y_ld[l][b], 16 * CHOICES[l])
                dst = xs(b).rearrange("p t c -> p (t c)")
                for c in range(CHOICES[l]):
                    last = nc.vector.tensor_tensor(dst, dst, yin[c][b], ALU.add)
                    if c < CHOICES[l] - 1:
                        link(last)
                last.then_inc(x_ok, 1)

            dve.wait_ge(ld_c, 64)
            nc.vector.tensor_copy(prefix16[:, :], cst[:, C_U:C_U + P])
            dve.wait_ge(ld_m, 16)
            dve.wait_ge(s_const, 1)
            nc.vector.tensor_scalar(augt[1][:, :, AUG_KEY:AUG_KEY + KEYS], maski[:, :, :], 0.0, MASKED, ALU.is_equal, ALU.mult).then_inc(s_masked, 1)
            dve.wait_ge(s_tanh, 1)
            dve.wait_ge(ld_w[0], 16)
            for l in range(LAYERS):
                n0 = NB * l
                for k in STEPS:
                    for b in due("router", k):
                        choose(n0 + b)
                    for b in due("ranks", k):
                        gate(n0 + b)
                        slots(n0 + b)
                    for b in due("project", k):
                        rotate(n0 + b)
                    for b in due("low", k):
                        low_q(n0 + b)
                    for b in due("output", k):
                        residual(n0 + b)
                    for b, u in max_units(k):
                        maxima(n0 + b, u)
                    for kl in range(LAYERS):
                        if l == 0 and k == KEYS_AT[kl]:
                            dve.wait_ge(ld_w[kl], 16)
                            keys(kl)
                        for j in range(KT):
                            if l == 0 and k == VALUES_AT[kl][j]:
                                values(kl, j)
                        if l == 0 and k == BLOCKS_AT[kl]:
                            mask_keys(kl)
                    for b in due("split", k):
                        split_max(n0 + b)
                    for b in due("den", k):
                        recip_den(n0 + b)
                    for b in due("rden", k):
                        weigh_out(n0 + b)
                    for b in due("stats2", k):
                        statistics(xs(n0 + b), st2, mv2, var2)
                    for b in due("results", k):
                        if l:
                            add_results(0, b)
                            dve.wait_ge(x_ok, b + 1)
                    for b in due("stats", k):
                        front_stats(n0 + b)
                    for b in due("normalise", k):
                        front_normalise(n0 + b)
                    for b in due("normalise2", k):
                        normalise2(n0 + b)
                plan(l)
                tiles_dve(l)
            for b in range(NB):
                add_results(1, b)


def _constants():
    import numpy as np

    c = np.zeros((P, C_END), np.float32)
    c[:, C_ID:C_ID + P] = np.eye(P)
    inv = (1.0 / np.float32(10000.0) ** (np.arange(0, HD, 2, dtype=np.float32) / np.float32(HD))).astype(np.float32)
    ang = (np.arange(SEQ, dtype=np.float32)[:, None] * inv[None, :]).astype(np.float32)
    for p in range(P):
        d = p % HD
        c[p, C_COS:C_COS + SEQ] = np.cos(ang[:, d % (HD // 2)])
        c[p, C_SIN:C_SIN + SEQ] = np.sin(ang[:, d % (HD // 2)]) * (-1 if d < HD // 2 else 1)
        c[p, C_HM + (p // HD) % HPG] = 1
    aug = np.zeros((P, GROUPS, GK), np.float32)
    for j in range(KT):
        for r in range(KSIZE[j]):
            h = (KROWS * j + r) // KEYS
            c[r, C_HMV + 32 * j + HD * h:C_HMV + 32 * j + HD * (h + 1)] = 1
    for g in range(GROUPS):
        for f in range(GK):
            h, k = divmod(f, KEYS)
            aug[g * HPG + h, g, f] = aug[HEADS + g * HPG + h, g, f] = 1
            aug[AUG_KEY + k, g, f] = 1
    c[:, C_U:C_U + P] = np.triu(np.ones((P, P)), 1)
    c[:, C_DESC:C_DESC + E] = E - np.arange(E)
    c[:, C_EB:C_EB + E] = REGION * np.arange(E)
    c[:, C_K128:C_K128 + NT] = P * np.arange(NT)
    c[:, C_LT:C_LT + E * E] = np.tril(np.ones((E, E))).reshape(-1)
    c[:, C_J:C_END] = np.arange(max(FT))
    token = np.arange(P)[:, None] + P * np.arange(NT)[None, :]
    ids = np.stack([token, token + TOKENS], 1).astype(np.int32)
    pad = np.zeros((P, PAY), np.float32)
    pad[:, D] = np.full(P, NOROW, np.int32).view(np.float32)
    return c, aug.reshape(P, -1), ids, pad


def kernel(**a):
    import numpy as np
    import concourse.bacc as bacc
    from concourse.bass_utils import run_bass_kernel_spmd

    a = {k: np.asarray(v) for k, v in a.items()}
    half_turned = np.arange(D).reshape(HEADS, 2, HD // 2)[:, ::-1].reshape(-1)
    rows = lambda v: np.broadcast_to(v[None, :], (P, v.shape[0]))
    col = lambda v: v[:, None]
    zero = np.zeros(D, np.float32)

    def attention(wq, wk, wv, wo, bq, bk, bv, bo, wr, br):
        return np.ascontiguousarray(np.concatenate(
            [wq, wq[:, half_turned], wk, wk[:, half_turned], wv, wo, rows(bv), rows(bo), wr, rows(br),
             col(bq), col(bk)], 1))

    wkv = a["L0_xattn_Wkv"]
    w0 = attention(a["L0_xattn_Wq"], wkv[:, :D], wkv[:, D:], a["L0_xattn_Wo"], zero, zero, zero, a["L0_xattn_bo"],
                   a["L0_ffn_Wr"], a["L0_ffn_br"])
    w1 = attention(a["L1_xattn_Wq"], a["L1_xattn_Wk"], a["L1_xattn_Wv"], a["L1_xattn_Wo"], a["L1_xattn_bq"], a["L1_xattn_bk"],
                   a["L1_xattn_bv"], a["L1_xattn_bo"], a["L1_ffn_w_gate"].T, np.zeros(E, np.float32))
    by_chunk = lambda m: m.reshape(E, HC, P, D).transpose(0, 2, 1, 3).reshape(E, P, HC * D)
    f0 = np.ascontiguousarray(np.concatenate(
        [a["L0_ffn_W1"], by_chunk(a["L0_ffn_W2"]), np.broadcast_to(a["L0_ffn_b2"][:, None, :], (E, P, D)),
         a["L0_ffn_b1"].reshape(E, HC, P).transpose(0, 2, 1)], 2))
    f1 = np.ascontiguousarray(np.concatenate(
        [a["L1_ffn_w_gate_proj"].transpose(0, 2, 1), a["L1_ffn_w_up_proj"].transpose(0, 2, 1),
         by_chunk(a["L1_ffn_w_down_proj"].transpose(0, 2, 1))], 2))
    const, aug, ids, pad = _constants()
    arrays = {
        "x_in": np.ascontiguousarray(a["x"].reshape(NT, P, D).transpose(1, 0, 2)),
        "ctx_in": np.ascontiguousarray(np.broadcast_to(a["ctx_1024"].transpose(2, 0, 1)[:, :, None, :], (P, NB, HPG, KEYS))),
        "mask_in": np.ascontiguousarray(a["mask_SxS2_ik0"].reshape(TPB, P, KEYS).transpose(1, 0, 2)),
        "gates_in": np.ascontiguousarray(rows(np.concatenate([a["g_xattn"][:1], a["g_ffn"][:1], a["g_xattn"][1:], a["g_ffn"][1:]]))),
        "w0_in": w0, "w1_in": w1, "f0_in": f0, "f1_in": f1,
        "const_in": const, "aug_in": aug, "ids_in": ids, "pad_in": pad,
    }
    nc = bacc.Bacc("TRN2", target_bir_lowering=False, num_devices=1)
    aps = {k: nc.dram_tensor(k, v.shape, mybir.dt.from_np(v.dtype), kind="ExternalInput").ap() for k, v in arrays.items()}
    out = nc.dram_tensor("out", (P, NT, D), F32, kind="ExternalOutput").ap()
    two_layers(nc, **aps, out=out)
    r = run_bass_kernel_spmd(nc, [arrays], core_ids=[0])
    got = r.results[0]["out"]
    return np.ascontiguousarray(got.transpose(1, 0, 2).reshape(NB, SEQ, D))
```

```python
from contextlib import ExitStack

import concourse.bass as bass
from concourse import mybir

F32 = mybir.dt.float32
F32R = mybir.dt.float32r
BF16 = mybir.dt.bfloat16
I32 = mybir.dt.int32
ALU = mybir.AluOpType
ACT = mybir.ActivationFunctionType
AX = mybir.AxisListType

P = 128
D = 128
LAYERS = 2
NB, SEQ, KEYS = 4, 512, 77
TPB = SEQ // P
NT = NB * TPB
TOKENS = NB * SEQ
HEADS, HD = 16, 8
GROUPS, HPG = 4, 4
GK = HPG * KEYS
KT = 3
KROWS = 103
KSIZE = [min(KROWS, GK - KROWS * j) for j in range(KT)]
NS = KT * GROUPS
SCALE = float(HD) ** -0.5
EPS = 1e-5
E, HID = 8, 256
HC = HID // P
MASKED = -1e30
CLAMP = 1e25
SLOTS = 8
SHORT = 4
LAG_UP, LAG_DOWN, LAG_OUT = 1, 3, 4
CHOICES = [1, 2]
FT = [-(-((TOKENS * c + E * (P - 1)) // P) // SLOTS) * SLOTS for c in CHOICES]
REGION = TOKENS + P
BLOCKS = REGION // P
DUMMY = E * BLOCKS
PAY = D + 2
FW = [2 * HID + D + HC, 3 * HID]
NOROW = 1 << 20

C_ID, C_COS, C_SIN = 0, P, P + SEQ
C_HM = C_SIN + SEQ
C_HMV = C_HM + HPG
C_U = C_HMV + KT * 32
C_DESC = C_U + P
C_EB = C_DESC + E
C_K128 = C_EB + E
C_LT = C_K128 + NT
C_J = C_LT + E * E
C_END = C_J + max(FT)
W_Q, W_QR, W_K, W_KR, W_V, W_O, W_BV, W_BO = [D * i for i in range(8)]
W_R = 8 * D
W_BR = W_R + E
W_BQ = W_BR + E
W_BK = W_BQ + 1
W_END = W_BK + 1
SCORE_BANKS, RING = 2, 3
AUG_KEY = 32

AT = {
    "results": -30, "stats": -26, "normalise": -25, "bias": 9, "turn": -22, "project": -20, "high": -19, "low": -19,
    "split": -3, "augment": -2, "weigh0": 5, "weigh1": 9, "weigh2": 13, "sums": 13, "den": 15, "widen": 15, "rden": 17,
    "output": 18, "stats2": 19, "normalise2": 23, "turn2": 23, "router": 25, "route_exp": 26, "ranks": 28,
    "scatter0": 29, "scatter1": 31, "scatter2": 34, "scatter3": 35,
}
MAX_FIRST = -12
MAX_UNITS = [1, 2, 2, 2, 1, 2, 2, 2, 1, 1]
FRONT = {"results", "stats", "normalise", "turn", "project", "high", "low"}
SECOND_FRONT = 6
LAST = NS * (NB - 1)
STEPS = range(AT["results"], LAST + AT["scatter3"] + 1)
KEYS_AT = [-21, LAST + 12]
VALUES_AT = [[-17, -16, -15], [LAST + 17, LAST + 20, LAST + 21]]
BLOCKS_AT = [-14, LAST + 27]
SET_UP_AT = -14
MASK_AT = -5


def due(stage, k):
    return [b for b in range(NB) if (SECOND_FRONT if b == 1 and stage in FRONT else NS * b) + AT[stage] == k]


def max_units(k):
    found = []
    for b in range(NB):
        i = k - NS * b - MAX_FIRST
        if 0 <= i < len(MAX_UNITS):
            found += [(b, sum(MAX_UNITS[:i]) + u) for u in range(MAX_UNITS[i])]
    return found


def bcast(ap, axis, n):
    ap = ap.unsqueeze(axis)
    shape = list(ap.shape)
    shape[axis] = n
    return ap.broadcast_to(shape)


def two_layers(nc, x_in, ctx_in, mask_in, gates_in, w0_in, w1_in, f0_in, f1_in, const_in, aug_in, ids_in, pad_in, out):
    w_in, f_in = [w0_in, w1_in], [f0_in, f1_in]
    with ExitStack() as ctx:
        def sb(name, shape, dt=F32):
            return ctx.enter_context(nc.sbuf_tensor(name, shape, dt))

        def pb(name):
            return ctx.enter_context(nc.psum_tensor(name, [P, 512], F32))

        def sem(name):
            return ctx.enter_context(nc.semaphore(name))

        routed = [nc.dram_tensor(f"routed{l}", (DUMMY * P + P, PAY), F32, kind="Internal").ap() for l in range(LAYERS)]
        q_rows = nc.dram_tensor("q_rows", (LAYERS * NB, GROUPS, 2, 32, SEQ), F32, kind="Internal").ap()
        k_rows = nc.dram_tensor("k_rows", (LAYERS, GROUPS, 4, 32, NB * KEYS), F32, kind="Internal").ap()
        expert_out = [nc.dram_tensor(f"expert_out{l}", (CHOICES[l] * TOKENS, D), F32, kind="Internal").ap() for l in range(LAYERS)]

        x = sb("x", [P, NT, D])
        cst = sb("cst", [P, C_END])
        ident = cst[:, C_ID:C_ID + P]
        cos, sin = cst[:, C_COS:C_COS + SEQ], cst[:, C_SIN:C_SIN + SEQ]
        hm = cst[:, C_HM:C_HM + HPG]
        hmv = cst[:, C_HMV:C_HMV + KT * 32].rearrange("p (j c) -> p j c", j=KT)
        desc, ebase = cst[:, C_DESC:C_DESC + E], cst[:, C_EB:C_EB + E]
        probs = [sb(f"probs{i}", [P, NS, SEQ]) for i in range(2)]
        spare = [probs[i][:, :, :].rearrange("p s c -> p (s c)") for i in range(2)]
        augf = spare[1][:, 0:GROUPS * GK]
        aug = sb("aug", [P, GROUPS, GK], F32R)
        ids = sb("ids", [P, 2, NT], I32)
        pad = sb("pad", [P, PAY])
        cx4 = sb("cx4", [P, NB, HPG, KEYS])
        maski = sb("maski", [P, TPB, KEYS], I32)
        gates = sb("gates", [P, 4])
        tg = sb("tg", [P, 4])
        w = [sb(f"w{l}", [P, W_END]) for l in range(LAYERS)]
        prefix16 = sb("prefix16", [P, P], BF16)
        ones16 = sb("ones16", [P, P], BF16)
        half = sb("half", [P, TPB])
        kr1 = sb("kr1", [P, NB * KEYS])
        kr2 = sb("kr2", [P, NB * KEYS])
        khl = [sb(f"khl{i}", [P, NB * KEYS], F32R) for i in range(2)]
        ksp = spare[1][:, GROUPS * GK:2 * GROUPS * GK]
        ks = sb("ks", [P, GROUPS, NB, GK], F32R)
        ks_by_head = ks[:, :, :, :].rearrange("p g b c -> p (g b) c")
        vb = sb("vb", [P, KT, NB, D])
        tgbo = [sb(f"tgbo{l}", [P, D]) for l in range(LAYERS)]
        st = sb("st", [P, TPB, 6])
        mv = sb("mv", [P, TPB, 2])
        ve = sb("ve", [P, TPB])
        rstd = sb("rstd", [P, TPB])
        nrm = sb("nrm", [P, TPB, D])
        nT = sb("nT", [P, SEQ])
        qr1 = sb("qr1", [P, SEQ])
        qr2 = sb("qr2", [P, SEQ])
        qhl = [sb(f"qhl{i}", [P, SEQ], F32R) for i in range(2)]
        qs = [sb(f"qs{i}", [P, GROUPS, SEQ], F32R) for i in range(3)]
        negm = sb("negm", [P, TPB, HEADS])
        negmh = sb("negmh", [P, TPB, HEADS], F32R)
        augt = [sb(f"augt{l}", [P, TPB, P]) for l in range(LAYERS)]
        augT = [sb(f"augT{i}", [P, SEQ], F32R) for i in range(2)]
        maskT = sb("maskT", [P, SEQ], F32R)
        nums = sb("nums", [P, SEQ])
        dens = sb("dens", [P, SEQ])
        rd = sb("rd", [P, TPB, HEADS])
        rdx = dens
        att = sb("att", [P, SEQ])
        st2 = sb("st2", [P, TPB, 6])
        mv2 = sb("mv2", [P, TPB, 2])
        ve2 = sb("ve2", [P, TPB])
        rstd2 = sb("rstd2", [P, TPB])
        pay = [sb(f"pay{c}", [P, NT, PAY]) for c in range(2)]
        nT2 = sb("nT2", [P, SEQ])
        lg = sb("lg", [P, TPB, E])
        lg2 = sb("lg2", [P, TPB, E])
        wt = sb("wt", [P, TPB, E])
        wm = sb("wm", [P, TPB])
        mx = [sb(f"mx{i}", [P, TPB]) for i in range(2)]
        oh = [sb(f"oh{i}", [P, TPB, E], BF16) for i in range(2)]
        ohs = sb("ohs", [P, TPB, E], BF16)
        run = [sb(f"run{l}", [P, NB + 1, E], BF16) for l in range(LAYERS)]
        tally = sb("tally", [P, E])
        shifted = sb("shifted", [P, TPB, E])
        expd = sb("expd", [P, TPB, E])
        se = sb("se", [P, TPB])
        re = sb("re", [P, TPB])
        rk = sb("rk", [P, TPB, E])
        ginv = sb("ginv", [P, TPB])
        slotf = sb("slotf", [P, TPB])
        slot = [sb(f"slot{c}", [P, NT], I32) for c in range(2)]
        gt = sb("gt", [P, E, NT])
        tiles = sb("tiles", [P, E])
        cumx = sb("cumx", [P, E, E])
        cum = sb("cum", [P, E])
        le = sb("le", [P, max(FT), E])
        let = sb("let", [P, max(FT), E])
        ej = sb("ej", [P, max(FT)])
        kj = sb("kj", [P, max(FT)])
        bj = sb("bj", [P, max(FT)])
        meta = [sb(f"meta{l}", [1, 2, FT[l]], I32) for l in range(LAYERS)]
        pad_row = sb("pad_row", [1, E])
        pad_at = [sb(f"pad_at{l}", [1, E], I32) for l in range(LAYERS)]
        xt = [sb(f"xt{i}", [P, PAY])[:, :] for i in range(SHORT)] + [spare[1][:, (8 + i) * SEQ:(8 + i) * SEQ + PAY] for i in range(SLOTS - SHORT)]
        fw = [spare[0][:, i * max(FW):(i + 1) * max(FW)] for i in range(SLOTS)]
        xT = [sb(f"xT{i}", [P, P]) for i in range(SHORT)]
        hid = [(nums, dens)[i // 2][:, (i % 2) * HID:(i % 2 + 1) * HID].rearrange("p (c t) -> p c t", c=HC) for i in range(SHORT)]
        tanhs = [qr1[:, i * HID:(i + 1) * HID] for i in range(2)]
        silu = [qr2[:, i * HID:(i + 1) * HID] for i in range(2)]
        rows_at = [sb(f"rows_at{i}", [P, 1], I32) for i in range(SHORT)]
        yb = [qr1[:, i * D:(i + 1) * D] for i in range(SHORT)]
        yo = [sb(f"yo{i}", [P, D]) for i in range(SHORT)]
        yin = [[sb(f"yin{b}", [P, SEQ])[:, :] for b in range(NB)], [probs[1][:, b, :] for b in range(NB)]]

        ps_s = [pb(f"ps_s{i}") for i in range(SCORE_BANKS)]
        ps_a = [pb(f"ps_a{i}") for i in range(RING)]
        ps_t = pb("ps_t")
        ps_n = pb("ps_n")
        ps_d = pb("ps_d")

        up_bank = [*ps_s, *ps_a[2:], ps_t]
        down_bank = [ps_n, ps_d]
        vtmp = yin[0]

        ld_x = [sem(f"ld_x{b}") for b in range(NB)]
        ld_m = sem("ld_m")
        ld_i, ld_g = sem("ld_i"), sem("ld_g")
        ld_c, ld_k, ld_aug = sem("ld_c"), sem("ld_k"), sem("ld_aug")
        ld_w = [sem(f"ld_w{l}") for l in range(LAYERS)]
        padded = [sem(f"padded{l}") for l in range(LAYERS)]
        s_aug, s_tanh, s_const, s_masked = sem("s_aug"), sem("s_tanh"), sem("s_const"), sem("s_masked")
        s_tgbo = sem("s_tgbo")
        ring_full, ring_used = sem("ring_full"), sem("ring_used")
        k_split, k_put, kspread, ks_ok, q_put = sem("k_split"), sem("k_put"), sem("kspread"), sem("ks_ok"), [sem(f"q_put{i}") for i in range(2)]
        pad_ok = sem("pad_ok")
        run_ok = sem("run_ok")
        s_vb = sem("s_vb")
        var1, rstd1_ok, nrm_ok, nrmT_ok, nT_ok = sem("var1"), sem("rstd1_ok"), sem("nrm_ok"), sem("nrmT_ok"), sem("nT_ok")
        rot_ok, q_ok, qh_ok, ql_ok, qspread = sem("rot_ok"), sem("q_ok"), sem("qh_ok"), sem("ql_ok"), [sem(f"qspread{i}") for i in range(3)]
        augt_ok, augt_tr, augT_ok = sem("augt_ok"), sem("augt_tr"), sem("augT_ok")
        mask_tr, maskT_ok = sem("mask_tr"), sem("maskT_ok")
        sc_full, exp_ok, pv_ok, nd_ok = sem("sc_full"), sem("exp_ok"), sem("pv_ok"), sem("nd_ok")
        rdx_ok = sem("rdx_ok")
        den_tr, rd_ok, rd_tr, att_ok = sem("den_tr"), sem("rd_ok"), sem("rd_tr"), sem("att_ok")
        xb_ok = sem("xb_ok")
        var2, rstd2_ok, nrm2_ok, pay_tr, nT2_ok = sem("var2"), sem("rstd2_ok"), sem("nrm2_ok"), sem("pay_tr"), sem("nT2_ok")
        pay2_ok = sem("pay2_ok")
        sh_ok, ex_ok, ohs_ok, slot_ok, scattered = sem("sh_ok"), sem("ex_ok"), sem("ohs_ok"), sem("slot_ok"), sem("scattered")
        meta_ok = sem("meta_ok")
        s_dve, s_pool = sem("s_dve"), sem("s_pool")
        def per_layer(name):
            return [sem(f"{name}{l}") for l in range(LAYERS)]
        f_ld = [[sem(f"f_ld{l}_{i}") for i in range(SLOTS)] for l in range(LAYERS)]
        f_xtr, f_xT, f_up, f_hid, f_dn = map(per_layer, ("f_xtr", "f_xT", "f_up", "f_hid", "f_dn"))
        f_th, f_y, f_silu, f_turn = map(per_layer, ("f_th", "f_y", "f_silu", "f_turn"))
        f_put = [[sem(f"f_put{l}_{i}") for i in range(SHORT)] for l in range(LAYERS)]
        y_ld = [[[sem(f"y_ld{l}_{b}_{c}") for c in range(CHOICES[l])] for b in range(NB)] for l in range(LAYERS)]
        x_ok, o_put = sem("x_ok"), sem("o_put")

        block = ctx.enter_context(nc.Block())

        def score_tile(s):
            return s // GROUPS, s % GROUPS

        class Count:
            def __init__(self, n=0):
                self.n = n

            def next(self):
                self.n += 1
                return self.n - 1

        def rounds(eng, l, body):
            body(0, True)
            with eng.Fori(1, FT[l] // SLOTS) as r:
                body(r, False)

        @block.sync
        def _(sp):
            sp.dma_start(x[:, 0:TPB, :], x_in[:, 0:TPB, :]).then_inc(ld_x[0], 16)
            sp.dma_start(cst[:, :], const_in).then_inc(ld_c, 16)
            sp.dma_start(w[0][:, :], w_in[0]).then_inc(ld_w[0], 16)
            sp.dma_start(cx4[:, :, :, :], ctx_in).then_inc(ld_k, 16)
            sp.dma_start(ids[:, :, :], ids_in).then_inc(ld_i, 16)
            sp.dma_start(maski[:, :, :], mask_in).then_inc(ld_m, 16)
            for b in range(1, NB):
                sp.dma_start(x[:, b * TPB:(b + 1) * TPB, :], x_in[:, b * TPB:(b + 1) * TPB, :]).then_inc(ld_x[b], 16)

            def put_k(l):
                sp.wait_ge(k_split, l + 1)
                for c in range(4):
                    sp.dma_start(k_rows[l, :, c, :, :], khl[c // 2][:, :].bitcast(F32)).then_inc(k_put, 16)

            def take_k(l):
                sp.wait_ge(k_put, 64 * (l + 1))
                if l:
                    sp.wait_ge(pv_ok, KT * NB * l)
                sp.dma_start(ksp.rearrange("p (g k) -> p g k", g=GROUPS), k_rows[l].rearrange("g c r k -> (c r) g k")).then_inc(kspread, 16)

            def put_q(n):
                for half, ready in enumerate((qh_ok, ql_ok)):
                    sp.wait_ge(ready, n + 1)
                    sp.dma_start(q_rows[n, :, half, :, :], qhl[half][:, :].bitcast(F32)).then_inc(q_put[half], 16)

            def take_q(n):
                if n >= 3:
                    sp.wait_ge(sc_full, NS * (n - 2))
                for half in range(2):
                    sp.wait_ge(q_put[half], 16 * (n + 1))
                    for c in range(2):
                        rows = 64 * c + 32 * half
                        sp.dma_start(qs[n % 3][rows:rows + 32, :, :].bitcast(F32), q_rows[n, :, half, :, :].rearrange("g r k -> r g k")).then_inc(qspread[n % 3], 16)

            def load_tiles(l):
                sp.wait_ge(meta_ok, l + 1)

                def body(r, first):
                    def offsets(row, last):
                        _, values = nc.values_load_multi_w_load_instructions(
                            meta[l][0:1, row, bass.ds(r * SLOTS, SLOTS)], engines=(mybir.EngineType.SP,), min_val=0, max_val=last,
                            skip_runtime_bounds_check_because="plan clamps it")
                        return values

                    weights_at, rows_from = offsets(0, (E - 1) * P * FW[l]), offsets(1, DUMMY * P * PAY)

                    def load_weights(i):
                        sp.dma_start(fw[i][:, 0:FW[l]], f_in[l].rearrange("e p f -> (e p f)")[bass.ds(weights_at[i], P * FW[l])].rearrange("(p f) -> p f", p=P)).then_inc(f_ld[l][i], 16)

                    def load_rows(i):
                        sp.dma_start(xt[i], routed[l].rearrange("k c -> (k c)")[bass.ds(rows_from[i], P * PAY)].rearrange("(p c) -> p c", p=P)).then_inc(f_ld[l][i], 16)

                    ahead = SLOTS // 2 if first else 0
                    for i in range(ahead):
                        load_weights(i)
                    if first:
                        sp.wait_ge(scattered, 16 * sum(CHOICES[:l + 1]) * NT)
                        sp.wait_ge(padded[l], 16 * (E + 1))
                    for i in range(SLOTS):
                        if not first:
                            sp.wait_ge(f_y[l], (r - 1) * SLOTS + i + 1)
                            sp.sem_inc(f_turn[l], 1)
                        if i >= ahead:
                            load_weights(i)
                        load_rows(i)

                rounds(sp, l, body)

            def load_results(l):
                for i in range(SHORT):
                    sp.wait_ge(f_put[l][i], 16 * (FT[l] // SHORT))
                for b in range(NB):
                    for c in range(CHOICES[l]):
                        src = expert_out[l][c * TOKENS + b * SEQ:c * TOKENS + (b + 1) * SEQ, :].rearrange("(t p) d -> p t d", p=P)
                        if l and not c:
                            sp.wait_ge(x_ok, b + 1)
                        sp.dma_start(yin[c][b].rearrange("p (t c) -> p t c", c=D), src).then_inc(y_ld[l][b][c], 16)

            for l in range(LAYERS):
                for b in range(NB):
                    if l == 0 and b == 0:
                        put_k(0)
                        take_k(0)
                    put_q(NB * l + b)
                    take_q(NB * l + b)
                    if l == 0 and b == 1:
                        sp.dma_start(w[1][:, :], w_in[1]).then_inc(ld_w[1], 16)
                if l == 0:
                    put_k(1)
                    take_k(1)
                load_tiles(l)
                load_results(l)
            for b in range(NB):
                sp.wait_ge(x_ok, NB + b + 1)
                sp.dma_start(out[:, b * TPB:(b + 1) * TPB, :], x[:, b * TPB:(b + 1) * TPB, :]).then_inc(o_put, 16)
            sp.wait_ge(o_put, 16 * NB)

        @block.gpsimd
        def _(pool):
            chain = Count()

            def link(ins):
                ins.then_inc(s_pool, 1)
                pool.wait_ge(s_pool, chain.next() + 1)

            nc.gpsimd.memset(half[:, :], -0.5)
            nc.gpsimd.memset(ones16[:, :], 1.0)
            for l in range(LAYERS):
                nc.gpsimd.memset(augt[l][:, :, :], 0.0)
                nc.gpsimd.memset(run[l][:, 0, :], 0.0)
            nc.gpsimd.memset(rows_at[0][:, :], 0).then_inc(s_const, 1)

            def power(var, ve_, rstd_, done, n):
                pool.wait_ge(var, n + 1)
                link(nc.gpsimd.tensor_scalar(ve_[:, :], (mv if var is var1 else mv2)[:, :, 1], EPS, None, ALU.add))
                nc.gpsimd.tensor_tensor(rstd_[:, :], ve_[:, :], half[:, :], ALU.pow).then_inc(done, 1)

            def add_q(n):
                pool.wait_ge(rot_ok, n + 1)
                if n:
                    pool.wait_ge(ql_ok, n)
                nc.gpsimd.tensor_tensor(qr1[:, :], qr1[:, :], qr2[:, :], ALU.add).then_inc(q_ok, 1)

            def add_bias(n):
                l, b = divmod(n, NB)
                pool.wait_ge(s_tgbo, l + 1)
                pool.wait_ge(nrm_ok, n + 1)
                xb = x[:, b * TPB:(b + 1) * TPB, :]
                nc.gpsimd.tensor_tensor(xb, xb, bcast(tgbo[l][:, :], 1, TPB), ALU.add).then_inc(xb_ok, 1)

            def scatter(n, i):
                l, b = divmod(n, NB)
                if i == 0:
                    pool.wait_ge(slot_ok, n + 1)
                    if l:
                        pool.wait_ge(pay2_ok, n - NB + 1)
                for c in range(CHOICES[l]):
                    t = b * TPB + i
                    pool.indirect_dma_start(
                        out=routed[l], out_offset=bass.IndirectOffsetOnAxis(ap=slot[c][:, t:t + 1], axis=0),
                        in_=pay[c][:, t, :], in_offset=None).then_inc(scattered, 16)

            def second_copy(n):
                b = n % NB
                pool.wait_ge(nrm2_ok, n + 1)
                nc.gpsimd.tensor_copy(pay[1][:, b * TPB:(b + 1) * TPB, 0:D], pay[0][:, b * TPB:(b + 1) * TPB, 0:D]).then_inc(pay2_ok, 1)

            def put_tiles(l):
                last_row = pool.alloc_register(f"last_row{l}")
                pool.reg_mov(last_row, CHOICES[l] * TOKENS - 1)

                def body(r, first):
                    for i in range(SLOTS):
                        pool.wait_ge(f_y[l], r * SLOTS + i + 1)
                        pool.sem_inc(f_turn[l], 1)
                        pool.indirect_dma_start(
                            out=expert_out[l], out_offset=bass.IndirectOffsetOnAxis(ap=rows_at[i % SHORT][:, :], axis=0),
                            in_=yo[i % SHORT][:, :], in_offset=None, bounds_check=last_row, oob_is_err=False).then_inc(f_put[l][i % SHORT], 16)

                rounds(pool, l, body)

            for l in range(LAYERS):
                n0 = NB * l
                for k in STEPS:
                    for b in due("project", k):
                        if l == 0:
                            add_q(n0 + b)
                    for b in due("stats", k):
                        power(var1, ve, rstd, rstd1_ok, n0 + b)
                    for b in due("bias", k):
                        add_bias(n0 + b)
                    for b in due("stats2", k):
                        power(var2, ve2, rstd2, rstd2_ok, n0 + b)
                    for b in due("normalise2", k):
                        if l:
                            second_copy(n0 + b)
                    for i in range(TPB):
                        for b in due(f"scatter{i}", k):
                            scatter(n0 + b, i)
                put_tiles(l)

        @block.scalar
        def _(act):
            act.dma_start(gates[:, :], gates_in).then_inc(ld_g, 16)
            act.wait_ge(ld_g, 16)
            nc.scalar.activation(tg[:, :], gates[:, :], ACT.Tanh).then_inc(s_tanh, 1)
            act.dma_start(pad[:, :], pad_in).then_inc(ld_i, 16)
            act.dma_start(augf, aug_in).then_inc(ld_aug, 16)
            act.wait_ge(ld_i, 32)
            for l in range(LAYERS):
                act.dma_start(routed[l][DUMMY * P:(DUMMY + 1) * P, :], pad[:, :]).then_inc(padded[l], 16)

            def copy_nT(n):
                act.wait_ge(nrmT_ok, n + 1)
                nc.scalar.activation(nT[:, :], ps_t[:, :], ACT.Copy).then_inc(nT_ok, 1)

            def high_q(n):
                act.wait_ge(q_ok, n + 1)
                if n:
                    act.wait_ge(q_put[0], 16 * n)
                nc.scalar.activation(qhl[0][:, :], qr1[:, :], ACT.Copy).then_inc(qh_ok, 1)

            def copy_augT(n):
                act.wait_ge(augt_tr, n + 1)
                if n >= 2:
                    act.wait_ge(sc_full, NS * (n - 1))
                nc.scalar.activation(augT[n % 2][:, :], ps_t[:, :], ACT.Copy).then_inc(augT_ok, 1)

            def exps(n, s):
                j, g = score_tile(s)
                act.wait_ge(sc_full, NS * n + s + 1)
                if n >= 2 and s == 0:
                    act.wait_ge(pv_ok, KT * (n - 1))
                nc.scalar.activation(probs[n % 2][0:KSIZE[j], s, :], ps_s[(NS * n + s) % SCORE_BANKS][0:KSIZE[j], :], ACT.Exp, scale=SCALE).then_inc(exp_ok, 1)

            def copy_nd(n):
                act.wait_ge(pv_ok, KT * (n + 1))
                if n:
                    act.wait_ge(att_ok, n)
                nc.scalar.activation(dens[:, :], ps_d[:, :], ACT.Copy).then_inc(nd_ok, 1)
                nc.scalar.activation(nums[:, :], ps_n[:, :], ACT.Copy).then_inc(nd_ok, 1)

            def widen_rd(n):
                act.wait_ge(rd_ok, n + 1)
                if n:
                    act.wait_ge(rd_tr, n)
                nc.scalar.activation(rdx[:, :].rearrange("p (q d) -> p q d", d=HD),
                                     bcast(rd[:, :, :].rearrange("p t h -> p (t h)"), 2, HD), ACT.Copy).then_inc(rdx_ok, 1)

            def copy_nT2(n):
                act.wait_ge(pay_tr, n + 1)
                nc.scalar.activation(nT2[:, :], ps_t[:, :], ACT.Copy).then_inc(nT2_ok, 1)

            def route_exp(n):
                act.wait_ge(sh_ok, n + 1)
                if n < NB:
                    nc.scalar.activation(expd[:, :, :], shifted[:, :, :], ACT.Exp).then_inc(ex_ok, 1)
                else:
                    nc.scalar.activation(se[:, :], shifted[:, :, 0], ACT.Exp).then_inc(ex_ok, 1)

            def mask_keys(l):
                act.wait_ge(kspread, 16 * (l + 1))
                if l:
                    act.wait_ge(sc_full, NS * NB * l)
                for h in range(HPG // 2):
                    last = nc.scalar.activation(ks_by_head[:, :, h * KEYS:(h + 1) * KEYS], ksp.rearrange("p (q k) -> p q k", k=KEYS),
                                                ACT.Copy, scale=hm[:, h:h + 1])
                last.then_inc(ks_ok, 1)

            def pad_rows(l):
                act.wait_ge(pad_ok, l + 1)
                _, offsets = nc.values_load_multi_w_load_instructions(
                    pad_at[l][0:1, :], engines=(mybir.EngineType.Activation,), min_val=0, max_val=(DUMMY - 1) * P * PAY,
                    skip_runtime_bounds_check_because="no expert has more rows than there are tokens")
                for e in range(E):
                    at = offsets[e]
                    act.dma_start(routed[l].rearrange("k c -> (k c)")[bass.ds(at, P * PAY)].rearrange("(p c) -> p c", p=P), pad[:, :]).then_inc(padded[l], 16)

            def relu(l, i, count, first):
                act.wait_ge(f_up[l], count)
                if not first:
                    act.wait_ge(f_dn[l], count - SHORT)
                for c in range(HC):
                    last = nc.scalar.activation(hid[i % SHORT][:, c, :], up_bank[i % SHORT][:, c * P:(c + 1) * P], ACT.Relu,
                                                bias=fw[i][:, FW[0] - HC + c:FW[0] - HC + c + 1])
                last.then_inc(f_hid[l], 1)

            def tanh(l, i, count, first):
                act.wait_ge(f_up[l], count)
                if not first:
                    act.wait_ge(f_silu[l], count - 2)
                nc.scalar.activation(tanhs[i % 2], up_bank[i % SHORT][:, 0:HID], ACT.Tanh, scale=0.5).then_inc(f_th[l], 1)

            def tiles_act(l):
                def body(r, first):
                    for i in range(SLOTS):
                        j = r * SLOTS + i
                        if l:
                            act.wait_ge(f_xtr[l], j + 1)
                            if not (first and i < SHORT):
                                act.wait_ge(f_up[l], j + 1 - SHORT)
                            nc.scalar.activation(xT[i % SHORT][:, :], ps_a[i % 2][:, 0:P], ACT.Copy).then_inc(f_xT[l], 1)
                        if not (first and i < LAG_UP):
                            if l:
                                tanh(l, (i - LAG_UP) % SLOTS, j, first and i < LAG_UP + 2)
                            else:
                                relu(l, (i - LAG_UP) % SLOTS, j, first and i < LAG_UP + SHORT)

                rounds(act, l, body)
                (tanh if l else relu)(l, SLOTS - 1, FT[l], False)

            for l in range(LAYERS):
                n0 = NB * l
                for k in STEPS:
                    if 0 <= k < NB * NS:
                        exps(n0 + k // NS, k % NS)
                    if l == 0 and k == MASK_AT:
                        act.wait_ge(mask_tr, 1)
                        nc.scalar.activation(maskT[:, :], ps_t[:, :], ACT.Copy).then_inc(maskT_ok, 1)
                    for b in due("turn", k):
                        copy_nT(n0 + b)
                    for b in due("high", k):
                        high_q(n0 + b)
                        if n0 + b == 0:
                            act.wait_ge(ld_aug, 16)
                            nc.scalar.activation(aug[:, :, :].rearrange("p g k -> p (g k)"), augf, ACT.Copy).then_inc(s_aug, 1)
                    for b in due("augment", k):
                        copy_augT(n0 + b)
                    for b in due("sums", k):
                        copy_nd(n0 + b)
                    for b in due("widen", k):
                        widen_rd(n0 + b)
                    for b in due("turn2", k):
                        copy_nT2(n0 + b)
                    for b in due("route_exp", k):
                        route_exp(n0 + b)
                    for kl in range(LAYERS):
                        if l == 0 and k == BLOCKS_AT[kl]:
                            mask_keys(kl)
                pad_rows(l)
                tiles_act(l)

        @block.tensor
        def _(pe):
            unit = Count()
            reader = []

            def ring():
                u = unit.next()
                if u >= RING:
                    pe.wait_ge(ring_used, u - RING + 1)
                return ps_a[u % RING]

            def keys(l):
                pe.wait_ge(ld_w[l], 16)
                pe.wait_ge(ld_k, 16)
                for c in ((W_K,) if l else (W_K, W_KR)):
                    nc.tensor.matmul(ring()[:, 0:NB * KEYS], w[l][:, c:c + D], cx4[:, :, 0, :], start=True, stop=True).then_inc(ring_full, 1)

            def values(l, j):
                bank = ring()
                for b in range(NB):
                    src = cx4[:, b, :, :].rearrange("p h k -> p (h k)")[:, KROWS * j:KROWS * j + KSIZE[j]]
                    last = nc.tensor.matmul(bank[0:KSIZE[j], b * D:(b + 1) * D], src, w[l][:, W_V:W_V + D], start=True, stop=True)
                last.then_inc(ring_full, 1)

            def transposes(src, done, read, value):
                if reader:
                    pe.wait_ge(*reader[-1])
                reader.append((read, value))
                for i in range(TPB):
                    last = nc.tensor.transpose(ps_t[:, i * P:(i + 1) * P], src(i), ident)
                last.then_inc(done, 1)

            def project(n):
                pe.wait_ge(nT_ok, n + 1)
                for c in ((W_Q, W_QR) if n < NB else (W_Q,)):
                    nc.tensor.matmul(ring()[:, :], w[n // NB][:, c:c + D], nT[:, :], start=True, stop=True).then_inc(ring_full, 1)

            def front(n):
                pe.wait_ge(nrm_ok, n + 1)
                transposes(lambda i: nrm[:, i, :], nrmT_ok, nT_ok, n + 1)

            def scores_for_max(n, u):
                l, b = divmod(n, NB)
                i, g = divmod(u, GROUPS)
                if u == 0:
                    pe.wait_ge(qspread[n % 3], 64 * (n // 3 + 1))
                    if b == 0:
                        pe.wait_ge(ks_ok, 2 * (l + 1))
                bank = ring()
                if l:
                    if n == NB and u == 0:
                        pe.wait_ge(maskT_ok, 1)
                    nc.tensor.matmul(bank[:, 0:GK], maskT[:, i * P:(i + 1) * P], aug[:, g, :], start=True, stop=False)
                nc.tensor.matmul(bank[:, 0:GK], qs[n % 3][:, g, i * P:(i + 1) * P], ks[:, g, b, :], start=not l, stop=True).then_inc(ring_full, 1)

            def augmenting(n):
                pe.wait_ge(augt_ok, n + 1)
                transposes(lambda i: augt[n // NB][:, i, :], augt_tr, augT_ok, n + 1)

            def scores(n, s):
                l, b = divmod(n, NB)
                j, g = score_tile(s)
                k = NS * n + s
                if s == 0:
                    pe.wait_ge(augT_ok, n + 1)
                    if n == 0:
                        pe.wait_ge(s_aug, 1)
                if k >= SCORE_BANKS:
                    pe.wait_ge(exp_ok, k - SCORE_BANKS + 1)
                bank = ps_s[k % SCORE_BANKS][0:KSIZE[j], :]
                lo, hi = KROWS * j, KROWS * j + KSIZE[j]
                nc.tensor.matmul(bank, ks[:, g, b, lo:hi], qs[n % 3][:, g, :], start=True, stop=False)
                nc.tensor.matmul(bank, aug[:, g, lo:hi], augT[n % 2][:, :], start=False, stop=True).then_inc(sc_full, 1)

            def weigh(n, j):
                l, b = divmod(n, NB)
                pe.wait_ge(exp_ok, NS * n + GROUPS * (j + 1))
                if j == 0:
                    if b == 0:
                        pe.wait_ge(s_vb, KT * (l + 1))
                    if n:
                        pe.wait_ge(nd_ok, 2 * n)
                kk = KSIZE[j]
                for bank, lhs in ((ps_n, lambda g: vb[0:kk, j, b, 32 * g:32 * g + 32]), (ps_d, lambda g: hmv[0:kk, j, :])):
                    for g in range(GROUPS):
                        last = nc.tensor.matmul(bank[32 * g:32 * g + 32, :], lhs(g), probs[n % 2][0:kk, j * GROUPS + g, :],
                                                start=j == 0, stop=j == KT - 1)
                last.then_inc(pv_ok, 1)

            def den_to_tokens(n):
                pe.wait_ge(nd_ok, 2 * n + 1)
                transposes(lambda i: dens[:, i * P:(i + 1) * P], den_tr, rd_ok, n + 1)

            def rden_to_dims(n):
                pe.wait_ge(rdx_ok, n + 1)
                transposes(lambda i: rdx[:, i * P:(i + 1) * P], rd_tr, att_ok, n + 1)

            def output(n):
                pe.wait_ge(att_ok, n + 1)
                bank = ring()
                for i in range(TPB):
                    last = nc.tensor.matmul(bank[:, i * D:(i + 1) * D], att[:, i * P:(i + 1) * P], w[n // NB][:, W_O:W_O + D], start=True, stop=True)
                last.then_inc(ring_full, 1)

            def routed_T(n):
                pe.wait_ge(nrm2_ok, n + 1)
                transposes(lambda i: pay[0][:, (n % NB) * TPB + i, 0:D], pay_tr, nT2_ok, n + 1)

            def router(n):
                pe.wait_ge(nT2_ok, n + 1)
                bank = ring()
                for i in range(TPB):
                    last = nc.tensor.matmul(bank[:, i * E:(i + 1) * E], nT2[:, i * P:(i + 1) * P], w[n // NB][:, W_R:W_R + E], start=True, stop=True)
                last.then_inc(ring_full, 1)

            def ranks(n):
                l, b = divmod(n, NB)
                pe.wait_ge(ohs_ok, n + 1)
                if n == 0:
                    pe.wait_ge(s_const, 1)
                bank = ring()
                nc.tensor.matmul(bank[:, 0:TPB * E], prefix16[:, :], ohs[:, :, :].rearrange("p t e -> p (t e)"), start=True, stop=False)
                for i in range(1, TPB):
                    nc.tensor.matmul(bank[:, i * E:TPB * E], ones16[:, :], ohs[:, 0:TPB - i, :].rearrange("p t e -> p (t e)"), start=False, stop=False)
                if b:
                    pe.wait_ge(run_ok, n)
                nc.tensor.matmul(bank[:, 0:TPB * E], ones16[:, :], bcast(run[l][:, b, :], 1, TPB), start=False, stop=True).then_inc(ring_full, 1)

            def totals(l):
                pe.wait_ge(run_ok, NB * (l + 1))
                nc.tensor.matmul(ring()[:, 0:E], ones16[:, :], run[l][:, NB, :], start=True, stop=True).then_inc(ring_full, 1)

            def tiles_pe(l):
                chunks = 2 * HC if l else HC
                dn0 = chunks * P

                def up(i, count):
                    pe.wait_ge(f_xT[l], count)
                    for c in range(chunks):
                        last = nc.tensor.matmul(up_bank[i % SHORT][:, c * P:(c + 1) * P], fw[i][:, c * P:(c + 1) * P], xT[i % SHORT][:, :], start=True, stop=True)
                    last.then_inc(f_up[l], 1)

                def down(i, count, first):
                    pe.wait_ge(f_hid[l], count)
                    if not first:
                        pe.wait_ge(f_y[l], count - 2)
                    for c in range(HC):
                        last = nc.tensor.matmul(down_bank[i % 2][:, 0:D], hid[i % SHORT][:, c, :], fw[i][:, dn0 + c * D:dn0 + (c + 1) * D], start=c == 0, stop=c == HC - 1)
                    last.then_inc(f_dn[l], 1)

                def body(r, first):
                    for i in range(SLOTS):
                        j = r * SLOTS + i
                        pe.wait_ge(f_ld[l][i], 32 * (r + 1))
                        if not (first and i < 2):
                            pe.wait_ge(f_xT[l], j - 1)
                        nc.tensor.transpose(ps_a[i % 2][:, 0:P], xt[i][:, 0:D], ident).then_inc(f_xtr[l], 1)
                        if not (first and i < LAG_UP):
                            up((i - LAG_UP) % SLOTS, j + 1 - LAG_UP)
                        if not (first and i < LAG_DOWN):
                            down((i - LAG_DOWN) % SLOTS, j + 1 - LAG_DOWN, first and i < LAG_DOWN + 2)

                rounds(pe, l, body)
                up(SLOTS - 1, FT[l])
                for i in range(SLOTS - LAG_DOWN, SLOTS):
                    down(i, FT[l] - SLOTS + i + 1, False)

            pe.wait_ge(ld_c, 16)
            for l in range(LAYERS):
                n0 = NB * l
                for k in STEPS:
                    if 0 <= k < NB * NS:
                        scores(n0 + k // NS, k % NS)
                    for b, u in max_units(k):
                        scores_for_max(n0 + b, u)
                    for b in due("den", k):
                        den_to_tokens(n0 + b)
                    for b in due("rden", k):
                        rden_to_dims(n0 + b)
                    for b in due("router", k):
                        router(n0 + b)
                    for b in due("ranks", k):
                        ranks(n0 + b)
                    for b in due("project", k):
                        project(n0 + b)
                    for b in due("output", k):
                        output(n0 + b)
                    for kl in range(LAYERS):
                        if l == 0 and k == KEYS_AT[kl]:
                            keys(kl)
                        for j in range(KT):
                            if l == 0 and k == VALUES_AT[kl][j]:
                                values(kl, j)
                    if l == 0 and k == MASK_AT:
                        pe.wait_ge(s_masked, 1)
                        transposes(lambda i: augt[1][:, i, :], mask_tr, maskT_ok, 1)
                    for b in due("turn", k):
                        front(n0 + b)
                    for b in due("augment", k):
                        augmenting(n0 + b)
                    for b in due("turn2", k):
                        routed_T(n0 + b)
                    for j in range(KT):
                        for b in due(f"weigh{j}", k):
                            weigh(n0 + b, j)
                totals(l)
                tiles_pe(l)

        @block.vector
        def _(dve):
            unit, chain = Count(), Count()

            def link(ins):
                ins.then_inc(s_dve, 1)
                dve.wait_ge(s_dve, chain.next() + 1)

            def ring():
                u = unit.next()
                dve.wait_ge(ring_full, u + 1)
                return ps_a[u % RING]

            def keys(l):
                wl = w[l]
                shape = "p (b k) -> p b k"
                a = ring()[:, 0:NB * KEYS]
                if l == 0:
                    nc.vector.tensor_tensor(kr1[:, :].rearrange(shape, b=NB), a.rearrange(shape, b=NB), bcast(cos[:, 0:KEYS], 1, NB),
                                            ALU.mult).then_inc(ring_used, 1)
                    a = ring()[:, 0:NB * KEYS]
                    nc.vector.tensor_tensor(kr2[:, :].rearrange(shape, b=NB), a.rearrange(shape, b=NB), bcast(sin[:, 0:KEYS], 1, NB),
                                            ALU.mult).then_inc(ring_used, 1)
                    dve.wait_ge(ring_used, unit.n)
                    link(nc.vector.tensor_tensor(kr1[:, :], kr1[:, :], kr2[:, :], ALU.add))
                else:
                    nc.vector.tensor_scalar(kr1[:, :], a, wl[:, W_BK:W_BK + 1], None, ALU.add).then_inc(ring_used, 1)
                    dve.wait_ge(ring_used, unit.n)
                if l:
                    dve.wait_ge(k_put, 64 * l)
                link(nc.vector.tensor_copy(khl[0][:, :], kr1[:, :]))
                link(nc.vector.tensor_tensor(khl[1][:, :], kr1[:, :], khl[0][:, :].bitcast(F32), ALU.subtract))
                dve.sem_inc(k_split, 1)
                nc.vector.tensor_scalar(tgbo[l][:, :], wl[:, W_BO:W_BO + D], tg[:, 2 * l:2 * l + 1], None, ALU.mult).then_inc(s_tgbo, 1)

            def values(l, j):
                kk = KSIZE[j]
                a = ring()
                if l:
                    dve.wait_ge(pv_ok, KT * NB * l)
                dst = vb[0:kk, j, :, :].rearrange("p b (g c) -> p (b g) c", g=GROUPS)
                link(nc.vector.tensor_tensor(vtmp[j][0:kk, :].rearrange("p (b c) -> p b c", b=NB), a[0:kk, :].rearrange("p (b c) -> p b c", b=NB),
                                             bcast(w[l][0:kk, W_BV:W_BV + D], 1, NB), ALU.add))
                dve.sem_inc(ring_used, 1)
                nc.vector.tensor_tensor(dst, vtmp[j][0:kk, :].rearrange("p (q c) -> p q c", c=32), bcast(hmv[0:kk, j, :], 1, NB * GROUPS), ALU.mult).then_inc(s_vb, 1)

            def mask_keys(l):
                dve.wait_ge(kspread, 16 * (l + 1))
                if l:
                    dve.wait_ge(sc_full, NS * NB * l)
                for h in range(HPG // 2, HPG):
                    last = nc.vector.tensor_scalar(ks_by_head[:, :, h * KEYS:(h + 1) * KEYS], ksp.rearrange("p (q k) -> p q k", k=KEYS),
                                                   hm[:, h:h + 1], None, ALU.mult)
                last.then_inc(ks_ok, 1)

            def set_up():
                dve.wait_ge(ld_c, 16)
                nc.vector.tensor_copy(prefix16[:, :], cst[:, C_U:C_U + P])
                dve.wait_ge(ld_m, 16)
                dve.wait_ge(s_const, 1)
                nc.vector.tensor_scalar(augt[1][:, :, AUG_KEY:AUG_KEY + KEYS], maski[:, :, :], 0.0, MASKED, ALU.is_equal, ALU.mult).then_inc(s_masked, 1)

            def statistics(src, st_, mv_, done):
                for i in range(TPB):
                    last = nc.vector.bn_stats(st_[:, i, :], src[:, i, :])
                link(last)
                for i in range(TPB):
                    last = nc.vector.bn_aggr(mv_[:, i, :], st_[:, i, :])
                last.then_inc(done, 1)

            def normalise(src, dst, mv_, rstd_, done):
                for i in range(TPB):
                    last = nc.vector.tensor_scalar(dst(i), src[:, i, :], mv_[:, i, 0:1], rstd_[:, i:i + 1], ALU.subtract, ALU.mult)
                last.then_inc(done, 1)

            def xs(n):
                b = n % NB
                return x[:, b * TPB:(b + 1) * TPB, :]

            def front_stats(n):
                if n < NB:
                    dve.wait_ge(ld_x[n], 16)
                if n:
                    dve.wait_ge(rstd1_ok, n)
                statistics(xs(n), st, mv, var1)

            def front_normalise(n):
                dve.wait_ge(rstd1_ok, n + 1)
                dve.wait_ge(var1, n + 1)
                if n:
                    dve.wait_ge(nrmT_ok, n)
                normalise(xs(n), lambda i: nrm[:, i, :], mv, rstd, nrm_ok)

            def rotate(n):
                wl = w[n // NB]
                if n:
                    dve.wait_ge(ql_ok, n)
                a = ring()
                if n < NB:
                    nc.vector.tensor_tensor(qr1[:, :], a[:, :], cos, ALU.mult).then_inc(ring_used, 1)
                    a = ring()
                    nc.vector.tensor_tensor(qr2[:, :], a[:, :], sin, ALU.mult).then_inc(ring_used, 1)
                    dve.wait_ge(ring_used, unit.n)
                    dve.sem_inc(rot_ok, 1)
                else:
                    nc.vector.tensor_scalar(qr1[:, :], a[:, :], wl[:, W_BQ:W_BQ + 1], None, ALU.add).then_inc(ring_used, 1)
                    dve.wait_ge(ring_used, unit.n)
                    dve.sem_inc(q_ok, 1)

            def low_q(n):
                dve.wait_ge(qh_ok, n + 1)
                dve.wait_ge(q_ok, n + 1)
                if n:
                    dve.wait_ge(q_put[1], 16 * n)
                nc.vector.tensor_tensor(qhl[1][:, :], qr1[:, :], qhl[0][:, :].bitcast(F32), ALU.subtract).then_inc(ql_ok, 1)

            def maxima(n, u):
                i, g = divmod(u, GROUPS)
                a = ring()
                nc.vector.tensor_reduce(negm[:, i, g * HPG:(g + 1) * HPG], a[:, 0:GK].rearrange("p (h k) -> p h k", h=HPG),
                                        AX.X, ALU.max, negate=True).then_inc(ring_used, 1)

            def split_max(n):
                l = n // NB
                at = augt[l]
                dve.wait_ge(ring_used, unit.n)
                if n == 0:
                    dve.wait_ge(s_const, 1)
                if n % NB:
                    dve.wait_ge(augt_tr, n)
                if l:
                    link(nc.vector.tensor_scalar(negm[:, :, :], negm[:, :, :], CLAMP, None, ALU.min))
                link(nc.vector.tensor_copy(negmh[:, :, :], negm[:, :, :]))
                nc.vector.tensor_copy(at[:, :, 0:HEADS], negmh[:, :, :].bitcast(F32))
                nc.vector.tensor_tensor(at[:, :, HEADS:2 * HEADS], negm[:, :, :], negmh[:, :, :].bitcast(F32), ALU.subtract).then_inc(augt_ok, 1)

            def recip_den(n):
                dve.wait_ge(den_tr, n + 1)
                if n:
                    dve.wait_ge(rdx_ok, n)
                link(nc.vector.tensor_scalar(rd[:, :, :], ps_t[:, :].rearrange("p (t h d) -> p t h d", t=TPB, d=HD)[:, :, :, 0], 1e-30, None, ALU.max))
                nc.vector.reciprocal(rd[:, :, :], rd[:, :, :]).then_inc(rd_ok, 1)

            def weigh_out(n):
                dve.wait_ge(rd_tr, n + 1)
                dve.wait_ge(nd_ok, 2 * n + 2)
                nc.vector.tensor_tensor(att[:, :], ps_t[:, :], nums[:, :], ALU.mult).then_inc(att_ok, 1)

            def residual(n):
                l = n // NB
                a = ring()
                dve.wait_ge(xb_ok, n + 1)
                nc.vector.scalar_tensor_tensor(xs(n).rearrange("p t c -> p (t c)"), a[:, :], tg[:, 2 * l:2 * l + 1],
                                               xs(n).rearrange("p t c -> p (t c)"), ALU.mult, ALU.add).then_inc(ring_used, 1)
                dve.wait_ge(ring_used, unit.n)

            def normalise2(n):
                dve.wait_ge(rstd2_ok, n + 1)
                dve.wait_ge(var2, n + 1)
                b = n % NB
                normalise(xs(n), lambda i: pay[0][:, b * TPB + i, 0:D], mv2, rstd2, nrm2_ok)

            def best(src, m, one_hot):
                link(nc.vector.tensor_reduce(m[:, :], src[:, :, :], AX.X, ALU.max))
                link(nc.vector.tensor_tensor(wt[:, :, :], src[:, :, :], bcast(m[:, :], 2, E), ALU.is_equal))
                link(nc.vector.tensor_tensor(wt[:, :, :], wt[:, :, :], bcast(desc, 1, TPB), ALU.mult))
                link(nc.vector.tensor_reduce(wm[:, :], wt[:, :, :], AX.X, ALU.max))
                link(nc.vector.tensor_tensor(one_hot[:, :, :], wt[:, :, :], bcast(wm[:, :], 2, E), ALU.is_equal))

            def choose(n):
                l, b = divmod(n, NB)
                a = ring()
                link(nc.vector.tensor_tensor(lg[:, :, :], a[:, 0:TPB * E].rearrange("p (t e) -> p t e", t=TPB),
                                             bcast(w[l][:, W_BR:W_BR + E], 1, TPB), ALU.add))
                dve.sem_inc(ring_used, 1)
                best(lg, mx[0], oh[0])
                if l == 0:
                    nc.vector.tensor_tensor(shifted[:, :, :], lg[:, :, :], bcast(mx[0][:, :], 2, E), ALU.subtract).then_inc(sh_ok, 1)
                    link(nc.vector.tensor_copy(ohs[:, :, :], oh[0][:, :, :]))
                    src = oh[0]
                else:
                    link(nc.vector.scalar_tensor_tensor(lg2[:, :, :], oh[0][:, :, :], MASKED, lg[:, :, :], ALU.mult, ALU.add))
                    best(lg2, mx[1], oh[1])
                    nc.vector.tensor_tensor(shifted[:, :, 0], mx[1][:, :], mx[0][:, :], ALU.subtract).then_inc(sh_ok, 1)
                    link(nc.vector.tensor_tensor(ohs[:, :, :], oh[0][:, :, :], oh[1][:, :, :], ALU.add))
                    src = ohs
                dve.sem_inc(ohs_ok, 1)
                link(nc.vector.tensor_reduce(tally[:, :], src[:, :, :].rearrange("p t e -> p e t"), AX.X, ALU.add))
                nc.vector.tensor_tensor(run[l][:, b + 1, :], run[l][:, b, :], tally[:, :], ALU.add).then_inc(run_ok, 1)

            def label(n):
                l, b = divmod(n, NB)
                if n == 0:
                    dve.wait_ge(ld_i, 32)
                for c in range(CHOICES[l]):
                    nc.vector.tensor_copy(pay[c][:, b * TPB:(b + 1) * TPB, D].bitcast(I32), ids[:, c, b * TPB:(b + 1) * TPB])

            def gate_and_slots(n):
                l, b = divmod(n, NB)
                now = slice(b * TPB, (b + 1) * TPB)
                scale = tg[:, 2 * l + 1:2 * l + 2]
                gcol = [pay[c][:, now, D + 1] for c in range(2)]
                picked, row = (wt, lg2), (slotf, wm)
                dve.wait_ge(ex_ok, n + 1)
                a = ring()
                if l == 0:
                    nc.vector.tensor_reduce(se[:, :], expd[:, :, :], AX.X, ALU.add)
                else:
                    nc.vector.tensor_scalar(re[:, :], se[:, :], 1.0, None, ALU.add)
                link(nc.vector.tensor_tensor(rk[:, :, :], a[:, 0:TPB * E].rearrange("p (t e) -> p t e", t=TPB), bcast(ebase, 1, TPB), ALU.add))
                dve.sem_inc(ring_used, 1)
                nc.vector.reciprocal(ginv[:, :], (re if l else se)[:, :])
                for c in range(CHOICES[l]):
                    last = nc.vector.tensor_tensor(picked[c][:, :, :], rk[:, :, :], oh[c][:, :, :], ALU.mult)
                link(last)
                nc.vector.tensor_scalar(gcol[0], ginv[:, :], scale, 0.5 if l else 1.0, ALU.mult, ALU.mult)
                for c in range(CHOICES[l]):
                    last = nc.vector.tensor_reduce(row[c][:, :], picked[c][:, :, :], AX.X, ALU.add)
                link(last)
                if l:
                    nc.vector.tensor_tensor(gcol[1], gcol[0], se[:, :], ALU.mult)
                for c in range(CHOICES[l]):
                    last = nc.vector.tensor_copy(slot[c][:, now], row[c][:, :])
                last.then_inc(slot_ok, 1)

            def plan(l):
                nt = FT[l]
                a = ring()
                link(nc.vector.tensor_tensor(pad_row[:, :], a[0:1, 0:E], ebase[0:1, :], ALU.add))
                nc.vector.tensor_scalar(pad_at[l][:, :], pad_row[:, :], float(PAY), None, ALU.mult).then_inc(pad_ok, 1)
                link(nc.vector.tensor_tensor(gt[:, :, :], bcast(a[:, 0:E], 2, NT), bcast(cst[:, C_K128:C_K128 + NT], 1, E), ALU.is_gt))
                dve.sem_inc(ring_used, 1)
                link(nc.vector.tensor_reduce(tiles[:, :], gt[:, :, :], AX.X, ALU.add))
                link(nc.vector.tensor_tensor(cumx[:, :, :], bcast(tiles[:, :], 1, E), cst[:, C_LT:C_LT + E * E].rearrange("p (e f) -> p e f", e=E), ALU.mult))
                link(nc.vector.tensor_reduce(cum[:, :], cumx[:, :, :], AX.X, ALU.add))
                jj = cst[:, C_J:C_J + nt]
                link(nc.vector.tensor_tensor(le[:, 0:nt, :], bcast(cum[:, :], 1, nt), bcast(jj, 2, E), ALU.is_le))
                nc.vector.tensor_tensor(let[:, 0:nt, :], le[:, 0:nt, :], bcast(tiles[:, :], 1, nt), ALU.mult)
                link(nc.vector.tensor_reduce(ej[:, 0:nt], le[:, 0:nt, :], AX.X, ALU.add))
                link(nc.vector.tensor_reduce(kj[:, 0:nt], let[:, 0:nt, :], AX.X, ALU.add))
                link(nc.vector.tensor_tensor(kj[:, 0:nt], jj, kj[:, 0:nt], ALU.subtract))
                link(nc.vector.scalar_tensor_tensor(bj[:, 0:nt], ej[:, 0:nt], float(BLOCKS), kj[:, 0:nt], ALU.mult, ALU.add))
                nc.vector.tensor_scalar(meta[l][0:1, 0, :], ej[0:1, 0:nt], float(E - 1), float(P * FW[l]), ALU.min, ALU.mult)
                nc.vector.tensor_scalar(meta[l][0:1, 1, :], bj[0:1, 0:nt], float(DUMMY), float(P * PAY), ALU.min, ALU.mult).then_inc(meta_ok, 1)

            def tiles_dve(l):
                def hidden(i, count, first):
                    dve.wait_ge(f_th[l], count)
                    bank = up_bank[i % SHORT]
                    nc.vector.scalar_tensor_tensor(silu[i % 2], tanhs[i % 2], 1.0, bank[:, 0:HID], ALU.add, ALU.mult).then_inc(f_silu[l], 1)
                    dve.wait_ge(f_silu[l], count)
                    if not first:
                        dve.wait_ge(f_dn[l], count - SHORT)
                    nc.vector.tensor_tensor(hid[i % SHORT].rearrange("p c t -> p (c t)"), silu[i % 2], bank[:, HID:2 * HID], ALU.mult).then_inc(f_hid[l], 1)

                def finish(i, count, put):
                    dve.wait_ge(f_dn[l], count)
                    if put is not None:
                        dve.wait_ge(f_put[l][i % SHORT], put)
                    src = down_bank[i % 2][:, 0:D]
                    nc.vector.tensor_copy(rows_at[i % SHORT][:, :], xt[i][:, D:D + 1].bitcast(I32))
                    if l == 0:
                        nc.vector.tensor_tensor(yb[i % SHORT], src, fw[i][:, 2 * HID:2 * HID + D], ALU.add).then_inc(f_th[l], 1)
                        dve.wait_ge(f_th[l], count)
                        src = yb[i % SHORT]
                    nc.vector.tensor_scalar(yo[i % SHORT][:, :], src, xt[i][:, D + 1:D + 2], None, ALU.mult).then_inc(f_y[l], 1)

                per = SLOTS // SHORT

                def body(r, first):
                    for i in range(SLOTS):
                        j = r * SLOTS + i
                        if l == 0:
                            dve.wait_ge(f_xtr[l], j + 1)
                            if not (first and i < SHORT):
                                dve.wait_ge(f_up[l], j + 1 - SHORT)
                            nc.vector.tensor_copy(xT[i % SHORT][:, :], ps_a[i % 2][:, 0:P]).then_inc(f_xT[l], 1)
                        if not (first and i < LAG_OUT):
                            finish((i - LAG_OUT) % SLOTS, j + 1 - LAG_OUT, None if first else 16 * (r * per + i // SHORT - 1))
                        if l and not (first and i < LAG_UP):
                            hidden((i - LAG_UP) % SLOTS, j, first and i < LAG_UP + SHORT)

                rounds(dve, l, body)
                if l:
                    hidden(SLOTS - 1, FT[l], False)
                for i in range(SLOTS - LAG_OUT, SLOTS):
                    finish(i, FT[l] - SLOTS + i + 1, 16 * (FT[l] // SHORT - 1))

            def add_results(l, b):
                dst = xs(b).rearrange("p t c -> p (t c)")
                for c in range(CHOICES[l]):
                    dve.wait_ge(y_ld[l][b][c], 16)
                    last = nc.vector.tensor_tensor(dst, dst, yin[c][b], ALU.add)
                    if c < CHOICES[l] - 1:
                        link(last)
                last.then_inc(x_ok, 1)

            for l in range(LAYERS):
                n0 = NB * l
                for k in STEPS:
                    for b, u in max_units(k):
                        maxima(n0 + b, u)
                    for b in due("den", k):
                        recip_den(n0 + b)
                    for b in due("rden", k):
                        weigh_out(n0 + b)
                    for b in due("router", k):
                        choose(n0 + b)
                    for b in due("ranks", k):
                        gate_and_slots(n0 + b)
                    for b in due("project", k):
                        rotate(n0 + b)
                    for b in due("low", k):
                        low_q(n0 + b)
                    for b in due("output", k):
                        residual(n0 + b)
                    for kl in range(LAYERS):
                        if l == 0 and k == KEYS_AT[kl]:
                            if kl == 0:
                                dve.wait_ge(s_tanh, 1)
                                dve.wait_ge(ld_c, 16)
                            dve.wait_ge(ld_w[kl], 16)
                            keys(kl)
                        for j in range(KT):
                            if l == 0 and k == VALUES_AT[kl][j]:
                                values(kl, j)
                        if l == 0 and k == BLOCKS_AT[kl] and kl == 0:
                            mask_keys(kl)
                    if l == 0 and k == SET_UP_AT:
                        set_up()
                    for b in due("split", k):
                        split_max(n0 + b)
                    for b in due("stats2", k):
                        statistics(xs(n0 + b), st2, mv2, var2)
                    for b in due("results", k):
                        if l:
                            add_results(0, b)
                            dve.wait_ge(x_ok, b + 1)
                    for b in due("stats", k):
                        front_stats(n0 + b)
                    for b in due("normalise", k):
                        front_normalise(n0 + b)
                    for b in due("normalise2", k):
                        normalise2(n0 + b)
                        label(n0 + b)
                plan(l)
                if l == 0:
                    mask_keys(1)
                tiles_dve(l)
            for b in range(NB):
                add_results(1, b)


def _constants():
    import numpy as np

    c = np.zeros((P, C_END), np.float32)
    c[:, C_ID:C_ID + P] = np.eye(P)
    inv = (1.0 / np.float32(10000.0) ** (np.arange(0, HD, 2, dtype=np.float32) / np.float32(HD))).astype(np.float32)
    ang = (np.arange(SEQ, dtype=np.float32)[:, None] * inv[None, :]).astype(np.float32)
    for p in range(P):
        d = p % HD
        c[p, C_COS:C_COS + SEQ] = np.cos(ang[:, d % (HD // 2)])
        c[p, C_SIN:C_SIN + SEQ] = np.sin(ang[:, d % (HD // 2)]) * (-1 if d < HD // 2 else 1)
        c[p, C_HM + (p // HD) % HPG] = 1
    aug = np.zeros((P, GROUPS, GK), np.float32)
    for j in range(KT):
        for r in range(KSIZE[j]):
            h = (KROWS * j + r) // KEYS
            c[r, C_HMV + 32 * j + HD * h:C_HMV + 32 * j + HD * (h + 1)] = 1
    for g in range(GROUPS):
        for f in range(GK):
            h, k = divmod(f, KEYS)
            aug[g * HPG + h, g, f] = aug[HEADS + g * HPG + h, g, f] = 1
            aug[AUG_KEY + k, g, f] = 1
    c[:, C_U:C_U + P] = np.triu(np.ones((P, P)), 1)
    c[:, C_DESC:C_DESC + E] = E - np.arange(E)
    c[:, C_EB:C_EB + E] = REGION * np.arange(E)
    c[:, C_K128:C_K128 + NT] = P * np.arange(NT)
    c[:, C_LT:C_LT + E * E] = np.tril(np.ones((E, E))).reshape(-1)
    c[:, C_J:C_END] = np.arange(max(FT))
    token = np.arange(P)[:, None] + P * np.arange(NT)[None, :]
    ids = np.stack([token, token + TOKENS], 1).astype(np.int32)
    pad = np.zeros((P, PAY), np.float32)
    pad[:, D] = np.full(P, NOROW, np.int32).view(np.float32)
    return c, aug.reshape(P, -1), ids, pad


def kernel(**a):
    import numpy as np
    import concourse.bacc as bacc
    from concourse.bass_utils import run_bass_kernel_spmd

    a = {k: np.asarray(v) for k, v in a.items()}
    half_turned = np.arange(D).reshape(HEADS, 2, HD // 2)[:, ::-1].reshape(-1)
    rows = lambda v: np.broadcast_to(v[None, :], (P, v.shape[0]))
    col = lambda v: v[:, None]
    zero = np.zeros(D, np.float32)

    def attention(wq, wk, wv, wo, bq, bk, bv, bo, wr, br):
        return np.ascontiguousarray(np.concatenate(
            [wq, wq[:, half_turned], wk, wk[:, half_turned], wv, wo, rows(bv), rows(bo), wr, rows(br),
             col(bq), col(bk)], 1))

    wkv = a["L0_xattn_Wkv"]
    w0 = attention(a["L0_xattn_Wq"], wkv[:, :D], wkv[:, D:], a["L0_xattn_Wo"], zero, zero, zero, a["L0_xattn_bo"],
                   a["L0_ffn_Wr"], a["L0_ffn_br"])
    w1 = attention(a["L1_xattn_Wq"], a["L1_xattn_Wk"], a["L1_xattn_Wv"], a["L1_xattn_Wo"], a["L1_xattn_bq"], a["L1_xattn_bk"],
                   a["L1_xattn_bv"], a["L1_xattn_bo"], a["L1_ffn_w_gate"].T, np.zeros(E, np.float32))
    by_chunk = lambda m: m.reshape(E, HC, P, D).transpose(0, 2, 1, 3).reshape(E, P, HC * D)
    f0 = np.ascontiguousarray(np.concatenate(
        [a["L0_ffn_W1"], by_chunk(a["L0_ffn_W2"]), np.broadcast_to(a["L0_ffn_b2"][:, None, :], (E, P, D)),
         a["L0_ffn_b1"].reshape(E, HC, P).transpose(0, 2, 1)], 2))
    f1 = np.ascontiguousarray(np.concatenate(
        [a["L1_ffn_w_gate_proj"].transpose(0, 2, 1), a["L1_ffn_w_up_proj"].transpose(0, 2, 1),
         by_chunk(a["L1_ffn_w_down_proj"].transpose(0, 2, 1))], 2))
    const, aug, ids, pad = _constants()
    arrays = {
        "x_in": np.ascontiguousarray(a["x"].reshape(NT, P, D).transpose(1, 0, 2)),
        "ctx_in": np.ascontiguousarray(np.broadcast_to(a["ctx_1024"].transpose(2, 0, 1)[:, :, None, :], (P, NB, HPG, KEYS))),
        "mask_in": np.ascontiguousarray(a["mask_SxS2_ik0"].reshape(TPB, P, KEYS).transpose(1, 0, 2)),
        "gates_in": np.ascontiguousarray(rows(np.concatenate([a["g_xattn"][:1], a["g_ffn"][:1], a["g_xattn"][1:], a["g_ffn"][1:]]))),
        "w0_in": w0, "w1_in": w1, "f0_in": f0, "f1_in": f1,
        "const_in": const, "aug_in": aug, "ids_in": ids, "pad_in": pad,
    }
    nc = bacc.Bacc("TRN2", target_bir_lowering=False, num_devices=1)
    aps = {k: nc.dram_tensor(k, v.shape, mybir.dt.from_np(v.dtype), kind="ExternalInput").ap() for k, v in arrays.items()}
    out = nc.dram_tensor("out", (P, NT, D), F32, kind="ExternalOutput").ap()
    two_layers(nc, **aps, out=out)
    r = run_bass_kernel_spmd(nc, [arrays], core_ids=[0])
    got = r.results[0]["out"]
    return np.ascontiguousarray(got.transpose(1, 0, 2).reshape(NB, SEQ, D))
```
